# Optimizing a Trainium2 kernel written in Bass

```python
import numpy as np
import jax
import jax.numpy as jnp

def _softmax(x, axis=-1):
    return jax.nn.softmax(x, axis=axis)

def _gelu(x):
    return jax.nn.gelu(x, approximate=True)

def _silu(x):
    return jax.nn.silu(x)

def _sigmoid(x):
    return jax.nn.sigmoid(x)

def _layernorm(x, axis=-1, eps=1e-05):
    m = jnp.mean(x, axis=axis, keepdims=True)
    v = jnp.var(x, axis=axis, keepdims=True)
    return (x - m) / jnp.sqrt(v + eps)

def _scatter_add(tgt, idx, src, axis=0):
    return tgt.at[idx].add(src)

def _segment_sum(src, seg, n):
    return jax.ops.segment_sum(src, seg, n)
kernel_name = 'mk_gnn_resnorm_d4_gnn_r32_e96ee6'

def setup_inputs(seed: int=0):
    np.random.seed(seed)
    _w = jnp.asarray

    def _rec_inputs():
        import jax
        import jax.numpy as jnp
        _gk = jax.random.key(seed)
        x = -6.415e-05 + 1 * jax.random.normal(jax.random.fold_in(_gk, 1), (625, 512), jnp.float32)
        src = jax.random.randint(jax.random.fold_in(_gk, 2), (20000,), 0, 625, jnp.int32)
        dst = jax.random.randint(jax.random.fold_in(_gk, 3), (20000,), 0, 625, jnp.int32)
        _o = jnp.argsort(dst, stable=True)
        src = src[_o]
        dst = dst[_o]
        edge_attr_64 = -5.3897e-05 + 0.999841 * jax.random.normal(jax.random.fold_in(_gk, 12), (20000, 64), jnp.float32)
        edge_type_10 = jax.random.randint(jax.random.fold_in(_gk, 14), (20000,), 0, 10, jnp.int32)
        edge_type_8 = jax.random.randint(jax.random.fold_in(_gk, 15), (20000,), 0, 8, jnp.int32)
        edge_weight = jax.random.uniform(jax.random.fold_in(_gk, 16), (20000,), jnp.float32, 0.0, 0.999999)
        return (x, src, dst, edge_attr_64, edge_type_10, edge_type_8, edge_weight)
    x, src, dst, edge_attr_64, edge_type_10, edge_type_8, edge_weight = _rec_inputs()

    def _L0_gnn_setup():
        import jax, jax.numpy as jnp
        import numpy as np
        N = 625
        E = 5000
        D = 512
        R = 8
        key = jax.random.key(seed)
        ks = jax.random.split(key, 8)
        inp = {'input': jax.random.normal(ks[0], (N, D), dtype=jnp.float32), 'heads': jax.random.randint(ks[1], (E,), 0, N), 'tails': jax.random.randint(ks[2], (E,), 0, N), 'rel': jax.random.randint(ks[3], (E,), 0, R), 'W_self': jax.random.normal(ks[4], (D, D), dtype=jnp.float32) * 0.03, 'b_self': jnp.zeros((D,), dtype=jnp.float32), 'W_rel': jax.random.normal(ks[5], (2 * R, D, D), dtype=jnp.float32) * 0.03, 'b_rel': jnp.zeros((2 * R, D), dtype=jnp.float32)}
        return inp
    _L0_gnn_all = _L0_gnn_setup()
    _L0_gnn_in = {k: v for k, v in _L0_gnn_all.items() if k in ('W_self', 'b_self', 'W_rel', 'b_rel')}
    del _L0_gnn_all

    def _L1_gnn_setup():
        import jax, jax.numpy as jnp
        import numpy as np
        N_NODES = 3125
        N_EDGES = 100000
        IN_F = 512
        OUT_F = 512
        RANK = 64
        key = jax.random.key(seed)
        ks = jax.random.split(key, 8)
        inp = jax.random.normal(ks[0], (N_NODES, IN_F), dtype=jnp.float32)
        U = jax.random.normal(ks[1], (IN_F, RANK), dtype=jnp.float32) / np.sqrt(IN_F)
        s = jax.random.uniform(ks[2], (RANK,), dtype=jnp.float32)
        Vt = jax.random.normal(ks[3], (RANK, OUT_F), dtype=jnp.float32) / np.sqrt(RANK)
        bias = jax.random.normal(ks[4], (OUT_F,), dtype=jnp.float32) * 0.01
        edge_row = jax.random.randint(ks[5], (N_EDGES,), 0, N_NODES, dtype=jnp.int64 if jax.config.jax_enable_x64 else jnp.int32)
        edge_col = jax.random.randint(ks[6], (N_EDGES,), 0, N_NODES, dtype=jnp.int64 if jax.config.jax_enable_x64 else jnp.int32)
        edge_val = jax.random.uniform(ks[7], (N_EDGES,), dtype=jnp.float32)
        return {'input': inp, 'U': U, 's': s, 'Vt': Vt, 'bias': bias, 'edge_row': edge_row, 'edge_col': edge_col, 'edge_val': edge_val}
    _L1_gnn_all = _L1_gnn_setup()
    _L1_gnn_in = {k: v for k, v in _L1_gnn_all.items() if k in ('U', 's', 'Vt', 'bias')}
    del _L1_gnn_all

    def _L2_gnn_setup():
        import jax, jax.numpy as jnp
        import numpy as np
        N, E, H, ED = (50000, 12500, 512, 64)
        BN_EPS = 1e-05

        def _bn(h, g, b):
            mu = jnp.mean(h, axis=0)
            var = jnp.mean(jnp.square(h - mu), axis=0)
            return (h - mu) * jax.lax.rsqrt(var + BN_EPS) * g + b
        key = jax.random.key(seed)
        ks = jax.random.split(key, 8)
        s = lambda d: 1.0 / np.sqrt(d)
        return {'x': jax.random.normal(ks[0], (N, H), jnp.float32), 'edge_attr': jax.random.normal(ks[1], (E, ED), jnp.float32), 'edge_index': jax.random.randint(ks[2], (2, E), 0, N, jnp.int32), 'W_e': jax.random.normal(ks[3], (ED, H), jnp.float32) * s(ED), 'b_e': jnp.zeros((H,), jnp.float32), 'W1': jax.random.normal(ks[4], (H, 2 * H), jnp.float32) * s(H), 'b1': jnp.zeros((2 * H,), jnp.float32), 'g1': jnp.ones((2 * H,), jnp.float32), 'beta1': jnp.zeros((2 * H,), jnp.float32), 'W2': jax.random.normal(ks[5], (2 * H, H), jnp.float32) * s(2 * H), 'b2': jnp.zeros((H,), jnp.float32), 'g2': jnp.ones((H,), jnp.float32), 'beta2': jnp.zeros((H,), jnp.float32), 'eps': jnp.zeros((), jnp.float32)}
    _L2_gnn_all = _L2_gnn_setup()
    _L2_gnn_in = {k: v for k, v in _L2_gnn_all.items() if k in ('W_e', 'b_e', 'W1', 'b1', 'g1', 'beta1', 'W2', 'b2', 'g2', 'beta2', 'eps')}
    del _L2_gnn_all

    def _L3_gnn_setup():
        import jax, jax.numpy as jnp
        import numpy as np
        N, E, H, D, C, L = (625, 10000, 8, 64, 512, 2)

        def layer_norm(x, g, b, eps=1e-05):
            mu = x.mean(-1, keepdims=True)
            var = ((x - mu) ** 2).mean(-1, keepdims=True)
            return (x - mu) / jnp.sqrt(var + eps) * g + b
        key = jax.random.key(seed)
        ks = jax.random.split(key, 14)
        s = 0.02
        x = jax.random.normal(ks[0], (N, C), jnp.float32)
        edge_index = jax.random.randint(ks[1], (2, E), 0, N, jnp.int32)
        edge_type = jax.random.randint(ks[2], (E,), 0, 10, jnp.int32)
        edge_repre = jax.random.normal(ks[3], (E,), jnp.float32)
        Wq = jax.random.normal(ks[4], (L, C, C), jnp.float32) * s
        Wk = jax.random.normal(ks[5], (L, C, C), jnp.float32) * s
        Wv = jax.random.normal(ks[6], (L, C, C), jnp.float32) * s
        Ws = jax.random.normal(ks[7], (L, C, C), jnp.float32) * s
        bq = jnp.zeros((L, C), jnp.float32)
        bk = jnp.zeros((L, C), jnp.float32)
        bv = jnp.zeros((L, C), jnp.float32)
        bs = jnp.zeros((L, C), jnp.float32)
        W1 = jax.random.normal(ks[8], (C, 2 * C), jnp.float32) * s
        b1 = jnp.zeros((2 * C,), jnp.float32)
        W2 = jax.random.normal(ks[9], (2 * C, C), jnp.float32) * s
        b2 = jnp.zeros((C,), jnp.float32)
        ln_g = jnp.ones((C,), jnp.float32)
        ln_b = jnp.zeros((C,), jnp.float32)
        return {'x': x, 'edge_index': edge_index, 'edge_type': edge_type, 'edge_repre': edge_repre, 'Wq': Wq, 'bq': bq, 'Wk': Wk, 'bk': bk, 'Wv': Wv, 'bv': bv, 'Ws': Ws, 'bs': bs, 'W1': W1, 'b1': b1, 'W2': W2, 'b2': b2, 'ln_g': ln_g, 'ln_b': ln_b}
    _L3_gnn_all = _L3_gnn_setup()
    _L3_gnn_in = {k: v for k, v in _L3_gnn_all.items() if k in ('Wq', 'bq', 'Wk', 'bk', 'Wv', 'bv', 'Ws', 'bs', 'W1', 'b1', 'W2', 'b2', 'ln_g', 'ln_b')}
    del _L3_gnn_all
    return {'x': x, 'src': src, 'dst': dst, 'edge_attr_64': edge_attr_64, 'edge_type_10': edge_type_10, 'edge_type_8': edge_type_8, 'edge_weight': edge_weight, 'L0_gnn_W_self': _L0_gnn_in['W_self'], 'L0_gnn_b_self': _L0_gnn_in['b_self'], 'L0_gnn_W_rel': _L0_gnn_in['W_rel'], 'L0_gnn_b_rel': _L0_gnn_in['b_rel'], 'L1_gnn_U': _L1_gnn_in['U'], 'L1_gnn_s': _L1_gnn_in['s'], 'L1_gnn_Vt': _L1_gnn_in['Vt'], 'L1_gnn_bias': _L1_gnn_in['bias'], 'L2_gnn_W_e': _L2_gnn_in['W_e'], 'L2_gnn_b_e': _L2_gnn_in['b_e'], 'L2_gnn_W1': _L2_gnn_in['W1'], 'L2_gnn_b1': _L2_gnn_in['b1'], 'L2_gnn_g1': _L2_gnn_in['g1'], 'L2_gnn_beta1': _L2_gnn_in['beta1'], 'L2_gnn_W2': _L2_gnn_in['W2'], 'L2_gnn_b2': _L2_gnn_in['b2'], 'L2_gnn_g2': _L2_gnn_in['g2'], 'L2_gnn_beta2': _L2_gnn_in['beta2'], 'L2_gnn_eps': _L2_gnn_in['eps'], 'L3_gnn_Wq': _L3_gnn_in['Wq'], 'L3_gnn_bq': _L3_gnn_in['bq'], 'L3_gnn_Wk': _L3_gnn_in['Wk'], 'L3_gnn_bk': _L3_gnn_in['bk'], 'L3_gnn_Wv': _L3_gnn_in['Wv'], 'L3_gnn_bv': _L3_gnn_in['bv'], 'L3_gnn_Ws': _L3_gnn_in['Ws'], 'L3_gnn_bs': _L3_gnn_in['bs'], 'L3_gnn_W1': _L3_gnn_in['W1'], 'L3_gnn_b1': _L3_gnn_in['b1'], 'L3_gnn_W2': _L3_gnn_in['W2'], 'L3_gnn_b2': _L3_gnn_in['b2'], 'L3_gnn_ln_g': _L3_gnn_in['ln_g'], 'L3_gnn_ln_b': _L3_gnn_in['ln_b']}

def reference(x, src, dst, edge_attr_64, edge_type_10, edge_type_8, edge_weight, L0_gnn_W_self, L0_gnn_b_self, L0_gnn_W_rel, L0_gnn_b_rel, L1_gnn_U, L1_gnn_s, L1_gnn_Vt, L1_gnn_bias, L2_gnn_W_e, L2_gnn_b_e, L2_gnn_W1, L2_gnn_b1, L2_gnn_g1, L2_gnn_beta1, L2_gnn_W2, L2_gnn_b2, L2_gnn_g2, L2_gnn_beta2, L2_gnn_eps, L3_gnn_Wq, L3_gnn_bq, L3_gnn_Wk, L3_gnn_bk, L3_gnn_Wv, L3_gnn_bv, L3_gnn_Ws, L3_gnn_bs, L3_gnn_W1, L3_gnn_b1, L3_gnn_W2, L3_gnn_b2, L3_gnn_ln_g, L3_gnn_ln_b):
    import jax
    import jax.numpy as jnp

    def _L0_gnn_ref(input, heads, tails, rel, W_self, b_self, W_rel, b_rel):
        import jax, jax.numpy as jnp
        import numpy as np
        N = 625
        E = 5000
        D = 512
        R = 8
        h_self = input @ W_self.T + b_self
        H_all = jnp.einsum('rod,nd->rno', W_rel, input) + b_rel[:, None, :]
        msg_to_heads = H_all[rel, tails]
        msg_to_tails = H_all[rel + R, heads]
        agg = jax.ops.segment_sum(msg_to_heads, heads, num_segments=N) + jax.ops.segment_sum(msg_to_tails, tails, num_segments=N)
        return jax.nn.relu(h_self + agg)

    def _L1_gnn_ref(input, U, s, Vt, bias, edge_row, edge_col, edge_val):
        import jax, jax.numpy as jnp
        import numpy as np
        N_NODES = 3125
        N_EDGES = 100000
        IN_F = 512
        OUT_F = 512
        RANK = 64
        support = input @ U * s
        support = support @ Vt
        gathered = support[edge_col] * edge_val[:, None]
        output = jax.ops.segment_sum(gathered, edge_row, num_segments=input.shape[0])
        output = output + bias
        return jax.nn.relu(output)

    def _L2_gnn_ref(x, edge_attr, edge_index, W_e, b_e, W1, b1, g1, beta1, W2, b2, g2, beta2, eps):
        import jax, jax.numpy as jnp
        import numpy as np
        N, E, H, ED = (50000, 12500, 512, 64)
        BN_EPS = 1e-05

        def _bn(h, g, b):
            mu = jnp.mean(h, axis=0)
            var = jnp.mean(jnp.square(h - mu), axis=0)
            return (h - mu) * jax.lax.rsqrt(var + BN_EPS) * g + b
        src, dst = (edge_index[0], edge_index[1])
        msg = jax.nn.relu(x[src] + edge_attr @ W_e + b_e)
        aggr = jax.ops.segment_sum(msg, dst, num_segments=x.shape[0])
        h = (1.0 + eps) * x + aggr
        h = jax.nn.silu(_bn(h @ W1 + b1, g1, beta1))
        h = h @ W2 + b2
        return jax.nn.silu(_bn(h, g2, beta2))

    def _L3_gnn_ref(x, edge_index, edge_type, edge_repre, Wq, bq, Wk, bk, Wv, bv, Ws, bs, W1, b1, W2, b2, ln_g, ln_b):
        import jax, jax.numpy as jnp
        import numpy as np
        N, E, H, D, C, L = (625, 10000, 8, 64, 512, 2)

        def layer_norm(x, g, b, eps=1e-05):
            mu = x.mean(-1, keepdims=True)
            var = ((x - mu) ** 2).mean(-1, keepdims=True)
            return (x - mu) / jnp.sqrt(var + eps) * g + b
        src, dst = (edge_index[0], edge_index[1])
        enc = x
        scale = 1.0 / jnp.sqrt(jnp.float32(D))
        for l in range(L):
            q = (x @ Wq[l] + bq[l]).reshape(N, H, D)
            k = (x @ Wk[l] + bk[l]).reshape(N, H, D)
            v = (x @ Wv[l] + bv[l]).reshape(N, H, D)
            a = (q[dst] * k[src]).sum(-1) * scale
            amax = jax.ops.segment_max(a, dst, num_segments=N)
            amax = jnp.where(jnp.isfinite(amax), amax, 0.0)
            e = jnp.exp(a - amax[dst])
            denom = jax.ops.segment_sum(e, dst, num_segments=N)
            alpha = e / (denom[dst] + 1e-16)
            agg = jax.ops.segment_sum(alpha[:, :, None] * v[src], dst, num_segments=N).reshape(N, C)
            x = agg + (x @ Ws[l] + bs[l]) + enc
        x = layer_norm(x, ln_g, ln_b)
        x = jax.nn.relu(x @ W1 + b1) @ W2 + b2 + x
        x = layer_norm(x, ln_g, ln_b)
        return x + enc
    edge_index = jnp.stack([src, dst])
    x = _layernorm(x + _L0_gnn_ref(x, src, dst, edge_type_8, L0_gnn_W_self, L0_gnn_b_self, L0_gnn_W_rel, L0_gnn_b_rel), axis=-1)
    x = _layernorm(x + _L1_gnn_ref(x, L1_gnn_U, L1_gnn_s, L1_gnn_Vt, L1_gnn_bias, src, dst, edge_weight), axis=-1)
    x = _layernorm(x + _L2_gnn_ref(x, edge_attr_64, edge_index, L2_gnn_W_e, L2_gnn_b_e, L2_gnn_W1, L2_gnn_b1, L2_gnn_g1, L2_gnn_beta1, L2_gnn_W2, L2_gnn_b2, L2_gnn_g2, L2_gnn_beta2, L2_gnn_eps), axis=-1)
    x = _layernorm(x + _L3_gnn_ref(x, edge_index, edge_type_10, edge_weight, L3_gnn_Wq, L3_gnn_bq, L3_gnn_Wk, L3_gnn_bk, L3_gnn_Wv, L3_gnn_bv, L3_gnn_Ws, L3_gnn_bs, L3_gnn_W1, L3_gnn_b1, L3_gnn_W2, L3_gnn_b2, L3_gnn_ln_g, L3_gnn_ln_b), axis=-1)
    return x

_drawn_inputs = setup_inputs


def setup_inputs(seed=0):
    import zlib

    import numpy as np

    out = dict(_drawn_inputs(seed))
    spreads = {'L0_gnn_b_self': (0.0, 0.1),
     'L0_gnn_b_rel': (0.0, 0.1),
     'L2_gnn_b_e': (0.0, 0.1),
     'L2_gnn_b1': (0.0, 0.8),
     'L2_gnn_g1': (1.0, 0.2),
     'L2_gnn_beta1': (0.0, 0.1),
     'L2_gnn_b2': (0.0, 0.8),
     'L2_gnn_g2': (1.0, 0.2),
     'L2_gnn_beta2': (0.0, 0.1),
     'L3_gnn_bq': (0.0, 0.8),
     'L3_gnn_bk': (0.0, 0.8),
     'L3_gnn_bv': (0.0, 0.1),
     'L3_gnn_bs': (0.0, 0.1),
     'L3_gnn_b1': (0.0, 0.553),
     'L3_gnn_b2': (0.0, 0.1),
     'L3_gnn_ln_g': (1.0, 0.2),
     'L3_gnn_ln_b': (0.0, 0.1)}
    factors = {'L1_gnn_bias': 8.0, 'L3_gnn_Wq': 8.0, 'L3_gnn_Wk': 8.0}
    for name, (base, spread) in spreads.items():
        noise = np.random.default_rng([zlib.crc32(name.encode()), seed]).standard_normal(out[name].shape)
        drawn = base * np.exp(spread * noise) if base else spread * noise
        out[name] = jnp.asarray(drawn.astype(out[name].dtype))
    for name, factor in factors.items():
        out[name] = (out[name] * factor).astype(out[name].dtype)
    return out
```

```python
from contextlib import ExitStack

import concourse.bass as bass
from concourse import mybir

F32 = mybir.dt.float32
F16 = mybir.dt.float16
I32 = mybir.dt.int32
ALU = mybir.AluOpType
ACT = mybir.ActivationFunctionType
X = mybir.AxisListType.X
ds = bass.ds

P = 128
N = 625
T = 125
NT = N // T
D = 512
KD = D // P
E = 20000
EC = E // T
R = 8
G = NT * R
CH = (E + G * (P - 1)) // P
CH += -CH % 4
EA = 64
ROW = EA + 4
SRC, DSTL, WGT, SRCI = EA, EA + 1, EA + 2, EA + 3
RANK = 64
HEADS, HD = 8, 64
LAYERS = 2
EPS = 1e-5
FAR = -1e30
H0 = 313
HALVES = ((0, H0), (H0, N - H0))
HALVES_B = ((0, 512), (512, N - 512))
TURNS = (4, 3, 3, 3, 3, 3, 3, 3)
CREDIT = 4
PIECES = 7


def done(c):
    return c + 1 + CREDIT


def program(nc, x, src, dst, edge_attr, edge_type, edge_weight, p0, p1, p2, p3, out):
    with ExitStack() as ctx:
        def sb(name, shape, dt=F32):
            return ctx.enter_context(nc.sbuf_tensor(name, shape, dt))

        def sem(name):
            return ctx.enter_context(nc.semaphore(name))

        table = nc.dram_tensor("sorted_rows", (P * CH, ROW), F32, kind="Internal").ap()
        xb_rows = nc.dram_tensor("x_plus_b_e", (N, D), F32, kind="Internal").ap()
        table_p = table.rearrange("(p c) e -> p (c e)", p=P)

        xN = sb("xN", [P, NT, D])
        xT = sb("xT", [P, KD * N])
        ident = sb("ident", [P, P])
        pairs = sb("pairs", [P, NT * N])
        wadj = sb("wadj", [P, NT * N])
        node_h = sb("node_h", [P, N], F16)
        node_f = sb("node_f", [P, N])
        arena = sb("arena", [P, G * N])
        annex = sb("annex", [P, CH * ROW])
        group = sb("group", [1, CH], I32)
        tile_of = sb("tile_of", [1, CH], I32)
        stat = sb("stat", [P, NT, 6])
        mv = sb("mv", [P, NT, 2])
        sd = sb("sd", [P, NT])
        rstd = sb("rstd", [P, NT])
        b_self = sb("b_self", [P, D])
        b_rel = sb("b_rel", [2 * R, D])
        deg = sb("deg", [P, NT, 2 * R])
        has_in = sb("has_in", [P, NT])
        PS = ctx.enter_context(nc.psum_tensor("PS", [P, 8, 512], F32))

        xTk = xT[:, :].rearrange("p (k n) -> p k n", n=N)
        identT = ident[0:T, 0:T]

        def view(tensor, at, shape, parts=P):
            size = 1
            for n in shape:
                size *= n
            v = tensor[0:parts, at:at + size]
            if len(shape) == 2:
                v = v.rearrange("p (a b) -> p a b", b=shape[1])
            return v

        def two_banks(b, parts, n=N):
            return PS[0:parts, b:b + 2, :].rearrange("p b n -> p (b n)")[:, 0:n]

        rows = view(annex, 0, [EC, ROW], T)
        hot = view(arena, 0, [G, EC], T)
        rank = view(arena, G * EC, [G, EC], T)
        keep = view(arena, 2 * G * EC, [G, EC], T)
        past = view(arena, 0, [CH, G], 1)
        (src_f, dst_f, typ_f, wgt, tile, key, dst_l, slot_f, lo_f, hi_f) = [
            view(pairs, n * EC, [EC], T) for n in range(10)]
        (src_i, dst_i, typ_i, slot_i, lo_i, hi_i, pos_i) = [
            view(pairs, n * EC, [EC], T).bitcast(I32) for n in range(10, 17)]
        (cnt, chunks_f, upto, start, base, ones_g) = [view(pairs, 17 * EC + n * G, [G]) for n in range(6)]
        chunks_i = view(pairs, 17 * EC + 6 * G, [G]).bitcast(I32)
        group_no = xT[:, 0:G]
        chunk_no = xT[0:1, G:G + CH]
        group_f = xT[0:1, G + CH:G + 2 * CH]
        before = xT[0:T, 600:600 + T]
        ones_m = xT[0:T, 800:800 + P]
        pad = view(wadj, 0, [CH // PIECES, ROW])

        sorted_rows = view(annex, 0, [CH, ROW])
        hot_dst_h = [xT[:, 64 * j:64 * j + 63].bitcast(F16)[:, 0:T] for j in range(2)]
        hot_src_h = [xT[:, 128 + 314 * j:128 + 314 * j + 313].bitcast(F16)[:, 0:N] for j in range(2)]
        hot_dst_f = [xT[:, 760 + 128 * j:760 + 128 * j + T] for j in range(2)]
        hot_src_w = [xT[:, 1020 + 626 * j:1020 + 626 * j + N] for j in range(2)]
        counts = arena[0:T, :]

        here = view(annex, 0, [NT, N], T)
        turned = view(annex, NT * N, [NT * N], T)
        turned3 = view(annex, NT * N, [NT, N], T)
        w_a = view(annex, 2 * NT * N, [KD, D])
        w_b = view(annex, 2 * NT * N + KD * D, [KD, D])
        y_a = xTk
        y_b = view(annex, 2 * NT * N + 2 * KD * D, [KD, N])
        deg_t = annex[0:2 * R, 0:N]
        pairs_t = view(pairs, 0, [NT, N], T)
        wadj_t = view(wadj, 0, [NT, N], T)
        sums = view(arena, 0, [NT, D], T)


        u_w = view(arena, 3000, [KD, RANK])
        vt_w = view(arena, 3300, [D], RANK)
        s_row = view(arena, 3900, [RANK], T)
        b1_row = view(arena, 4000, [D], T)
        support = view(arena, 4600, [NT, RANK], T)
        mixed = view(arena, 5000, [N], RANK)
        be_row = view(arena, 6000, [D], T)
        xb = view(arena, 6600, [NT, D], T)
        ln_pairs = view(arena, 20000, [NT * N], T)

        row_buf = view(arena, 9300, [4, ROW])
        x_src = view(arena, 9600, [4, D])
        msg_in = view(arena, 11700, [2, D])
        msg = view(arena, 12800, [2, D])
        attr_t = view(arena, 13900, [2, P], EA)
        hot_dst = view(arena, 14200, [2, P])
        agg = view(arena, 14500, [NT, D], T)
        h_t = view(arena, 17100, [KD * N])
        h_tk = view(arena, 17100, [KD, N])
        z1 = view(arena, 20000, [2 * KD, N])
        z2 = view(arena, 0, [KD, N])
        w1 = view(annex, 0, [KD, 2 * D])
        w2 = view(annex, 2 * KD * D, [2 * KD, D])
        w_e = view(annex, 4 * KD * D, [D], EA)
        small2 = 4 * KD * D + D
        (b1_c, g1_c, beta1_c, b2_c, g2_c, beta2_c, scale_c, shift_c, bn_ve, bn_sd) = [
            view(annex, small2 + 8 * n, [8]) for n in range(10)]
        eps_c = view(annex, small2 + 80, [1], T)
        bn_stat = view(annex, small2 + 96, [2 * KD, 12])
        bn_mv = view(annex, small2 + 192, [2 * KD, 2])

        q_t = view(arena, 0, [KD, N])
        k_t = view(arena, 2500, [KD, N])
        val = view(arena, 5000, [NT, D], T)
        rest = view(arena, 7560, [NT, D], T)
        enc = view(arena, 10120, [NT, D], T)
        scores = view(arena, 12700, [2, N], T)
        probs = view(arena, 13950, [2, N], T)
        probs_t = view(arena, 15200, [2, N], T)
        top = view(arena, 16450, [4], T)
        minus_top = view(arena, 16454, [4], T)
        denom = view(arena, 16460, [NT, HEADS], T)
        inv = view(arena, 16500, [NT, HEADS], T)
        mlp1 = view(arena, 16600, [KD, 2 * D])
        mlp2 = view(arena, 16600 + 2 * KD * D, [2 * KD, D])
        hid = view(arena, 0, [2 * KD, N])
        w_qkvs = [view(annex, n * KD * D, [KD, D]) for n in range(4)]
        bq_c = view(annex, 8200, [KD])
        bk_c = view(annex, 8210, [KD])
        mb1_c = view(annex, 8220, [2 * KD])
        bv_row, bs_row, mb2_row, ln_g, ln_b = [view(annex, 8300 + D * n, [D], T) for n in range(5)]

        edges_in = sem("edges_in")
        attr_in = sem("attr_in")
        pad_ready = sem("pad_ready")
        cleared = sem("cleared")
        x_in = sem("x_in")
        consts = sem("consts")
        rows_ready = sem("rows_ready")
        ranked = sem("ranked")
        prefixed = sem("prefixed")
        slots_ready = sem("slots_ready")
        scattered = sem("scattered")
        sorted_in = sem("sorted_in")
        v_step = sem("v_step")
        a_step = sem("a_step")
        g_step = sem("g_step")
        zeroed = sem("zeroed")
        onehots = sem("onehots")
        counted = sem("counted")
        added = sem("added")
        xt_psum = sem("xt_psum")
        xt_ready = sem("xt_ready")
        w_self_in = sem("w_self_in")
        w_a_in = sem("w_a_in")
        w_b_in = sem("w_b_in")
        bias0_in = sem("bias0_in")
        self_done = sem("self_done")
        here_ready = sem("here_ready")
        deg_done = sem("deg_done")
        scratch = sem("scratch")
        out_act = sem("out_act")
        out_dve = sem("out_dve")
        a_used = sem("a_used")
        b_used = sem("b_used")
        deg_psum = sem("deg_psum")
        deg_ready = sem("deg_ready")
        acc_done = sem("acc_done")
        var_ready = sem("var_ready")
        sd_ready = sem("sd_ready")
        x_ready = sem("x_ready")

        p1_in = sem("p1_in")
        support_psum = sem("support_psum")
        support_ready = sem("support_ready")
        mixed_psum = sem("mixed_psum")
        mixed_ready = sem("mixed_ready")
        l1_psum = sem("l1_psum")
        clipped = sem("clipped")
        logs_ready = sem("logs_ready")
        p2_in = sem("p2_in")
        xb_ready = sem("xb_ready")
        xb_stored = sem("xb_stored")
        rows_in = [sem(f"rows_in{n}") for n in range(2)]
        src_in = [sem(f"src_in{n}") for n in range(4)]
        pool_tick = sem("pool_tick")
        attr_psum = sem("attr_psum")
        attr_out = sem("attr_out")
        edge_psum = sem("edge_psum")
        msg_sum = sem("msg_sum")
        hot_ready = sem("hot_ready")
        msg_ready = sem("msg_ready")
        agg_psum = sem("agg_psum")
        agg_added = sem("agg_added")
        h_ready = sem("h_ready")
        z_psum = sem("z_psum")
        z_out = sem("z_out")
        bn_var = sem("bn_var")
        bn_dev = sem("bn_dev")
        bn_ready = sem("bn_ready")
        act_out = sem("act_out")
        back_psum = sem("back_psum")
        l3_x = sem("l3_x")
        l3_in = sem("l3_in")
        l3_rows = sem("l3_rows")
        proj = sem("proj")
        qk_out = sem("qk_out")
        vs_out = sem("vs_out")
        w_used = sem("w_used")
        score_psum = sem("score_psum")
        top_ready = sem("top_ready")
        score_out = sem("score_out")
        probs_out = sem("probs_out")
        turn_psum = sem("turn_psum")
        turn_out = sem("turn_out")
        pv_done = sem("pv_done")
        tile_out = sem("tile_out")
        o_step = sem("o_step")
        mlp_in = sem("mlp_in")
        hid_psum = sem("hid_psum")
        hid_out = sem("hid_out")
        mlp_psum = sem("mlp_psum")
        stored = sem("stored")
        tick = sem("tick")

        block = ctx.enter_context(nc.Block())

        def load_rows(sp, to, row, done_sem, n):
            sp.dma_start(to, row.rearrange("(a d) -> a d", a=1).to_broadcast((n, row.shape[0]))).then_inc(done_sem, 16)

        def sync_sort(sp):
            for tile_to, row in ((src_i, src), (dst_i, dst), (typ_i, edge_type), (wgt, edge_weight)):
                sp.dma_start(tile_to, row.rearrange("(p c) -> p c", p=T)).then_inc(edges_in, 16)
            sp.dma_start(rows[:, :, 0:EA], edge_attr.rearrange("(p c) e -> p c e", p=T)).then_inc(attr_in, 16)
            sp.wait_ge(pad_ready, 1)
            piece = CH // PIECES * ROW
            for n in range(PIECES):
                sp.dma_start(table_p[:, n * piece:(n + 1) * piece],
                             pad.rearrange("p c e -> p (c e)")).then_inc(cleared, 16)
            sp.dma_start(xN[0:T, :, :], x.rearrange("(t p) d -> p t d", p=T)).then_inc(x_in, 16)
            load_rows(sp, b_self[0:T, :], p0["b_self"], bias0_in, T)
            sp.dma_start(b_rel[:, :], p0["b_rel"]).then_inc(bias0_in, 16)
            sp.wait_ge(scattered, 16 * EC)
            sp.dma_start(annex[:, :], table_p).then_inc(sorted_in, 16)

        def sync_l0(sp):
            sp.wait_ge(counted, done(CH - 1))
            sp.wait_ge(onehots, done(CH - 1))
            sp.dma_start(w_a, p0["W_self"]).then_inc(w_self_in, 16)
            sp.wait_ge(self_done, 1)
            with sp.Fori(0, R) as r:
                sp.wait_ge(a_used, r + 1)
                sp.dma_start(w_a, p0["W_rel"][ds(r, 1)].rearrange("a p k o -> p (a k) o")).then_inc(w_a_in, 16)
                sp.wait_ge(b_used, r + 1)
                sp.dma_start(w_b, p0["W_rel"][ds(r + R, 1)].rearrange("a p k o -> p (a k) o")).then_inc(w_b_in, 16)

        def pool_sort(pool):
            g = nc.gpsimd
            g.iota(node_f[:, :], pattern=[[1, N]], base=0, channel_multiplier=0,
                   allow_small_or_imprecise_dtypes=True).then_inc(consts, 1)
            g.iota(node_h[:, :], pattern=[[1, N]], base=0, channel_multiplier=0,
                   allow_small_or_imprecise_dtypes=True).then_inc(consts, 1)
            g.iota(group_no, pattern=[[1, G]], base=0, channel_multiplier=0,
                   allow_small_or_imprecise_dtypes=True).then_inc(consts, 1)
            g.iota(chunk_no, pattern=[[1, CH]], base=0, channel_multiplier=0,
                   allow_small_or_imprecise_dtypes=True).then_inc(consts, 1)
            g.memset(ident[:, :], 0.0).then_inc(g_step, 1)
            g.memset(before, 1.0).then_inc(g_step, 1)
            g.memset(ones_m, 1.0).then_inc(consts, 1)
            pool.wait_ge(g_step, 2)
            g.affine_select(out=ident[:, :], in_=ident[:, :], compare_op=ALU.not_equal, fill=1.0, base=0,
                            pattern=[[-1, P]], channel_multiplier=1).then_inc(consts, 1)
            g.affine_select(out=before, in_=before, compare_op=ALU.is_gt, fill=0.0, base=0,
                            pattern=[[1, T]], channel_multiplier=-1).then_inc(consts, 1)
            pool.wait_ge(slots_ready, 1)
            pool.wait_ge(rows_ready, 1)
            pool.wait_ge(attr_in, 16)
            pool.wait_ge(cleared, 16 * PIECES)
            for c in range(EC):
                g.indirect_dma_start(out=table, out_offset=bass.IndirectOffsetOnAxis(ap=pos_i[:, c:c + 1], axis=0),
                                     in_=rows[:, c, :], in_offset=None).then_inc(scattered, 16)

        def pool_l0(pool):
            g = nc.gpsimd
            pool.wait_ge(added, done(CH - 1))
            pool.wait_ge(counted, done(CH - 1))
            pool.wait_ge(onehots, done(CH - 1))
            with pool.Fori(0, R) as r:
                pool.wait_ge(a_used, r + 1)
                pool.wait_ge(deg_done, r + 1)
                by_rel = counts.rearrange("p (t r n) -> p t r n", t=NT, r=R)
                g.tensor_copy(here, by_rel[:, :, ds(r, 1), :].rearrange("p t a n -> p t (a n)")).then_inc(here_ready, 1)

        def transposes(tile):
            for b in range(KD * NT):
                k, t = divmod(b, NT)
                mm = nc.tensor.transpose(PS[:, b // 4, b % 4 * T:(b % 4 + 1) * T], tile[0:T, t, k * P:(k + 1) * P], identT)
                if b % 4 == 3:
                    mm.then_inc(xt_psum, 1)

        def pe_sort(pe):
            pe.wait_ge(consts, 7)
            pe.wait_ge(ranked, 1)
            nc.tensor.matmul(PS[0:T, 0, 0:G], before, cnt[0:T, :], start=True, stop=True)
            nc.tensor.matmul(PS[:, 1, 0:G], ones_m, cnt[0:T, :], start=True, stop=True).then_inc(prefixed, 1)

        def pe_count(pe):
            pe.sem_inc(counted, CREDIT)
            with pe.Fori(0, CH, 2) as c0:
                for j in range(2):
                    c = c0 + j
                    pe.wait_ge(onehots, done(c))
                    pe.wait_ge(added, done(c - 2))
                    for at, n in HALVES_B:
                        nc.tensor.matmul(PS[0:T, 2 * j + at // 512, 0:n], hot_dst_h[j], hot_src_h[j][:, at:at + n],
                                         start=True, stop=True)
                    for at, n in HALVES_B:
                        mm = nc.tensor.matmul(PS[0:T, 4 + 2 * j + at // 512, 0:n], hot_dst_f[j],
                                              hot_src_w[j][:, at:at + n], start=True, stop=True)
                    mm.then_inc(counted, 1)

        def pe_l0(pe):
            t_ = nc.tensor
            pe.wait_ge(x_in, 16)
            pe.wait_ge(added, done(CH - 1))
            transposes(xN)
            pe.wait_ge(xt_ready, NT)
            pe.wait_ge(w_self_in, 16)
            for t in range(NT):
                for k in range(KD):
                    mm = t_.matmul(PS[0:T, t, :], xTk[:, k, t * T:(t + 1) * T], w_a[:, k, :],
                                   start=(k == 0), stop=False, skip_group_check=True)
            mm.then_inc(self_done, 1)
            pe.sem_inc(a_used, 1)
            pe.sem_inc(b_used, 1)
            with pe.Fori(0, R) as r:
                use = [0]

                def bank():
                    u = use[0]
                    use[0] += 1
                    before_ = r * 12 + (u - 3) // 2 + 1 + 2
                    pe.wait_ge(out_act if (u - 3) % 2 == 0 else out_dve, before_)
                    return 5 + u % 3

                pe.wait_ge(here_ready, r + 1)
                block_ = 0
                for n in TURNS:
                    b = bank()
                    for i in range(n):
                        st, t = divmod(block_, NT)
                        block_ += 1
                        mm = t_.transpose(PS[0:T, b, i * T:(i + 1) * T], here[:, t, st * T:(st + 1) * T], identT)
                    mm.then_inc(scratch, 1)
                for side, counts_ in ((0, here), (1, turned3)):
                    if side == 1:
                        pe.wait_ge(out_act, r * 12 + 4 + 2)
                    for k in range(KD):
                        for at, n in HALVES:
                            b = bank()
                            for t in range(NT):
                                mm = t_.matmul(PS[:, b, 0:n], xN[0:T, t, k * P:(k + 1) * P], counts_[:, t, at:at + n],
                                               start=(t == 0), stop=(t == NT - 1))
                            mm.then_inc(scratch, 1)
                for side, (y, w, w_in, used) in enumerate(((y_a, w_a, w_a_in, a_used), (y_b, w_b, w_b_in, b_used))):
                    pe.wait_ge(w_in, 16 * r + 16)
                    pe.wait_ge(out_act, r * 12 + 8 + 4 * side + 2)
                    pe.wait_ge(out_dve, r * 12 + 8 + 4 * side + 2)
                    for t in range(NT):
                        for k in range(KD):
                            mm = t_.matmul(PS[0:T, t, :], y[:, k, t * T:(t + 1) * T], w[:, k, :],
                                           start=False, stop=False, skip_group_check=True)
                    mm.then_inc(used, 1)
            pe.wait_ge(deg_done, R + 1)
            pe.wait_ge(out_act, R * 12 + 2)
            pe.wait_ge(out_dve, R * 12 + 2)
            for t in range(NT):
                mm = t_.transpose(PS[0:2 * R, 5 + t // 4, t % 4 * T:(t % 4 + 1) * T], deg[0:T, t, :], identT)
            mm.then_inc(deg_psum, 1)
            pe.wait_ge(deg_ready, 1)
            pe.wait_ge(bias0_in, 32)
            for t in range(NT):
                mm = t_.matmul(PS[0:T, t, :], deg_t[:, t * T:(t + 1) * T], b_rel[:, :], start=False, stop=True,
                               skip_group_check=True)
            mm.then_inc(acc_done, 1)

        def act_turn(act, turn, to):
            for b in range(NT):
                act.wait_ge(xt_psum, NT * turn + b + 1)
                nc.scalar.copy(to[:, b * 4 * T:(b + 1) * 4 * T], PS[:, b, 0:4 * T]).then_inc(xt_ready, 1)

        def act_deviation(act, turn):
            act.wait_ge(var_ready, turn + 1)
            nc.scalar.activation(sd[0:T, :], rstd[0:T, :], ACT.Sqrt).then_inc(sd_ready, 1)

        def emptied(u):
            if u < len(TURNS):
                at = sum(TURNS[:u]) * T
                n = TURNS[u] * T
                return T, n, turned[:, at:at + n]
            side, v = divmod(u - len(TURNS), 2 * KD)
            k, h = divmod(v, 2)
            at, n = HALVES[h]
            return P, n, (y_a, y_b)[side][:, k, at:at + n]

        def act_l0(act):
            act_turn(act, 0, xT)
            act.sem_inc(out_act, 2)
            with act.Fori(0, R) as r:
                for u in range(0, 24, 2):
                    parts, n, to = emptied(u)
                    act.wait_ge(scratch, r * 24 + u + 1)
                    if u == 0:
                        act.wait_ge(deg_done, r + 1)
                        act.wait_ge(b_used, r + 1)
                    if u == 8:
                        act.wait_ge(a_used, r + 1)
                    nc.scalar.copy(to, PS[0:parts, 5 + u % 3, 0:n]).then_inc(out_act, 1)
            act_deviation(act, 0)

        v_steps = [0]

        def link(dve, ins):
            v_steps[0] += 1
            ins.then_inc(v_step, 1)
            dve.wait_ge(v_step, v_steps[0])

        def dve_sort(dve):
            v = nc.vector

            def step(ins):
                link(dve, ins)

            v.memset(pad, 0.0).then_inc(v_step, 1)
            v_steps[0] += 1
            dve.wait_ge(v_step, v_steps[0])
            v.memset(pad[:, :, DSTL:DSTL + 1], -1.0).then_inc(pad_ready, 1)
            v.memset(rank, 1.0)
            v.memset(ones_g, 1.0)
            step(v.memset(keep, 1.0))
            step(v.memset(keep[:, :, 0:1], 0.0))
            dve.wait_ge(edges_in, 64)
            v.tensor_copy(src_f, src_i)
            v.tensor_copy(dst_f, dst_i)
            step(v.tensor_copy(typ_f, typ_i))
            step(v.tensor_scalar(tile, dst_f, float(T), None, ALU.is_ge))
            for t in range(2, NT):
                step(v.scalar_tensor_tensor(out=tile, in0=dst_f, scalar=float(t * T), in1=tile, op0=ALU.is_ge, op1=ALU.add))
            step(v.scalar_tensor_tensor(out=key, in0=tile, scalar=float(R), in1=typ_f, op0=ALU.mult, op1=ALU.add))
            step(v.scalar_tensor_tensor(out=dst_l, in0=tile, scalar=-float(T), in1=dst_f, op0=ALU.mult, op1=ALU.add))
            dve.wait_ge(consts, 7)
            step(v.tensor_tensor(hot, key.unsqueeze(1).broadcast_to([T, G, EC]),
                                 group_no[0:T, :].unsqueeze(2).broadcast_to([T, G, EC]), ALU.is_equal))
            step(v.tensor_tensor_scan(rank.rearrange("p g c -> p (g c)"), keep.rearrange("p g c -> p (g c)"),
                                      hot.rearrange("p g c -> p (g c)"), 0.0, ALU.mult, ALU.add))
            v.tensor_copy(cnt[0:T, :], rank[:, :, EC - 1:EC].rearrange("p g a -> p (g a)")).then_inc(ranked, 1)
            for col, what in ((SRC, src_f), (DSTL, dst_l), (WGT, wgt)):
                v.tensor_copy(rows[:, :, col:col + 1], what.unsqueeze(2))
            v.tensor_copy(rows[:, :, SRCI:SRCI + 1].bitcast(I32), src_i.unsqueeze(2)).then_inc(rows_ready, 1)
            dve.wait_ge(prefixed, 1)
            step(v.tensor_scalar(chunks_f, PS[:, 1, 0:G], float(P - 1), None, ALU.add))
            step(v.tensor_copy(chunks_i, chunks_f))
            step(v.tensor_scalar(chunks_i, chunks_i, 7, None, ALU.arith_shift_right))
            step(v.tensor_copy(chunks_f, chunks_i))
            step(v.tensor_tensor_scan(upto, ones_g, chunks_f, 0.0, ALU.mult, ALU.add))
            step(v.tensor_tensor(start, upto, chunks_f, ALU.subtract))
            step(v.scalar_tensor_tensor(out=base[0:T, :], in0=start[0:T, :], scalar=float(P), in1=PS[0:T, 0, 0:G],
                                        op0=ALU.mult, op1=ALU.add))
            step(v.tensor_scalar(base[0:T, :], base[0:T, :], -1.0, None, ALU.add))
            step(v.tensor_tensor(rank, rank, base[0:T, :].unsqueeze(2).broadcast_to([T, G, EC]), ALU.add))
            step(v.tensor_tensor(rank, rank, hot, ALU.mult))
            step(v.tensor_reduce(slot_f, rank.rearrange("p g c -> p c g"), X, ALU.add))
            step(v.tensor_copy(slot_i, slot_f))
            v.tensor_scalar(lo_i, slot_i, P - 1, None, ALU.bitwise_and)
            step(v.tensor_scalar(hi_i, slot_i, 7, None, ALU.arith_shift_right))
            v.tensor_copy(hi_f, hi_i)
            step(v.tensor_copy(lo_f, lo_i))
            step(v.scalar_tensor_tensor(out=slot_f, in0=lo_f, scalar=float(CH), in1=hi_f, op0=ALU.mult, op1=ALU.add))
            v.tensor_copy(pos_i, slot_f).then_inc(slots_ready, 1)
            step(v.tensor_tensor(past, upto[0:1, :].unsqueeze(1).broadcast_to([1, CH, G]),
                                 chunk_no.unsqueeze(2).broadcast_to([1, CH, G]), ALU.is_le))
            step(v.tensor_reduce(group_f, past, X, ALU.add))
            step(v.tensor_scalar(group_f, group_f, float(G - 1), None, ALU.min))
            step(v.tensor_copy(group[:, :], group_f))
            step(v.tensor_scalar(tile_of[:, :], group[:, :], 3, None, ALU.arith_shift_right))

        def dve_count(dve):
            v = nc.vector
            v.memset(arena[0:T, :], 0.0)
            dve.wait_ge(cleared, 16 * PIECES)
            link(dve, v.memset(wadj[0:T, :], 0.0))
            dve.sem_inc(onehots, CREDIT)
            dve.sem_inc(added, CREDIT)
            dve.wait_ge(sorted_in, 16)

            def one_hots(c, j):
                col = lambda n: sorted_rows[:, ds(c, 1), n:n + 1].rearrange("p a b -> p (a b)")
                v.tensor_scalar(hot_dst_h[j], node_h[:, 0:T], col(DSTL), None, ALU.is_equal)
                v.tensor_scalar(hot_src_h[j], node_h[:, :], col(SRC), None, ALU.is_equal)
                v.tensor_scalar(hot_dst_f[j], node_f[:, 0:T], col(DSTL), None, ALU.is_equal)
                v.tensor_scalar(hot_src_w[j], node_f[:, :], col(SRC), col(WGT), ALU.is_equal, ALU.mult).then_inc(onehots, 1)

            def add(c, j):
                g = dve.value_load(group[0:1, ds(c, 1)], min_val=0, max_val=G - 1)
                t = dve.value_load(tile_of[0:1, ds(c, 1)], min_val=0, max_val=NT - 1)
                dve.wait_ge(counted, done(c))
                dve.wait_ge(added, done(c - 1))
                to = counts[:, ds(g * N, N)]
                v.tensor_tensor(to, two_banks(2 * j, T), to, ALU.add)
                to = wadj[0:T, ds(t * N, N)]
                v.tensor_tensor(to, two_banks(4 + 2 * j, T), to, ALU.add).then_inc(added, 1)

            one_hots(0, 0)
            with dve.Fori(0, CH - 2, 2) as c0:
                for j in range(2):
                    one_hots(c0 + j + 1, 1 - j)
                    add(c0 + j, j)
            one_hots(CH - 1, 1)
            add(CH - 2, 0)
            add(CH - 1, 1)

        def dve_norm(dve, turn, scale_row=None, shift_row=None):
            v = nc.vector
            for t in range(NT):
                ins = v.bn_stats(stat[0:T, t, :], xN[0:T, t, :])
            link(dve, ins)
            for t in range(NT):
                ins = v.bn_aggr(mv[0:T, t, :], stat[0:T, t, :])
            link(dve, ins)
            v.tensor_scalar(rstd[0:T, :], mv[0:T, :, 1:2].rearrange("p t a -> p (t a)"), EPS, None,
                            ALU.add).then_inc(var_ready, 1)
            dve.wait_ge(sd_ready, turn + 1)
            link(dve, v.reciprocal(rstd[0:T, :], sd[0:T, :]))
            for t in range(NT):
                ins = v.tensor_scalar(xN[0:T, t, :], xN[0:T, t, :], mv[0:T, t, 0:1], rstd[0:T, t:t + 1],
                                      ALU.subtract, ALU.mult)
            if scale_row is not None:
                link(dve, ins)
                link(dve, v.tensor_tensor(xN[0:T, :, :], xN[0:T, :, :], over_tiles(scale_row), ALU.mult))
                ins = v.tensor_tensor(xN[0:T, :, :], xN[0:T, :, :], over_tiles(shift_row), ALU.add)
            ins.then_inc(x_ready, 1)
            dve.wait_ge(x_ready, turn + 1)

        def over_tiles(row):
            return row[0:T, :].unsqueeze(1).broadcast_to([T, NT, D])

        def dve_relu_and_add(dve, bias):
            v = nc.vector
            for t in range(NT):
                ins = v.tensor_tensor(sums[:, t, :], PS[0:T, t, :], bias[0:T, :], ALU.add)
            link(dve, ins)
            for t in range(NT):
                ins = v.scalar_tensor_tensor(out=xN[0:T, t, :], in0=sums[:, t, :], scalar=0.0, in1=xN[0:T, t, :],
                                             op0=ALU.max, op1=ALU.add)
            link(dve, ins)

        def dve_l0(dve):
            v = nc.vector
            v.memset(pairs[0:T, :], 0.0).then_inc(deg_done, 1)
            dve.sem_inc(out_dve, 2)
            with dve.Fori(0, R) as r:
                for u in range(1, 24, 2):
                    parts, n, to = emptied(u)
                    dve.wait_ge(scratch, r * 24 + u + 1)
                    if u == 1:
                        dve.wait_ge(b_used, r + 1)
                    if u == 9:
                        dve.wait_ge(a_used, r + 1)
                    v.tensor_copy(to, PS[0:parts, 5 + u % 3, 0:n]).then_inc(out_dve, 1)
                dve.wait_ge(out_act, r * 12 + 4 + 2)
                dve.wait_ge(out_dve, r * 12 + 12 + 2)
                v.tensor_reduce(deg[0:T, :, ds(r, 1)].rearrange("p t a -> p (t a)"), turned3, X, ALU.add)
                v.tensor_reduce(deg[0:T, :, ds(r + R, 1)].rearrange("p t a -> p (t a)"), here, X, ALU.add)
                v.tensor_tensor(pairs_t, pairs_t, here, ALU.add).then_inc(deg_done, 1)
                dve.wait_ge(deg_done, r + 2)
            dve.wait_ge(deg_psum, 1)
            v.tensor_copy(deg_t[:, 0:4 * T], PS[0:2 * R, 5, 0:4 * T])
            v.tensor_copy(deg_t[:, 4 * T:N], PS[0:2 * R, 6, 0:T]).then_inc(deg_ready, 1)
            dve.wait_ge(acc_done, 1)
            dve.wait_ge(bias0_in, 32)
            dve_relu_and_add(dve, b_self)
            dve_norm(dve, 0)

        def sync_l1(sp):
            sp.wait_ge(here_ready, R)
            sp.dma_start(u_w, p1["U"]).then_inc(p1_in, 16)
            sp.dma_start(vt_w, p1["Vt"]).then_inc(p1_in, 16)
            load_rows(sp, s_row, p1["s"], p1_in, T)
            load_rows(sp, b1_row, p1["bias"], p1_in, T)
            load_rows(sp, be_row, p2["b_e"], p1_in, T)

        def pe_l1(pe):
            t_ = nc.tensor
            pe.wait_ge(x_ready, 1)
            transposes(xN)
            pe.wait_ge(xt_ready, 2 * NT)
            pe.wait_ge(p1_in, 16 * 5)
            for t in range(NT):
                for k in range(KD):
                    mm = t_.matmul(PS[0:T, 5, t * RANK:(t + 1) * RANK], xTk[:, k, t * T:(t + 1) * T], u_w[:, k, :],
                                   start=(k == 0), stop=(k == KD - 1))
            mm.then_inc(support_psum, 1)
            pe.wait_ge(support_ready, 1)
            for h, (at, n) in enumerate(HALVES):
                for t in range(NT):
                    mm = t_.matmul(PS[0:RANK, 6 + h, 0:n], support[:, t, :], wadj_t[:, t, at:at + n],
                                   start=(t == 0), stop=(t == NT - 1))
            mm.then_inc(mixed_psum, 1)
            pe.wait_ge(mixed_ready, 1)
            for t in range(NT):
                mm = t_.matmul(PS[0:T, t, :], mixed[:, t * T:(t + 1) * T], vt_w, start=True, stop=True)
            mm.then_inc(l1_psum, 1)

        def act_l1(act):
            act.wait_ge(clipped, 1)
            nc.scalar.activation(ln_pairs, ln_pairs, ACT.Ln).then_inc(logs_ready, 1)
            act_turn(act, 1, xT)
            act.wait_ge(mixed_psum, 1)
            for h, (at, n) in enumerate(HALVES):
                ins = nc.scalar.copy(mixed[:, at:at + n], PS[0:RANK, 6 + h, 0:n])
            ins.then_inc(mixed_ready, 1)
            act_deviation(act, 1)

        def dve_l1(dve):
            v = nc.vector
            link(dve, v.tensor_reduce(has_in[0:T, :], pairs_t, X, ALU.max))
            v.tensor_scalar(has_in[0:T, :], has_in[0:T, :], 1.0, None, ALU.min)
            link(dve, v.tensor_scalar(ln_pairs, pairs[0:T, :], 1.0, None, ALU.max))
            v.tensor_scalar(pairs[0:T, :], pairs[0:T, :], 0.0, FAR, ALU.is_equal, ALU.mult).then_inc(clipped, 1)
            dve.wait_ge(p1_in, 16 * 5)
            dve.wait_ge(support_psum, 1)
            v.tensor_tensor(support, PS[0:T, 5, 0:NT * RANK].rearrange("p (t n) -> p t n", n=RANK),
                            s_row.unsqueeze(1).broadcast_to([T, NT, RANK]), ALU.mult).then_inc(support_ready, 1)
            dve.wait_ge(logs_ready, 1)
            dve.wait_ge(clipped, 1)
            v.scalar_tensor_tensor(out=pairs[0:T, :], in0=ln_pairs, scalar=float(HD) ** 0.5, in1=pairs[0:T, :],
                                   op0=ALU.mult, op1=ALU.add)
            dve.wait_ge(l1_psum, 1)
            dve_relu_and_add(dve, b1_row)
            dve_norm(dve, 1)
            v.tensor_tensor(xb, xN[0:T, :, :], over_tiles(be_row), ALU.add).then_inc(xb_ready, 1)

        def sync_l2(sp):
            sp.wait_ge(acc_done, 1)
            for to, what in ((w1, "W1"), (w2, "W2"), (w_e, "W_e"), (b1_c, "b1"), (g1_c, "g1"), (beta1_c, "beta1"),
                             (b2_c[:, 0:KD], "b2"), (g2_c[:, 0:KD], "g2"), (beta2_c[:, 0:KD], "beta2")):
                sp.dma_start(to, p2[what]).then_inc(p2_in, 16)
            load_rows(sp, eps_c, p2["eps"], p2_in, T)
            sp.wait_ge(xb_ready, 1)
            sp.dma_start(xb_rows.rearrange("(t p) d -> p t d", p=T), xb).then_inc(xb_stored, 16)
            with sp.Fori(0, CH // 4) as step:
                c0 = step * 4
                for pair in range(2):
                    c = c0 + 2 * pair
                    sp.wait_ge(attr_psum, done(c - 3))
                    sp.wait_ge(hot_ready, done(c - 3))
                    sp.wait_ge(msg_sum, done(c - 3))
                    sp.dma_start(row_buf[:, 2 * pair:2 * pair + 2, :].rearrange("p c e -> p (c e)"),
                                 table_p[:, ds(c * ROW, 2 * ROW)]).then_inc(rows_in[pair], 16)

        def rows_there(eng, c, j):
            eng.wait_ge(rows_in[j // 2], (c - j) * 4 + 16)

        def pool_l2(pool):
            g = nc.gpsimd
            pool.wait_ge(xb_stored, 16)
            with pool.Fori(0, CH // 4) as step:
                c0 = step * 4
                for j in range(4):
                    c = c0 + j
                    rows_there(pool, c, j)
                    pool.wait_ge(msg_sum, done(c - 4))
                    pool.sem_inc(pool_tick, 1)
                    g.indirect_dma_start(out=x_src[:, j, :], out_offset=None, in_=xb_rows,
                                         in_offset=bass.IndirectOffsetOnAxis(
                                             ap=row_buf[:, j, SRCI:SRCI + 1].bitcast(I32), axis=0)
                                         ).then_inc(src_in[j], 16)

        def pe_l2(pe):
            t_ = nc.tensor
            pe.sem_inc(attr_psum, CREDIT)
            pe.sem_inc(edge_psum, CREDIT)
            pe.sem_inc(agg_psum, CREDIT)
            pe.wait_ge(p2_in, 16 * 10)
            pe.wait_ge(x_ready, 2)

            def turn_attr(c, j):
                rows_there(pe, c, j)
                pe.wait_ge(attr_out, done(c - 2))
                t_.transpose(PS[0:ROW, j % 2, 0:P], row_buf[:, j, :], ident[:, :]).then_inc(attr_psum, 1)

            def edge_product(c, j):
                pe.wait_ge(attr_out, done(c))
                pe.wait_ge(msg_sum, done(c - 2))
                t_.matmul(PS[:, 2 + j % 2, :], attr_t[:, j % 2, :], w_e, start=True, stop=True).then_inc(edge_psum, 1)

            def sum_by_dst(c, j):
                pe.wait_ge(msg_ready, done(c))
                pe.wait_ge(hot_ready, done(c))
                pe.wait_ge(agg_added, done(c - 2))
                t_.matmul(PS[0:T, 4 + j % 2, :], hot_dst[:, j % 2, 0:T], msg[:, j % 2, :],
                          start=True, stop=True).then_inc(agg_psum, 1)

            turn_attr(0, 0)
            turn_attr(1, 1)
            edge_product(0, 0)
            with pe.Fori(0, CH // 4 - 1) as step:
                c0 = step * 4
                for j in range(4):
                    turn_attr(c0 + j + 2, (j + 2) % 4)
                    edge_product(c0 + j + 1, (j + 1) % 4)
                    sum_by_dst(c0 + j, j)
            for j in range(4):
                c = CH - 4 + j
                if j < 2:
                    turn_attr(c + 2, j + 2)
                if j < 3:
                    edge_product(c + 1, j + 1)
                sum_by_dst(c, j)

            pe.wait_ge(h_ready, 1)
            transposes(agg)
            pe.wait_ge(xt_ready, 3 * NT)
            use = 0
            for m in range(2 * KD):
                for at, n in HALVES:
                    if use >= 8:
                        pe.wait_ge(z_out, use - 7)
                    for k in range(KD):
                        mm = t_.matmul(PS[:, use % 8, 0:n], w1[:, k, m * P:(m + 1) * P], h_tk[:, k, at:at + n],
                                       start=(k == 0), stop=(k == KD - 1))
                    mm.then_inc(z_psum, 1)
                    use += 1
            for m in range(KD):
                for at, n in HALVES:
                    pe.wait_ge(z_out, use - 7)
                    for k in range(2 * KD):
                        if m == 0 and at == 0:
                            pe.wait_ge(act_out, k + 1)
                        mm = t_.matmul(PS[:, use % 8, 0:n], w2[:, k, m * P:(m + 1) * P], z1[:, k, at:at + n],
                                       start=(k == 0), stop=(k == 2 * KD - 1))
                    mm.then_inc(z_psum, 1)
                    use += 1
            pe.wait_ge(z_out, use)
            pe.wait_ge(act_out, 3 * KD)
            for t in range(NT):
                for k in range(KD):
                    mm = t_.transpose(PS[0:T, t, k * P:(k + 1) * P], z2[:, k, t * T:(t + 1) * T], ident[:, :])
            mm.then_inc(back_psum, 1)

        def act_l2(act):
            act.sem_inc(attr_out, CREDIT)
            act.sem_inc(msg_ready, CREDIT)

            def keep_attr(c, j):
                act.wait_ge(attr_psum, done(c))
                act.wait_ge(edge_psum, done(c - 2))
                nc.scalar.copy(attr_t[:, j % 2, :], PS[0:EA, j % 2, 0:P]).then_inc(attr_out, 1)

            def relu(c, j):
                act.wait_ge(msg_sum, done(c))
                act.wait_ge(agg_psum, done(c - 2))
                nc.scalar.activation(msg[:, j % 2, :], msg_in[:, j % 2, :], ACT.Relu).then_inc(msg_ready, 1)

            keep_attr(0, 0)
            keep_attr(1, 1)
            relu(0, 0)
            with act.Fori(0, CH // 4 - 1) as step:
                c0 = step * 4
                for j in range(4):
                    keep_attr(c0 + j + 2, (j + 2) % 4)
                    relu(c0 + j + 1, (j + 1) % 4)
            for j in range(3):
                if j < 2:
                    keep_attr(CH - 2 + j, j + 2)
                relu(CH - 3 + j, j + 1)
            act_turn(act, 2, h_t)

            use = 0
            tiles = 0
            for phase, (z, bias, parts) in enumerate(((z1, b1_c, 2 * KD), (z2, b2_c, KD))):
                for m in range(parts):
                    for at, n in HALVES:
                        act.wait_ge(z_psum, use + 1)
                        nc.scalar.activation(z[:, m, at:at + n], PS[:, use % 8, 0:n], ACT.Identity,
                                             bias=bias[:, m:m + 1]).then_inc(z_out, 1)
                        use += 1
                act.wait_ge(bn_var, phase + 1)
                nc.scalar.activation(bn_sd[:, 0:parts], bn_ve[:, 0:parts], ACT.Sqrt).then_inc(bn_dev, 1)
                act.wait_ge(bn_ready, phase + 1)
                for m in range(parts):
                    nc.scalar.activation(z[:, m, :], z[:, m, :], ACT.Silu, bias=shift_c[:, m:m + 1],
                                         scale=scale_c[:, m:m + 1]).then_inc(act_out, 1)
            act_deviation(act, 2)

        def dve_l2(dve):
            v = nc.vector
            link(dve, v.memset(agg, 0.0))
            dve.sem_inc(msg_sum, CREDIT)
            dve.sem_inc(hot_ready, CREDIT)
            dve.sem_inc(agg_added, CREDIT)

            def message(c, j):
                rows_there(dve, c, j)
                dve.wait_ge(agg_psum, done(c - 2))
                v.tensor_scalar(hot_dst[:, j % 2, 0:T], node_f[:, 0:T], row_buf[:, j, DSTL:DSTL + 1], None,
                                ALU.is_equal).then_inc(hot_ready, 1)
                dve.wait_ge(edge_psum, done(c))
                dve.wait_ge(src_in[j], (c - j) * 4 + 16)
                dve.wait_ge(msg_ready, done(c - 2))
                v.tensor_tensor(msg_in[:, j % 2, :], PS[:, 2 + j % 2, :], x_src[:, j, :], ALU.add).then_inc(msg_sum, 1)

            def add(c, j):
                t = dve.value_load(tile_of[0:1, ds(c, 1)], min_val=0, max_val=NT - 1)
                dve.wait_ge(agg_psum, done(c))
                dve.wait_ge(agg_added, done(c - 1))
                to = agg[:, ds(t, 1), :].rearrange("p a d -> p (a d)")
                v.tensor_tensor(to, PS[0:T, 4 + j % 2, :], to, ALU.add).then_inc(agg_added, 1)

            message(0, 0)
            with dve.Fori(0, CH // 4 - 1) as step:
                c0 = step * 4
                for j in range(4):
                    message(c0 + j + 1, (j + 1) % 4)
                    add(c0 + j, j)
            for j in range(4):
                if j < 3:
                    message(CH - 3 + j, j + 1)
                add(CH - 4 + j, j)
            dve.wait_ge(agg_added, done(CH - 1))
            dve.wait_ge(p2_in, 16 * 10)
            link(dve, v.tensor_scalar(eps_c, eps_c, 1.0, None, ALU.add))
            v.scalar_tensor_tensor(out=agg, in0=xN[0:T, :, :], scalar=eps_c, in1=agg, op0=ALU.mult,
                                   op1=ALU.add).then_inc(h_ready, 1)
            out_uses = 0
            for phase, (z, parts, gain, offset) in enumerate(((z1, 2 * KD, g1_c, beta1_c), (z2, KD, g2_c, beta2_c))):
                for m in range(parts):
                    out_uses += 2
                    dve.wait_ge(z_out, out_uses)
                    for h, (at, n) in enumerate(HALVES):
                        ins = v.bn_stats(bn_stat[:, m, 6 * h:6 * h + 6], z[:, m, at:at + n])
                link(dve, ins)
                for m in range(parts):
                    ins = v.bn_aggr(bn_mv[:, m, :], bn_stat[:, m, :].rearrange("p (a b) -> p a b", b=6))
                link(dve, ins)
                mean = bn_mv[:, 0:parts, 0:1].rearrange("p m a -> p (m a)")
                var = bn_mv[:, 0:parts, 1:2].rearrange("p m a -> p (m a)")
                v.tensor_scalar(bn_ve[:, 0:parts], var, EPS, None, ALU.add).then_inc(bn_var, 1)
                dve.wait_ge(bn_dev, phase + 1)
                link(dve, v.reciprocal(bn_ve[:, 0:parts], bn_sd[:, 0:parts]))
                link(dve, v.tensor_tensor(scale_c[:, 0:parts], bn_ve[:, 0:parts], gain[:, 0:parts], ALU.mult))
                link(dve, v.tensor_tensor(bn_ve[:, 0:parts], mean, scale_c[:, 0:parts], ALU.mult))
                v.tensor_tensor(shift_c[:, 0:parts], offset[:, 0:parts], bn_ve[:, 0:parts],
                                ALU.subtract).then_inc(bn_ready, 1)
            dve.wait_ge(back_psum, 1)
            for t in range(NT):
                ins = v.tensor_tensor(xN[0:T, t, :], PS[0:T, t, :], xN[0:T, t, :], ALU.add)
            link(dve, ins)
            dve_norm(dve, 2)

        def sync_l3(sp):
            sp.wait_ge(x_ready, 3)
            for to, row in ((mb2_row, p3["b2"]), (ln_g, p3["ln_g"]), (ln_b, p3["ln_b"])):
                load_rows(sp, to, row, l3_rows, T)
            sp.dma_start(mb1_c, p3["b1"]).then_inc(l3_rows, 16)
            with sp.Fori(0, LAYERS) as l:
                sp.wait_ge(w_used, l + 1)
                for n, name in enumerate(("Wq", "Wk", "Wv", "Ws")):
                    sp.dma_start(w_qkvs[n], p3[name][ds(l, 1)].rearrange("a p k o -> p (a k) o")).then_inc(l3_in, 16)
                sp.wait_ge(qk_out, l * 4 * KD + 1)
                sp.wait_ge(vs_out, l * 2 * NT + 1)
                for to, name in ((bq_c, "bq"), (bk_c, "bk")):
                    sp.dma_start(to, p3[name][ds(l, 1)].rearrange("a p k -> p (a k)")).then_inc(l3_in, 16)
                for to, name in ((bv_row, "bv"), (bs_row, "bs")):
                    sp.dma_start(to, p3[name][ds(l, 1)].to_broadcast((T, D))).then_inc(l3_in, 16)
            sp.dma_start(mlp1, p3["W1"]).then_inc(mlp_in, 16)
            sp.dma_start(mlp2, p3["W2"]).then_inc(mlp_in, 16)
            sp.wait_ge(x_ready, 6)
            sp.dma_start(out.rearrange("(t p) d -> p t d", p=T), xN[0:T, :, :]).then_inc(stored, 16)
            sp.wait_ge(stored, 16)

        STEPS = NT * HEADS

        def through(n):
            return n + 1 + 2

        def pe_l3(pe):
            t_ = nc.tensor
            pe.wait_ge(x_ready, 3)
            for q in (w_used, ):
                pe.sem_inc(q, 1)
            for q in (score_psum, turn_psum, pv_done):
                pe.sem_inc(q, 2)
            with pe.Fori(0, LAYERS) as l:
                pe.wait_ge(l3_x, l + 1)
                transposes(xN)
                pe.wait_ge(xt_ready, NT * 3 + NT + l * NT)
                pe.wait_ge(l3_in, l * 128 + 128)
                use = 0
                for w in range(2):
                    for m in range(KD):
                        for at, n in HALVES:
                            if use >= 8:
                                pe.wait_ge(qk_out, l * 4 * KD + use - 7 + 1)
                            for k in range(KD):
                                mm = t_.matmul(PS[:, use % 8, 0:n], w_qkvs[w][:, k, m * P:(m + 1) * P],
                                               xTk[:, k, at:at + n], start=(k == 0), stop=(k == KD - 1))
                            mm.then_inc(proj, 1)
                            use += 1
                for w in range(2, 4):
                    for t in range(NT):
                        if use < 24:
                            pe.wait_ge(qk_out, l * 4 * KD + use - 7 + 1)
                        else:
                            pe.wait_ge(vs_out, l * 2 * NT + use - 23 + 1)
                        for k in range(KD):
                            mm = t_.matmul(PS[0:T, use % 8, :], xTk[:, k, t * T:(t + 1) * T], w_qkvs[w][:, k, :],
                                           start=(k == 0), stop=(k == KD - 1))
                        mm.then_inc(proj, 1)
                        use += 1
                pe.wait_ge(qk_out, l * 4 * KD + 4 * KD + 1)
                pe.wait_ge(vs_out, l * 2 * NT + 2 * NT + 1)
                pe.sem_inc(w_used, 1)

                def score(n):
                    t, h = divmod(n, HEADS)
                    part = slice(HD * (h % 2), HD * (h % 2) + HD)
                    pe.wait_ge(score_out, through(l * STEPS + n - 2))
                    for at, m in HALVES_B:
                        mm = t_.matmul(PS[0:T, n % 2 * 2 + at // 512, 0:m], q_t[part, h // 2, t * T:(t + 1) * T],
                                       k_t[part, h // 2, at:at + m], start=True, stop=True)
                    mm.then_inc(score_psum, 1)

                def turn(n):
                    pe.wait_ge(probs_out, through(l * STEPS + n))
                    pe.wait_ge(turn_out, through(l * STEPS + n - 1))
                    for st in range(NT):
                        mm = t_.transpose(PS[0:T, 4 + st // 4, st % 4 * P:st % 4 * P + T],
                                          probs[:, n % 2, st * T:(st + 1) * T], identT)
                    mm.then_inc(turn_psum, 1)

                def mix(n):
                    t, h = divmod(n, HEADS)
                    pe.wait_ge(turn_out, through(l * STEPS + n))
                    if h == 0:
                        pe.wait_ge(tile_out, through(l * NT + t - 2))
                    for st in range(NT):
                        mm = t_.matmul(PS[0:T, 6 + t % 2, h * HD:(h + 1) * HD], probs_t[:, n % 2, st * T:(st + 1) * T],
                                       val[:, st, h * HD:(h + 1) * HD], start=(st == 0), stop=(st == NT - 1))
                    mm.then_inc(pv_done, 1)

                score(0)
                for n in range(STEPS):
                    if n + 1 < STEPS:
                        score(n + 1)
                    turn(n)
                    if n >= 1:
                        mix(n - 1)
                mix(STEPS - 1)
            pe.wait_ge(x_ready, 4)
            transposes(xN)
            pe.wait_ge(xt_ready, NT * (4 + LAYERS))
            pe.wait_ge(mlp_in, 32)
            use = 0
            for m in range(2 * KD):
                for at, n in HALVES:
                    if use >= 8:
                        pe.wait_ge(hid_out, use - 7)
                    for k in range(KD):
                        mm = t_.matmul(PS[:, use % 8, 0:n], mlp1[:, k, m * P:(m + 1) * P], xTk[:, k, at:at + n],
                                       start=(k == 0), stop=(k == KD - 1))
                    mm.then_inc(hid_psum, 1)
                    use += 1
            pe.wait_ge(hid_out, use)
            for t in range(NT):
                for k in range(2 * KD):
                    mm = t_.matmul(PS[0:T, t, :], hid[:, k, t * T:(t + 1) * T], mlp2[:, k, :],
                                   start=(k == 0), stop=(k == 2 * KD - 1))
            mm.then_inc(mlp_psum, 1)

        def act_l3(act):
            act.sem_inc(qk_out, 1)
            act.sem_inc(probs_out, 2)
            act.sem_inc(turn_out, 2)
            with act.Fori(0, LAYERS) as l:
                for b in range(NT):
                    act.wait_ge(xt_psum, 3 * NT + l * NT + b + 1)
                    nc.scalar.copy(xT[:, b * 4 * T:(b + 1) * 4 * T], PS[:, b, 0:4 * T]).then_inc(xt_ready, 1)
                act.wait_ge(l3_in, l * 128 + 128)
                use = 0
                for to, bias in ((q_t, bq_c), (k_t, bk_c)):
                    for m in range(KD):
                        for at, n in HALVES:
                            act.wait_ge(proj, l * (4 * KD + 2 * NT) + use + 1)
                            nc.scalar.activation(to[:, m, at:at + n], PS[:, use % 8, 0:n], ACT.Identity,
                                                 bias=bias[:, m:m + 1]).then_inc(qk_out, 1)
                            use += 1

                def exponent(n):
                    act.wait_ge(score_out, through(l * STEPS + n))
                    act.wait_ge(turn_psum, through(l * STEPS + n - 2))
                    nc.scalar.activation(probs[:, n % 2, :], scores[:, n % 2, :], ACT.Exp,
                                         bias=minus_top[:, n % 4:n % 4 + 1], scale=float(HD) ** -0.5,
                                         accum_out=denom[:, n // HEADS, n % HEADS:n % HEADS + 1]).then_inc(probs_out, 1)

                def keep_turned(n):
                    act.wait_ge(turn_psum, through(l * STEPS + n))
                    act.wait_ge(pv_done, through(l * STEPS + n - 2))
                    nc.scalar.copy(probs_t[:, n % 2, :].rearrange("p (t n) -> p t n", n=T),
                                   two_banks(4, T, NT * P).rearrange("p (t n) -> p t n", n=P)[:, :, 0:T]
                                   ).then_inc(turn_out, 1)

                exponent(0)
                for n in range(STEPS):
                    if n + 1 < STEPS:
                        exponent(n + 1)
                    keep_turned(n)
            act_deviation(act, 3)
            act_turn(act, 3 + LAYERS, xT)
            act.wait_ge(l3_rows, 64)
            use = 0
            for m in range(2 * KD):
                for at, n in HALVES:
                    act.wait_ge(hid_psum, use + 1)
                    nc.scalar.activation(hid[:, m, at:at + n], PS[:, use % 8, 0:n], ACT.Relu,
                                         bias=mb1_c[:, m:m + 1]).then_inc(hid_out, 1)
                    use += 1
            act_deviation(act, 4)
            act_deviation(act, 5)

        def dve_l3(dve):
            v = nc.vector
            dve.sem_inc(vs_out, 1)
            dve.sem_inc(score_out, 2)
            dve.sem_inc(tile_out, 2)
            v.tensor_copy(enc, xN[0:T, :, :]).then_inc(l3_x, 1)
            with dve.Fori(0, LAYERS) as l:
                dve.wait_ge(l3_in, l * 128 + 128)
                use = 16
                for to, row in ((val, bv_row), (rest, bs_row)):
                    for t in range(NT):
                        dve.wait_ge(proj, l * (4 * KD + 2 * NT) + use + 1)
                        v.tensor_tensor(to[:, t, :], PS[0:T, use % 8, :], row, ALU.add).then_inc(vs_out, 1)
                        use += 1
                dve.wait_ge(vs_out, l * 2 * NT + 2 * NT + 1)
                v.tensor_tensor(rest, rest, enc, ALU.add).then_inc(o_step, 1)

                def mask(n):
                    t = n // HEADS
                    dve.wait_ge(score_psum, through(l * STEPS + n))
                    dve.wait_ge(probs_out, through(l * STEPS + n - 2))
                    dve.sem_inc(tick, 1)
                    v.tensor_tensor_reduce(out=scores[:, n % 2, :], in0=two_banks(n % 2 * 2, T), in1=pairs_t[:, t, :],
                                           scale=1.0, scalar=3 * FAR, op0=ALU.add, op1=ALU.max,
                                           accum_out=top[:, n % 4:n % 4 + 1]).then_inc(top_ready, 1)
                    dve.wait_ge(top_ready, l * STEPS + n + 1)
                    v.tensor_scalar(minus_top[:, n % 4:n % 4 + 1], top[:, n % 4:n % 4 + 1], -float(HD) ** -0.5, None,
                                    ALU.mult).then_inc(score_out, 1)

                def finish(t):
                    at = l * (1 + 4 * NT) + 1 + 4 * t
                    dve.wait_ge(pv_done, through(l * STEPS + (t + 1) * HEADS - 1))
                    dve.wait_ge(o_step, at)
                    v.tensor_scalar(inv[:, t, :], denom[:, t, :], 1e-16, None, ALU.add).then_inc(o_step, 1)
                    dve.wait_ge(o_step, at + 1)
                    v.reciprocal(inv[:, t, :], inv[:, t, :]).then_inc(o_step, 1)
                    dve.wait_ge(o_step, at + 2)
                    v.tensor_scalar(inv[:, t, :], inv[:, t, :], has_in[0:T, t:t + 1], None, ALU.mult).then_inc(o_step, 1)
                    dve.wait_ge(o_step, at + 3)
                    v.tensor_tensor(xN[0:T, t, :].rearrange("p (h d) -> p h d", d=HD),
                                    PS[0:T, 6 + t % 2, :].rearrange("p (h d) -> p h d", d=HD),
                                    inv[:, t, :].unsqueeze(2).broadcast_to([T, HEADS, HD]), ALU.mult).then_inc(tile_out, 1)
                    dve.wait_ge(tile_out, through(l * NT + t))
                    v.tensor_tensor(xN[0:T, t, :], xN[0:T, t, :], rest[:, t, :], ALU.add).then_inc(o_step, 1)

                for n in range(STEPS):
                    mask(n)
                    if n >= HEADS + 2 and n % HEADS == 2:
                        finish(n // HEADS - 1)
                finish(NT - 1)
                dve.wait_ge(o_step, (l + 1) * (1 + 4 * NT))
                dve.sem_inc(l3_x, 1)
            dve.wait_ge(l3_rows, 64)
            dve_norm(dve, 3, ln_g, ln_b)
            dve.wait_ge(mlp_psum, 1)
            link(dve, v.tensor_tensor(xN[0:T, :, :], xN[0:T, :, :], over_tiles(mb2_row), ALU.add))
            for t in range(NT):
                ins = v.tensor_tensor(xN[0:T, t, :], PS[0:T, t, :], xN[0:T, t, :], ALU.add)
            link(dve, ins)
            dve_norm(dve, 4, ln_g, ln_b)
            for _ in range(2):
                link(dve, v.tensor_tensor(xN[0:T, :, :], xN[0:T, :, :], enc, ALU.add))
            dve_norm(dve, 5)

        @block.sync
        def _(sp):
            sync_sort(sp)
            sync_l0(sp)
            sync_l1(sp)
            sync_l2(sp)
            sync_l3(sp)

        @block.gpsimd
        def _(pool):
            pool_sort(pool)
            pool_l0(pool)
            pool_l2(pool)

        @block.tensor
        def _(pe):
            pe_sort(pe)
            pe_count(pe)
            pe_l0(pe)
            pe_l1(pe)
            pe_l2(pe)
            pe_l3(pe)

        @block.scalar
        def _(act):
            act_l0(act)
            act_l1(act)
            act_l2(act)
            act_l3(act)

        @block.vector
        def _(dve):
            dve_sort(dve)
            dve_count(dve)
            dve_l0(dve)
            dve_l1(dve)
            dve_l2(dve)
            dve_l3(dve)


def _tiles(w):
    import numpy as np
    w = np.asarray(w)
    k = w.shape[-2] // 128
    return np.ascontiguousarray(np.moveaxis(w.reshape(w.shape[:-2] + (k, 128, w.shape[-1])), -2, -3))


def _columns(b):
    import numpy as np
    b = np.asarray(b)
    return np.ascontiguousarray(np.moveaxis(b.reshape(b.shape[:-1] + (b.shape[-1] // 128, 128)), -1, -2))


def kernel(**inputs):
    import numpy as np
    import concourse.bacc as bacc
    from concourse.bass_utils import run_bass_kernel_spmd as run

    a = {name: np.ascontiguousarray(v) for name, v in inputs.items()}
    layers = [{}, {}, {}, {}]
    plain = {}
    for name, v in a.items():
        if name[0] == "L" and name[2:6] == "_gnn":
            layers[int(name[1])][name[7:]] = v
        else:
            plain[name] = v
    for name in ("W_self", "W_rel"):
        layers[0][name] = _tiles(np.swapaxes(layers[0][name], -1, -2))
    layers[1]["U"] = _tiles(layers[1]["U"])
    layers[2]["eps"] = layers[2]["eps"].reshape(1)
    for n, names in ((2, ("W1", "W2")), (3, ("Wq", "Wk", "Wv", "Ws", "W1", "W2"))):
        for name in names:
            layers[n][name] = _tiles(layers[n][name])
    for n, names in ((2, ("b1", "g1", "beta1", "b2", "g2", "beta2")), (3, ("bq", "bk", "b1"))):
        for name in names:
            layers[n][name] = _columns(layers[n][name])

    nc = bacc.Bacc("TRN2", target_bir_lowering=False, num_devices=1)
    arrays = {}

    def given(name, v):
        arrays[name] = v
        return nc.dram_tensor(name, v.shape, mybir.dt.from_np(v.dtype), kind="ExternalInput").ap()

    args = [given("in_" + name, plain[name]) for name in ("x", "src", "dst", "edge_attr_64", "edge_type_8", "edge_weight")]
    parameters = [{name: given(f"in_L{n}_{name}", v) for name, v in layer.items()} for n, layer in enumerate(layers)]
    out = nc.dram_tensor("out_x", (N, D), F32, kind="ExternalOutput").ap()
    program(nc, *args, *parameters, out)
    return run(nc, [arrays], core_ids=[0]).results[0]["out_x"]
```

```python
from contextlib import ExitStack

import concourse.bass as bass
from concourse import mybir

F32 = mybir.dt.float32
F16 = mybir.dt.float16
FR = mybir.dt.float32r
I32 = mybir.dt.int32
U16 = mybir.dt.uint16
ALU = mybir.AluOpType
ACT = mybir.ActivationFunctionType
X = mybir.AxisListType.X
ds = bass.ds

P = 128
N = 625
T = 125
NT = N // T
NP = N + 1
D = 512
KD = D // P
E = 20000
EC = E // T
R = 8
G = NT * R
GC = 5
TC = R * GC
CH = G * GC
assert CH * P >= E + G * (P - 1)
STEP = 4
CHX = CH + STEP
EA = 64
ROW = EA + 4
SRC, DSTL, WGT, SRCI = EA, EA + 1, EA + 2, EA + 3
RANK = 64
HEADS, HD = 8, 64
LAYERS = 2
EPS = 1e-5
FAR = -1e30
H0 = 313
HALVES = ((0, H0), (H0, N - H0))
HALVES_P = ((0, 512), (512, NP - 512))
HALVES_B = ((0, 512), (512, N - 512))
TURNS = (4, 4, 4, 4, 3, 3, 3)
T2 = T + 1
PRODUCTS = 1 + 2 * R
BY_POOL = 3
CREDIT = 4
PIECES = 17


def done(c):
    return c + 1 + CREDIT


def program(nc, x, src, dst, edge_attr, edge_type, edge_weight, p0, p1, p2, p3, out):
    with ExitStack() as ctx:
        def sb(name, shape, dt=F32):
            return ctx.enter_context(nc.sbuf_tensor(name, shape, dt))

        def sem(name):
            return ctx.enter_context(nc.semaphore(name))

        table = nc.dram_tensor("sorted_rows", (P * CHX, ROW), F32, kind="Internal").ap()
        xb_rows = nc.dram_tensor("x_plus_b_e", (N, D), F32, kind="Internal").ap()
        products = nc.dram_tensor("x_times_w", (PRODUCTS, N, D), F32, kind="Internal").ap()
        table_p = table.rearrange("(p c) e -> p (c e)", p=P)

        base_bytes = -(-nc.sbuf_base // 64) * 64
        last = [0]

        def up(n):
            return n + (-n) % 8

        def place(name, shape, dt=F32, at=None):
            size = 1
            for n in shape[1:]:
                size *= n
            if at is None:
                at = last[0]
                last[0] += up(size)
            return nc.alloc_sbuf_tensor_at(name, shape, dt, offset=base_bytes + 4 * at)

        xN_at = last[0]
        xN = place("xN", [P, NT, D])
        xT_at = last[0]
        xT = place("xT", [P, KD * N])
        pairs_at = last[0]
        pairs = place("pairs", [P, NT * N])
        wadj = place("wadj", [P, NT * N])
        ident = place("ident", [P, P])
        node_f = place("node_f", [P, NP])
        arena_at = last[0]
        arena = place("arena", [P, G * N])
        counts = place("counts", [P, G * N], U16, arena_at)
        upper_at = arena_at + up(G * N // 2)
        annex_at = last[0]
        annex = place("annex", [P, CHX * ROW])
        group = place("group", [1, CH], I32)
        tile_of = place("tile_of", [1, CH], I32)
        packed = place("packed", [1, 1], I32)
        stat = place("stat", [P, NT, 6])
        mv = place("mv", [P, NT, 2])
        sd = place("sd", [P, NT])
        rstd = place("rstd", [P, NT])
        ident_r = place("ident_r", [P, P], FR)
        has_in = place("has_in", [P, NT])
        w_lo = place("w_lo", [P, CH])
        w_hi = place("w_hi", [P, CH], FR)
        PS = ctx.enter_context(nc.psum_tensor("PS", [P, 8, 512], F32))

        xTk = xT[:, :].rearrange("p (k n) -> p k n", n=N)
        identT = ident[0:T, 0:T]

        def view(tensor, at, shape, parts=P):
            size = 1
            for n in shape:
                size *= n
            v = tensor[0:parts, at:at + size]
            if len(shape) == 2:
                v = v.rearrange("p (a b) -> p a b", b=shape[1])
            return v

        def two_banks(b, parts, n=N):
            return PS[0:parts, b:b + 2, :].rearrange("p b n -> p (b n)")[:, 0:n]

        rows = view(annex, 0, [EC, ROW], T)
        hot = place("hot", [T, G, EC], F16, arena_at)
        keep = place("keep", [T, G, EC], F16, arena_at + G * EC // 2)
        rank = view(arena, G * EC, [G, EC], T)
        past = view(arena, 0, [CH, G], 1)
        (src_f, dst_f, typ_f, wgt, tile, key, dst_l, slot_f, lo_f, hi_f) = [
            view(pairs, n * EC, [EC], T) for n in range(10)]
        (src_i, dst_i, typ_i, slot_i, lo_i, hi_i, pos_i) = [
            view(pairs, n * EC, [EC], T).bitcast(I32) for n in range(10, 17)]
        (cnt, chunks_f, upto, start, base, ones_g) = [view(pairs, 17 * EC + n * G, [G]) for n in range(6)]
        chunks_i = view(pairs, 17 * EC + 6 * G, [G]).bitcast(I32)
        group_no = xT[:, 0:G]
        chunk_no = xT[0:1, G:G + CH]
        group_f = xT[0:1, G + CH:G + 2 * CH]
        before = xT[0:T, 600:600 + T]
        ones_m = xT[0:T, 800:800 + P]
        pad = view(wadj, 0, [CHX // PIECES, ROW])
        crowded = xT[:, 950:951]
        slots_f = xT[:, 960:960 + G]

        sorted_rows = view(annex, 0, [CH, ROW])
        hot_src = place("hot_src", [P, 4, NP], FR, xT_at)
        hot_dst = place("hot_dst", [P, 4, P], FR, pairs_at + 64)
        hot_hi = place("hot_hi", [P, 4, P], FR, pairs_at + 64 + 4 * P)
        hot_lo = place("hot_lo", [P, 4, P], FR, pairs_at + 64 + 8 * P)

        x_hi = place("x_hi", [P, KD * N], FR, arena_at + 2 * G * EC)
        x_lo = place("x_lo", [P, KD * N], FR, arena_at + 2 * G * EC + up(KD * N))
        mat_at = arena_at + 2 * G * EC + 2 * up(KD * N)
        mat_hi = place("mat_hi", [P, KD, D], FR, mat_at)
        mat_lo = place("mat_lo", [P, KD, D], FR, mat_at + KD * D)
        mat = (view(arena, mat_at - arena_at + 2 * KD * D, [KD, D]), view(wadj, 12 * ROW, [KD, D]))
        product = view(annex, EC * ROW, [NT, D], T)

        here = place("here", [P, NT, N], FR, annex_at)
        turned_at = annex_at + up(NT * N)
        turned = place("turned", [P, NT, NT, T2], FR, turned_at)
        h_out_at = turned_at + up(NT * NT * T2)
        h_hi = [place("h_hi_out", [T, NT, D], FR, h_out_at), place("h_hi_in", [T, NT, D], FR, upper_at)]
        h_lo = [place("h_lo_out", [T, NT, D], FR, h_out_at + NT * D),
                place("h_lo_in", [T, NT, D], FR, upper_at + NT * D)]
        h = [view(arena, upper_at - arena_at + (2 + n) * NT * D, [NT, D], T) for n in range(2)]
        h_bias = [view(arena, upper_at - arena_at + 4 * NT * D + n * D, [D], T) for n in range(2)]
        pairs_t = view(pairs, 0, [NT, N], T)
        wadj_t = view(wadj, 0, [NT, N], T)
        sums = view(arena, 0, [NT, D], T)

        u_w = view(arena, 3000, [KD, RANK])
        vt_w = view(arena, 3300, [D], RANK)
        s_row = view(arena, 3900, [RANK], T)
        b1_row = view(arena, 4000, [D], T)
        support = view(arena, 4600, [NT, RANK], T)
        mixed = view(arena, 5000, [N], RANK)
        be_row = view(arena, 6000, [D], T)
        xb = view(arena, 6600, [NT, D], T)
        ln_pairs = view(arena, 20000, [NT * N], T)

        row_buf = view(arena, 9300, [4, ROW])
        x_src = view(arena, 9600, [4, D])
        msg_in = view(arena, 11700, [2, D])
        msg = view(arena, 12800, [2, D])
        attr_t = view(arena, 13900, [2, P], EA)
        zero_w = view(arena, 19620, [T])
        hot_dst2 = view(arena, 14200, [2, P])
        agg = view(arena, 14500, [NT, D], T)
        h_t = view(arena, 17100, [KD * N])
        h_tk = view(arena, 17100, [KD, N])
        z1 = view(arena, 20000, [2 * KD, N])
        z2 = view(arena, 0, [KD, N])
        w1 = view(annex, 0, [KD, 2 * D])
        w2 = view(annex, 2 * KD * D, [2 * KD, D])
        w_e = view(annex, 4 * KD * D, [D], EA)
        small2 = 4 * KD * D + D
        (b1_c, g1_c, beta1_c, b2_c, g2_c, beta2_c, scale_c, shift_c, bn_ve, bn_sd) = [
            view(annex, small2 + 8 * n, [8]) for n in range(10)]
        eps_c = view(annex, small2 + 80, [1], T)
        bn_stat = view(annex, small2 + 96, [2 * KD, 12])
        bn_mv = view(annex, small2 + 192, [2 * KD, 2])

        q_t = [view(arena, n * KD * N, [KD, N]) for n in range(2)]
        k_t = view(arena, 2 * KD * N, [KD, N])
        val_at = 3 * KD * N
        val = view(arena, val_at, [NT, HEADS * P], T)
        probs_at = val_at + NT * HEADS * P
        probs_t = view(arena, probs_at, [2, NT * N], T)
        mixed_t = view(arena, probs_at + 2 * NT * N, [KD, N])
        scores_at = probs_at + 2 * NT * N + KD * N
        scores = view(arena, scores_at, [2, N], T)
        probs = view(arena, scores_at + 2 * N, [2, N], T)
        top = view(arena, scores_at + 4 * N, [4], T)
        minus_top = view(arena, scores_at + 4 * N + 4, [4], T)
        denom = view(arena, scores_at + 4 * N + 8, [NT, HEADS], T)
        inv = view(arena, scores_at + 4 * N + 8 + NT * HEADS, [NT, HEADS], T)
        enc = view(wadj, 0, [NT, D], T)
        rest = view(annex, 10880, [NT, D], T)
        mlp1 = view(annex, 0, [KD, 2 * D])
        mlp2 = view(annex, 2 * KD * D, [2 * KD, D])
        hid = view(arena, 0, [2 * KD, N])
        w_qkvs = [view(annex, n * KD * D, [KD, D]) for n in range(4)]
        bq_c = view(annex, 8200, [KD])
        bk_c = view(annex, 8210, [KD])
        mb1_c = view(annex, 8220, [2 * KD])
        bv_row, bs_row, mb2_row, ln_g, ln_b = [view(annex, 8300 + D * n, [D], T) for n in range(5)]

        edges_in = sem("edges_in")
        attr_in = sem("attr_in")
        pad_ready = sem("pad_ready")
        cleared = sem("cleared")
        x_in = sem("x_in")
        consts = sem("consts")
        rows_ready = sem("rows_ready")
        ranked = sem("ranked")
        prefixed = sem("prefixed")
        slots_ready = sem("slots_ready")
        scattered = sem("scattered")
        sorted_in = sem("sorted_in")
        v_step = sem("v_step")
        a_step = sem("a_step")
        g_step = sem("g_step")
        zeroed = sem("zeroed")
        plan_ready = sem("plan_ready")
        plan_step = sem("plan_step")
        weights_ready = sem("weights_ready")
        hot_made = sem("hot_made")
        hot_scaled = sem("hot_scaled")
        chunk_done = sem("chunk_done")
        counts_out = sem("counts_out")
        weights_out = sem("weights_out")
        tallied = sem("tallied")
        onehots = sem("onehots")
        counted = sem("counted")
        added = sem("added")
        xt_psum = sem("xt_psum")
        xt_ready = sem("xt_ready")
        x_split = sem("x_split")
        mat_in = [sem(f"mat_in{n}") for n in range(2)]
        mat_hi_ready = sem("mat_hi_ready")
        mat_lo_ready = sem("mat_lo_ready")
        mat_used = sem("mat_used")
        product_psum = sem("product_psum")
        product_out = sem("product_out")
        product_stored = sem("product_stored")
        here_rounded = sem("here_rounded")
        here_ready = sem("here_ready")
        here_added = sem("here_added")
        scratch = sem("scratch")
        out_act = sem("out_act")
        out_dve = sem("out_dve")
        h_in = [sem(f"h_in_{side}") for side in ("out", "in")]
        h_biased = [sem(f"h_biased_{side}") for side in ("out", "in")]
        h_hi_ready = [sem(f"h_hi_ready_{side}") for side in ("out", "in")]
        h_split = [sem(f"h_split_{side}") for side in ("out", "in")]
        h_used = [sem(f"h_used_{side}") for side in ("out", "in")]
        acc_done = sem("acc_done")
        var_ready = sem("var_ready")
        sd_ready = sem("sd_ready")
        x_ready = sem("x_ready")

        p1_in = sem("p1_in")
        support_psum = sem("support_psum")
        support_ready = sem("support_ready")
        mixed_psum = sem("mixed_psum")
        mixed_ready = sem("mixed_ready")
        l1_psum = sem("l1_psum")
        clipped = sem("clipped")
        logs_ready = sem("logs_ready")
        p2_in = sem("p2_in")
        xb_ready = sem("xb_ready")
        xb_stored = sem("xb_stored")
        rows_in = [sem(f"rows_in{n}") for n in range(2)]
        src_in = [sem(f"src_in{n}") for n in range(4)]
        pool_tick = sem("pool_tick")
        attr_psum = sem("attr_psum")
        attr_out = sem("attr_out")
        edge_psum = sem("edge_psum")
        msg_sum = sem("msg_sum")
        hot_ready = sem("hot_ready")
        msg_ready = sem("msg_ready")
        agg_psum = sem("agg_psum")
        agg_added = sem("agg_added")
        tile_psum = sem("tile_psum")
        tile_added = sem("tile_added")
        agg_ready = sem("agg_ready")
        h_ready = sem("h_ready")
        z_psum = sem("z_psum")
        z_out = sem("z_out")
        bn_var = sem("bn_var")
        bn_dev = sem("bn_dev")
        bn_ready = sem("bn_ready")
        act_out = sem("act_out")
        back_psum = sem("back_psum")
        l3_x = sem("l3_x")
        l3_in = sem("l3_in")
        l3_rows = sem("l3_rows")
        proj = sem("proj")
        qk_out = sem("qk_out")
        q_odd_out = sem("q_odd_out")
        vs_out = sem("vs_out")
        w_used = sem("w_used")
        score_psum = sem("score_psum")
        top_ready = sem("top_ready")
        score_out = sem("score_out")
        probs_out = sem("probs_out")
        turn_psum = sem("turn_psum")
        turn_out = sem("turn_out")
        mixed_part = sem("mixed_part")
        pair_out = sem("pair_out")
        heads_psum = sem("heads_psum")
        tile_out = sem("tile_out")
        o_step = sem("o_step")
        mlp_in = sem("mlp_in")
        hid_psum = sem("hid_psum")
        hid_out = sem("hid_out")
        mlp_psum = sem("mlp_psum")
        stored = sem("stored")
        tick = sem("tick")

        block = ctx.enter_context(nc.Block())

        def load_rows(sp, to, row, done_sem, n):
            sp.dma_start(to, row.rearrange("(a d) -> a d", a=1).to_broadcast((n, row.shape[0]))).then_inc(done_sem, 16)

        def sync_sort(sp):
            for tile_to, row in ((src_i, src), (dst_i, dst), (typ_i, edge_type), (wgt, edge_weight)):
                sp.dma_start(tile_to, row.rearrange("(p c) -> p c", p=T)).then_inc(edges_in, 16)
            sp.dma_start(xN[0:T, :, :], x.rearrange("(t p) d -> p t d", p=T)).then_inc(x_in, 16)
            sp.dma_start(mat[0], p0["W_self"]).then_inc(mat_in[0], 16)
            sp.dma_start(mat[1], p0["W_rel"][0]).then_inc(mat_in[1], 16)
            sp.dma_start(rows[:, :, 0:EA], edge_attr.rearrange("(p c) e -> p c e", p=T)).then_inc(attr_in, 16)
            sp.wait_ge(mat_lo_ready, KD)
            sp.dma_start(mat[0], p0["W_rel"][1]).then_inc(mat_in[0], 16)
            sp.wait_ge(pad_ready, 1)
            piece = CHX // PIECES * ROW
            for n in range(PIECES):
                sp.dma_start(table_p[:, n * piece:(n + 1) * piece],
                             pad.rearrange("p c e -> p (c e)")).then_inc(cleared, 16)

            def store(i):
                sp.wait_ge(product_out, emptied(i, NT - 1))
                sp.dma_start(products[ds(i, 1)].rearrange("a (t p) d -> p (a t) d", p=T), product).then_inc(product_stored, 16)

            with sp.Fori(0, R - 1) as pair:
                for j in range(2):
                    i = pair * 2 + j
                    sp.wait_ge(mat_lo_ready, (i + 2) * KD)
                    sp.dma_start(mat[1 - j], p0["W_rel"][ds(i + 2, 1)].rearrange("a p k o -> p (a k) o")
                                 ).then_inc(mat_in[1 - j], 16)
                    store(i)
            for i in range(PRODUCTS - 3, PRODUCTS):
                store(i)
            sp.wait_ge(scattered, 16 * EC)
            sp.wait_ge(product_stored, 16 * (PRODUCTS + 1))
            sp.dma_start(annex[:, :], table_p).then_inc(sorted_in, 16)

        def sync_l0(sp):
            def load(side, row, bias):
                sp.dma_start(h[side], row.rearrange("a (t p) d -> p (a t) d", p=T)).then_inc(h_in[side], 16)
                sp.dma_start(h_bias[side], bias.to_broadcast((T, D))).then_inc(h_in[side], 16)

            sp.wait_ge(product_psum, NT * PRODUCTS)
            sp.sem_inc(h_split[0], 1)
            load(1, products[0:1], p0["b_self"].rearrange("(a d) -> a d", a=1))

            def relations(first):
                with sp.Fori(0, R) as r:
                    for side in range(2):
                        sp.wait_ge(h_split[side], first + r + 1)
                        load(side, products[ds(r + 1 + side * R, 1)], p0["b_rel"][ds(r + side * R, 1), :])

            relations(0)
            is_packed = sp.value_load(packed[0:1, 0:1], min_val=0, max_val=1)
            with sp.If(is_packed):
                relations(R)

        def split_rest(eng, unit, i, j):
            for k in range(KD):
                eng.wait_ge(mat_hi_ready, i * KD + k + 1)
                unit.tensor_tensor(mat_lo[:, k, :], mat[j][:, k, :], mat_hi[:, k, :].bitcast(F32),
                                  ALU.subtract).then_inc(mat_lo_ready, 1)

        def pool_sort(pool):
            g = nc.gpsimd
            g.iota(node_f[:, :], pattern=[[1, NP]], base=0, channel_multiplier=0,
                   allow_small_or_imprecise_dtypes=True).then_inc(consts, 1)
            g.iota(group_no, pattern=[[1, G]], base=0, channel_multiplier=0,
                   allow_small_or_imprecise_dtypes=True).then_inc(consts, 1)
            g.iota(chunk_no, pattern=[[1, CH]], base=0, channel_multiplier=0,
                   allow_small_or_imprecise_dtypes=True).then_inc(consts, 1)
            g.memset(ident[:, :], 0.0).then_inc(g_step, 1)
            g.memset(before, 1.0).then_inc(g_step, 1)
            g.memset(ones_m, 1.0).then_inc(consts, 1)
            pool.wait_ge(g_step, 2)
            g.affine_select(out=ident[:, :], in_=ident[:, :], compare_op=ALU.not_equal, fill=1.0, base=0,
                            pattern=[[-1, P]], channel_multiplier=1).then_inc(consts, 1)
            g.affine_select(out=before, in_=before, compare_op=ALU.is_gt, fill=0.0, base=0,
                            pattern=[[1, T]], channel_multiplier=-1).then_inc(consts, 1)
            for i in range(BY_POOL):
                split_rest(pool, g, i, i % 2)
            pool.wait_ge(slots_ready, 1)
            pool.wait_ge(rows_ready, 1)
            pool.wait_ge(attr_in, 16)
            pool.wait_ge(cleared, 16 * PIECES)
            for c in range(EC):
                g.indirect_dma_start(out=table, out_offset=bass.IndirectOffsetOnAxis(ap=pos_i[:, c:c + 1], axis=0),
                                     in_=rows[:, c, :], in_offset=None).then_inc(scattered, 16)

        def transposes(tile):
            for b in range(KD * NT):
                k, t = divmod(b, NT)
                mm = nc.tensor.transpose(PS[:, b // 4, b % 4 * T:(b % 4 + 1) * T], tile[0:T, t, k * P:(k + 1) * P], identT)
                if b % 4 == 3:
                    mm.then_inc(xt_psum, 1)

        def pe_sort(pe):
            pe.wait_ge(consts, 6)
            pe.wait_ge(x_in, 16)
            transposes(xN)
            pe.wait_ge(x_split, 1)
            multiply(pe, 0, 0, first=True)
            pe.wait_ge(ranked, 1)
            nc.tensor.matmul(PS[0:T, 7, 0:G], before, cnt[0:T, :], start=True, stop=True)
            nc.tensor.matmul(PS[:, 7, G:2 * G], ones_m, cnt[0:T, :], start=True, stop=True).then_inc(prefixed, 1)
            with pe.Fori(0, R) as pair:
                for j in range(2):
                    multiply(pe, pair * 2 + 1 + j, 1 - j)
            pe.wait_ge(product_out, emptied(PRODUCTS - 1, NT - 1))

        def bank_of(j, t):
            return 2 * j + t if t < 2 else t + 2

        def emptied(i, t):
            return i * NT + t + 1 + NT

        def multiply(pe, i, j, first=False):
            for k in range(KD):
                pe.wait_ge(mat_lo_ready, i * KD + k + 1)
                for t in range(NT):
                    if k == 0:
                        if not first:
                            pe.wait_ge(product_out, emptied(i - 2 if t < 2 else i - 1, t))
                    at = k * N + t * T
                    for n, (a, b) in enumerate(((x_hi, mat_hi), (x_hi, mat_lo), (x_lo, mat_hi))):
                        mm = nc.tensor.matmul(PS[0:T, bank_of(j, t), :], a[:, at:at + T], b[:, k, :],
                                              start=(k == 0 and n == 0), stop=(k == KD - 1 and n == 2))
                    if k == KD - 1:
                        mm.then_inc(product_psum, 1)
                    elif t == NT - 1:
                        mm.then_inc(mat_used, 1)
        def pe_count(pe):
            mm = nc.tensor.matmul
            pe.sem_inc(chunk_done, CREDIT)
            with pe.Fori(0, NT) as t:
                for r in range(R):
                    bank = r % 2 * 2
                    pe.wait_ge(counts_out, t * R + r + 1)
                    for i in range(GC):
                        c = r * GC + i
                        pe.wait_ge(hot_made, t * TC + c + 1)
                        for at, n in HALVES_P:
                            mm(PS[0:T, bank + at // 512, 0:n], hot_dst[:, c % 4, 0:T], hot_src[:, c % 4, at:at + n],
                               start=(i == 0), stop=(i == GC - 1))
                        pe.wait_ge(hot_scaled, t * TC + c + 1)
                        if c == 0:
                            pe.wait_ge(weights_out, t + 1)
                        for part in (hot_hi, hot_lo):
                            for at, n in HALVES_P:
                                ins = mm(PS[0:T, 4 + at // 512, 0:n], part[:, c % 4, 0:T], hot_src[:, c % 4, at:at + n],
                                         start=(c == 0 and part is hot_hi), stop=(c == TC - 1 and part is hot_lo))
                        ins.then_inc(chunk_done, 1)

        def pe_count_packed(pe):
            mm = nc.tensor.matmul
            pe.sem_inc(counted, CREDIT)
            with pe.Fori(0, CH // 2) as step:
                for j in range(2):
                    c = step * 2 + j
                    pe.wait_ge(onehots, done(c))
                    pe.wait_ge(added, done(c - 2))
                    for at, n in HALVES_P:
                        mm(PS[0:T, 2 * j + at // 512, 0:n], hot_dst[:, j, 0:T], hot_src[:, j, at:at + n],
                           start=True, stop=True)
                    for part in (hot_hi, hot_lo):
                        for at, n in HALVES_P:
                            ins = mm(PS[0:T, 4 + 2 * j + at // 512, 0:n], part[:, j, 0:T], hot_src[:, j, at:at + n],
                                     start=(part is hot_hi), stop=(part is hot_lo))
                    ins.then_inc(counted, 1)

        def pe_l0(pe):
            t_ = nc.tensor
            pe.wait_ge(tallied, 1)
            pe.wait_ge(h_split[1], 1)
            for t in range(NT):
                for part in (h_hi[1], h_lo[1]):
                    mm = t_.matmul(PS[0:T, t, :], ident_r[0:T, 0:T], part[:, t, :],
                                   start=(part is h_hi[1]), stop=False, skip_group_check=True)
            mm.then_inc(h_used[1], 1)

            def relations(first):
                with pe.Fori(0, R) as r:
                    q = first + r
                    pe.wait_ge(here_ready, q + 1)
                    block_ = 0
                    for u, n in enumerate(TURNS):
                        if u >= 3:
                            if u % 2:
                                pe.wait_ge(out_act, q * 4 + (u - 3) // 2 + 1)
                            else:
                                pe.wait_ge(out_dve, q * 3 + (u - 3) // 2 + 1)
                        for i in range(n):
                            st, t = divmod(block_, NT)
                            block_ += 1
                            mm = t_.transpose(PS[0:T, 5 + u % 3, i * T2:(i + 1) * T2].bitcast(FR),
                                              here[0:T2, t, st * T:(st + 1) * T], ident_r[0:T2, 0:T2])
                        mm.then_inc(scratch, 1)
                    for side in range(2):
                        pe.wait_ge(h_split[side], q + 2)
                        if side == 1:
                            pe.wait_ge(out_act, q * 4 + 4)
                            pe.wait_ge(out_dve, q * 3 + 3)
                        for k in range(NT):
                            for t in range(NT):
                                edges = here[0:T, k, t * T:(t + 1) * T] if side == 0 else turned[0:T, k, t, 0:T]
                                for part in (h_hi[side], h_lo[side]):
                                    mm = t_.matmul(PS[0:T, t, :], edges, part[:, k, :], start=False,
                                                   stop=(k == NT - 1 and part is h_lo[side]), skip_group_check=True)
                        mm.then_inc(h_used[side], 1)
                pe.wait_ge(h_used[1], first + R + 1)

            relations(0)
            is_packed = pe.value_load(packed[0:1, 0:1], min_val=0, max_val=1)
            with pe.If(is_packed):
                relations(R)
            pe.sem_inc(acc_done, 1)

        def act_turn(act, turn, to):
            for b in range(NT):
                act.wait_ge(xt_psum, NT * turn + b + 1)
                nc.scalar.copy(to[:, b * 4 * T:(b + 1) * 4 * T], PS[:, b, 0:4 * T]).then_inc(xt_ready, 1)

        def act_deviation(act, turn):
            act.wait_ge(var_ready, turn + 1)
            nc.scalar.activation(sd[0:T, :], rstd[0:T, :], ACT.Sqrt).then_inc(sd_ready, 1)

        def act_products(act):
            for b in range(NT):
                act.wait_ge(xt_psum, b + 1)
                nc.scalar.copy(x_hi[:, b * 4 * T:(b + 1) * 4 * T], PS[:, b, 0:4 * T]).then_inc(xt_ready, 1)

            def out_(i, j):
                for t in range(NT):
                    act.wait_ge(product_psum, i * NT + t + 1)
                    if t == 0:
                        act.wait_ge(product_stored, i * 16 + 16)
                    nc.scalar.copy(product[:, t, :], PS[0:T, bank_of(j, t), :]).then_inc(product_out, 1)

            def parts(i, j, ks):
                for k in ks:
                    if k == 0:
                        act.wait_ge(mat_in[j], (i - j) * 8 + 16)
                    if k < KD - 1:
                        act.wait_ge(mat_used, (i - 1) * (KD - 1) + k + 1)
                    else:
                        act.wait_ge(product_psum, i * NT)
                    nc.scalar.copy(mat_hi[:, k, :], mat[j][:, k, :]).then_inc(mat_hi_ready, 1)

            act.sem_inc(product_out, NT)
            act.sem_inc(product_stored, 16)
            act.wait_ge(mat_in[0], 16)
            for k in range(KD):
                nc.scalar.copy(mat_hi[:, k, :], mat[0][:, k, :]).then_inc(mat_hi_ready, 1)
            with act.Fori(0, R) as pair:
                for j in range(2):
                    i = pair * 2 + j
                    parts(i + 1, 1 - j, (0, 1, 2))
                    out_(i, j)
                    parts(i + 1, 1 - j, (3,))
            out_(PRODUCTS - 1, 0)

        def act_count(act):
            act.wait_ge(weights_ready, 1)
            act.sem_inc(counts_out, 2)
            w_hi_f = w_hi[:, :].bitcast(F32)
            with act.Fori(0, NT) as t:
                def counts_to_sbuf(r):
                    act.wait_ge(chunk_done, done(t * TC + (r + 1) * GC - 1))
                    nc.scalar.copy(counts[0:T, ds((t * R + r) * N, N)], two_banks(r % 2 * 2, T)).then_inc(counts_out, 1)

                for i in range(TC):
                    c = t * TC + i
                    act.wait_ge(hot_made, c + 1)
                    act.wait_ge(chunk_done, done(c - 4))
                    for part, w in ((hot_hi, w_hi_f), (hot_lo, w_lo)):
                        ins = nc.scalar.activation(part[:, i % 4, 0:T], hot_dst[:, i % 4, 0:T].bitcast(F32), ACT.Copy,
                                                   scale=w[:, ds(c, 1)])
                    ins.then_inc(hot_scaled, 1)
                    if i % GC == 2 and i > GC:
                        counts_to_sbuf(i // GC - 1)
                counts_to_sbuf(R - 1)

        def act_l0(act):
            def rounded(side, q):
                act.wait_ge(h_biased[side], q + 1)
                if side == 0:
                    act.wait_ge(h_used[0], q + 1)
                nc.scalar.copy(h_hi[side][:, :, :], h[side]).then_inc(h_hi_ready[side], 1)

            def stage(q, r, rest):
                act.wait_ge(h_used[0], q + 1)
                act.wait_ge(here_added, q + 1)
                by_rel = counts[0:T, :].rearrange("p (t r n) -> p t r n", t=NT, r=R)
                nc.scalar.copy(here[0:T, :, :], by_rel[:, :, ds(r, 1), :].rearrange("p t a n -> p t (a n)")
                               ).then_inc(here_rounded if rest else here_ready, 1)

            def turn(q, r, rest, more):
                for u in range(0, 7, 2):
                    act.wait_ge(scratch, q * 7 + u + 1)
                    if u == 0:
                        act.wait_ge(h_used[1], q + 1)
                    nc.scalar.copy(turned_blocks(u), PS[0:T, 5 + u % 3, 0:TURNS[u] * T2]).then_inc(out_act, 1)
                rounded(1, q + 1)
                if more:
                    stage(q + 1, r + 1, rest)
                    rounded(0, q + 1)

            def relations(first, rest):
                stage(first, 0, rest)
                rounded(0, first)
                with act.Fori(0, R - 1) as r:
                    turn(first + r, r, rest, True)
                turn(first + R - 1, R - 1, rest, False)

            act.wait_ge(tallied, 1)
            act.sem_inc(h_used[0], 1)
            rounded(1, 0)
            relations(0, False)
            is_packed = act.value_load(packed[0:1, 0:1], min_val=0, max_val=1)
            with act.If(is_packed):
                relations(R, True)
            act_deviation(act, 0)

        def turned_blocks(u):
            at = sum(TURNS[:u])
            return turned[0:T, :, :, :].rearrange("p s t n -> p (s t n)")[:, at * T2:(at + TURNS[u]) * T2]

        v_steps = [0]

        def link(dve, ins):
            v_steps[0] += 1
            ins.then_inc(v_step, 1)
            dve.wait_ge(v_step, v_steps[0])

        def dve_sort(dve):
            v = nc.vector

            def step(ins):
                link(dve, ins)

            v.memset(pad, 0.0).then_inc(v_step, 1)
            v_steps[0] += 1
            dve.wait_ge(v_step, v_steps[0])
            v.memset(pad[:, :, DSTL:DSTL + 1], -1.0).then_inc(pad_ready, 1)
            v.memset(rank, 1.0)
            v.memset(ones_g, 1.0)
            step(v.memset(keep[:, :, :], 1.0))
            step(v.memset(keep[:, :, 0:1], 0.0))
            dve.wait_ge(edges_in, 64)
            v.tensor_copy(src_f, src_i)
            v.tensor_copy(dst_f, dst_i)
            step(v.tensor_copy(typ_f, typ_i))
            step(v.tensor_scalar(tile, dst_f, float(T), None, ALU.is_ge))
            for t in range(2, NT):
                step(v.scalar_tensor_tensor(out=tile, in0=dst_f, scalar=float(t * T), in1=tile, op0=ALU.is_ge, op1=ALU.add))
            step(v.scalar_tensor_tensor(out=key, in0=tile, scalar=float(R), in1=typ_f, op0=ALU.mult, op1=ALU.add))
            step(v.scalar_tensor_tensor(out=dst_l, in0=tile, scalar=-float(T), in1=dst_f, op0=ALU.mult, op1=ALU.add))
            dve.wait_ge(consts, 6)
            step(v.tensor_tensor(hot[:, :, :], key.unsqueeze(1).broadcast_to([T, G, EC]),
                                 group_no[0:T, :].unsqueeze(2).broadcast_to([T, G, EC]), ALU.is_equal))
            dve.wait_ge(xt_ready, NT)
            for b in range(NT):
                at = slice(b * 4 * T, (b + 1) * 4 * T)
                ins = v.tensor_tensor(x_lo[:, at], PS[:, b, 0:4 * T], x_hi[:, at].bitcast(F32), ALU.subtract)
            ins.then_inc(x_split, 1)
            step(v.tensor_tensor_scan(rank.rearrange("p g c -> p (g c)"), keep[:, :, :].rearrange("p g c -> p (g c)"),
                                      hot[:, :, :].rearrange("p g c -> p (g c)"), 0.0, ALU.mult, ALU.add))
            v.tensor_copy(cnt[0:T, :], rank[:, :, EC - 1:EC].rearrange("p g a -> p (g a)")).then_inc(ranked, 1)
            for col, what in ((SRC, src_f), (DSTL, dst_l), (WGT, wgt)):
                v.tensor_copy(rows[:, :, col:col + 1], what.unsqueeze(2))
            v.tensor_copy(rows[:, :, SRCI:SRCI + 1].bitcast(I32), src_i.unsqueeze(2)).then_inc(rows_ready, 1)
            dve.wait_ge(prefixed, 1)
            step(v.tensor_scalar(chunks_f, PS[:, 7, G:2 * G], float(P - 1), None, ALU.add))
            step(v.tensor_copy(chunks_i, chunks_f))
            step(v.tensor_scalar(chunks_i, chunks_i, 7, None, ALU.arith_shift_right))
            step(v.tensor_copy(chunks_f, chunks_i))
            step(v.tensor_tensor_scan(upto, ones_g, chunks_f, 0.0, ALU.mult, ALU.add))
            step(v.tensor_tensor(start, upto, chunks_f, ALU.subtract))
            step(v.tensor_reduce(crowded, PS[:, 7, G:2 * G], X, ALU.max))
            step(v.tensor_scalar(crowded, crowded, float(GC * P), None, ALU.is_gt))
            v.tensor_copy(packed[:, :], crowded[0:1, :])
            v.tensor_scalar(slots_f, group_no, float(GC * P), None, ALU.mult)
            step(v.tensor_scalar(start, start, float(P), None, ALU.mult))
            step(v.tensor_tensor(start, start, slots_f, ALU.subtract))
            step(v.scalar_tensor_tensor(out=start, in0=start, scalar=crowded, in1=slots_f, op0=ALU.mult, op1=ALU.add))
            step(v.tensor_tensor(base[0:T, :], start[0:T, :], PS[0:T, 7, 0:G], ALU.add))
            step(v.tensor_scalar(base[0:T, :], base[0:T, :], -1.0, None, ALU.add))
            step(v.tensor_tensor(rank, rank, base[0:T, :].unsqueeze(2).broadcast_to([T, G, EC]), ALU.add))
            step(v.tensor_tensor(rank, rank, hot[:, :, :], ALU.mult))
            step(v.tensor_reduce(slot_f, rank.rearrange("p g c -> p c g"), X, ALU.add))
            step(v.tensor_copy(slot_i, slot_f))
            v.tensor_scalar(lo_i, slot_i, P - 1, None, ALU.bitwise_and)
            step(v.tensor_scalar(hi_i, slot_i, 7, None, ALU.arith_shift_right))
            v.tensor_copy(hi_f, hi_i)
            step(v.tensor_copy(lo_f, lo_i))
            step(v.scalar_tensor_tensor(out=slot_f, in0=lo_f, scalar=float(CHX), in1=hi_f, op0=ALU.mult, op1=ALU.add))
            v.tensor_copy(pos_i, slot_f).then_inc(slots_ready, 1)
            dve.sem_inc(plan_ready, 1)
            dve.wait_ge(product_psum, NT * (BY_POOL - 1) + 1)
            with dve.Fori(0, (PRODUCTS - BY_POOL) // 2) as pair:
                for j in range(2):
                    split_rest(dve, v, pair * 2 + BY_POOL + j, (BY_POOL + j) % 2)

        def dve_count_start(dve):
            v = nc.vector
            dve.wait_ge(cleared, 16 * PIECES)
            v.memset(wadj[0:T, :], 0.0)
            v.tensor_copy(ident_r[:, :], ident[:, :])
            dve.wait_ge(sorted_in, 16)
            weight = sorted_rows[:, 0:CH, WGT:WGT + 1].rearrange("p c a -> p (c a)")
            link(dve, v.tensor_copy(w_hi[:, :], weight))
            link(dve, v.tensor_tensor(w_lo[:, :], weight, w_hi[:, :].bitcast(F32), ALU.subtract))
            dve.sem_inc(weights_ready, 1)

        def column(c, n):
            return sorted_rows[:, ds(c, 1), n:n + 1].rearrange("p a b -> p (a b)")

        def dve_count(dve):
            v = nc.vector
            dve.sem_inc(weights_out, 1)
            with dve.Fori(0, NT) as t:
                for i in range(TC):
                    c = t * TC + i
                    dve.wait_ge(chunk_done, done(c - 4))
                    v.tensor_scalar(hot_dst[:, i % 4, 0:T], node_f[:, 0:T], column(c, DSTL), None, ALU.is_equal)
                    v.tensor_scalar(hot_src[:, i % 4, :], node_f[:, :], column(c, SRC), None, ALU.is_equal).then_inc(hot_made, 1)
                dve.wait_ge(chunk_done, done(t * TC + TC - 1))
                v.tensor_copy(wadj[0:T, ds(t * N, N)], two_banks(4, T)).then_inc(weights_out, 1)
            dve.wait_ge(weights_out, 1 + NT)
            dve.wait_ge(counts_out, 2 + G)

        def dve_count_packed(dve):
            v = nc.vector
            plan = [0]

            def step(ins):
                plan[0] += 1
                ins.then_inc(plan_step, 1)
                dve.wait_ge(plan_step, plan[0])

            step(v.tensor_tensor(past, upto[0:1, :].unsqueeze(1).broadcast_to([1, CH, G]),
                                 chunk_no.unsqueeze(2).broadcast_to([1, CH, G]), ALU.is_le))
            step(v.tensor_reduce(group_f, past, X, ALU.add))
            step(v.tensor_scalar(group_f, group_f, float(G - 1), None, ALU.min))
            step(v.tensor_copy(group[:, :], group_f))
            step(v.tensor_scalar(tile_of[:, :], group[:, :], 3, None, ALU.arith_shift_right))
            step(v.memset(counts[0:T, :], 0))
            dve.sem_inc(onehots, CREDIT)
            dve.sem_inc(added, CREDIT)

            def one_hots(c, j):
                v.tensor_scalar(hot_dst[:, j, 0:T], node_f[:, 0:T], column(c, DSTL), None, ALU.is_equal)
                v.tensor_scalar(hot_src[:, j, :], node_f[:, :], column(c, SRC), None, ALU.is_equal)
                for part, w in ((hot_hi, w_hi[:, :].bitcast(F32)), (hot_lo, w_lo)):
                    ins = v.tensor_scalar(part[:, j, 0:T], node_f[:, 0:T], column(c, DSTL), w[:, ds(c, 1)],
                                          ALU.is_equal, ALU.mult)
                ins.then_inc(onehots, 1)

            def add(c, j):
                g = dve.value_load(group[0:1, ds(c, 1)], min_val=0, max_val=G - 1)
                t = dve.value_load(tile_of[0:1, ds(c, 1)], min_val=0, max_val=NT - 1)
                dve.wait_ge(counted, done(c))
                dve.wait_ge(added, done(c - 1))
                to = counts[0:T, ds(g * N, N)]
                v.tensor_tensor(to, two_banks(2 * j, T), to, ALU.add)
                to = wadj[0:T, ds(t * N, N)]
                v.tensor_tensor(to, two_banks(4 + 2 * j, T), to, ALU.add).then_inc(added, 1)

            one_hots(0, 0)
            with dve.Fori(0, CH // 2 - 1) as s_:
                for j in range(2):
                    one_hots(s_ * 2 + j + 1, 1 - j)
                    add(s_ * 2 + j, j)
            one_hots(CH - 1, 1)
            add(CH - 2, 0)
            add(CH - 1, 1)
            dve.wait_ge(added, done(CH - 1))

        def dve_norm(dve, turn, scale_row=None, shift_row=None):
            v = nc.vector
            for t in range(NT):
                ins = v.bn_stats(stat[0:T, t, :], xN[0:T, t, :])
            link(dve, ins)
            for t in range(NT):
                ins = v.bn_aggr(mv[0:T, t, :], stat[0:T, t, :])
            link(dve, ins)
            v.tensor_scalar(rstd[0:T, :], mv[0:T, :, 1:2].rearrange("p t a -> p (t a)"), EPS, None,
                            ALU.add).then_inc(var_ready, 1)
            dve.wait_ge(sd_ready, turn + 1)
            link(dve, v.reciprocal(rstd[0:T, :], sd[0:T, :]))
            for t in range(NT):
                ins = v.tensor_scalar(xN[0:T, t, :], xN[0:T, t, :], mv[0:T, t, 0:1], rstd[0:T, t:t + 1],
                                      ALU.subtract, ALU.mult)
            if scale_row is not None:
                link(dve, ins)
                link(dve, v.tensor_tensor(xN[0:T, :, :], xN[0:T, :, :], over_tiles(scale_row), ALU.mult))
                ins = v.tensor_tensor(xN[0:T, :, :], xN[0:T, :, :], over_tiles(shift_row), ALU.add)
            ins.then_inc(x_ready, 1)
            dve.wait_ge(x_ready, turn + 1)

        def over_tiles(row):
            return row[0:T, :].unsqueeze(1).broadcast_to([T, NT, D])

        def dve_relu_and_add(dve, bias):
            v = nc.vector
            for t in range(NT):
                ins = v.tensor_tensor(sums[:, t, :], PS[0:T, t, :], bias[0:T, :], ALU.add)
            link(dve, ins)
            for t in range(NT):
                ins = v.scalar_tensor_tensor(out=xN[0:T, t, :], in0=sums[:, t, :], scalar=0.0, in1=xN[0:T, t, :],
                                             op0=ALU.max, op1=ALU.add)
            link(dve, ins)

        def dve_l0(dve):
            v = nc.vector
            step = [0]

            def split(side, q):
                dve.wait_ge(h_in[side], q * 32 + 32)
                v.tensor_tensor(h[side], h[side], over_tiles(h_bias[side]), ALU.add).then_inc(h_biased[side], 1)
                dve.wait_ge(h_hi_ready[side], q + 1)
                v.tensor_tensor(h_lo[side][:, :, :], h[side], h_hi[side][:, :, :].bitcast(F32),
                                ALU.subtract).then_inc(h_split[side], 1)

            def add_here(q, r, rest):
                if rest:
                    dve.wait_ge(here_rounded, r + 1)
                    by_rel = counts[0:T, :].rearrange("p (t r n) -> p t r n", t=NT, r=R)
                    v.tensor_tensor(here[0:T, :, :], by_rel[:, :, ds(r, 1), :].rearrange("p t a n -> p t (a n)"),
                                    here[0:T, :, :].bitcast(F32), ALU.subtract).then_inc(here_ready, 1)
                dve.wait_ge(here_ready, q + 1)
                v.tensor_tensor(pairs_t, pairs_t, here[0:T, :, :].bitcast(F32), ALU.add).then_inc(here_added, 1)

            def turn(q, r, rest, more):
                for u in range(1, 7, 2):
                    dve.wait_ge(scratch, q * 7 + u + 1)
                    if u == 1:
                        dve.wait_ge(h_used[1], q + 1)
                    v.tensor_copy(turned_blocks(u), PS[0:T, 5 + u % 3, 0:TURNS[u] * T2]).then_inc(out_dve, 1)
                split(1, q + 1)
                if more:
                    add_here(q + 1, r + 1, rest)
                    split(0, q + 1)

            def relations(first, rest):
                add_here(first, 0, rest)
                split(0, first)
                with dve.Fori(0, R - 1) as r:
                    turn(first + r, r, rest, True)
                turn(first + R - 1, R - 1, rest, False)

            link(dve, v.memset(here[:, :, :].bitcast(F32), 0.0))
            link(dve, v.memset(pairs[0:T, :], 0.0))
            dve.sem_inc(here_added, 1)
            split(1, 0)
            relations(0, False)
            is_packed = dve.value_load(packed[0:1, 0:1], min_val=0, max_val=1)
            with dve.If(is_packed):
                relations(R, True)
            dve.wait_ge(acc_done, 1)
            for t in range(NT):
                ins = v.scalar_tensor_tensor(out=xN[0:T, t, :], in0=PS[0:T, t, :], scalar=0.0, in1=xN[0:T, t, :],
                                             op0=ALU.max, op1=ALU.add)
            link(dve, ins)
            dve_norm(dve, 0)

        def sync_l1(sp):
            sp.wait_ge(acc_done, 1)
            sp.dma_start(u_w, p1["U"]).then_inc(p1_in, 16)
            sp.dma_start(vt_w, p1["Vt"]).then_inc(p1_in, 16)
            load_rows(sp, s_row, p1["s"], p1_in, T)
            load_rows(sp, b1_row, p1["bias"], p1_in, T)
            load_rows(sp, be_row, p2["b_e"], p1_in, T)

        def pe_l1(pe):
            t_ = nc.tensor
            pe.wait_ge(x_ready, 1)
            transposes(xN)
            pe.wait_ge(xt_ready, 2 * NT)
            pe.wait_ge(p1_in, 16 * 5)
            for t in range(NT):
                for k in range(KD):
                    mm = t_.matmul(PS[0:T, 5, t * RANK:(t + 1) * RANK], xTk[:, k, t * T:(t + 1) * T], u_w[:, k, :],
                                   start=(k == 0), stop=(k == KD - 1))
            mm.then_inc(support_psum, 1)
            pe.wait_ge(support_ready, 1)
            for h, (at, n) in enumerate(HALVES):
                for t in range(NT):
                    mm = t_.matmul(PS[0:RANK, 6 + h, 0:n], support[:, t, :], wadj_t[:, t, at:at + n],
                                   start=(t == 0), stop=(t == NT - 1))
            mm.then_inc(mixed_psum, 1)
            pe.wait_ge(mixed_ready, 1)
            for t in range(NT):
                mm = t_.matmul(PS[0:T, t, :], mixed[:, t * T:(t + 1) * T], vt_w, start=True, stop=True)
            mm.then_inc(l1_psum, 1)

        def act_l1(act):
            act.wait_ge(clipped, 1)
            nc.scalar.activation(ln_pairs, ln_pairs, ACT.Ln).then_inc(logs_ready, 1)
            act_turn(act, 1, xT)
            act.wait_ge(mixed_psum, 1)
            for h, (at, n) in enumerate(HALVES):
                ins = nc.scalar.copy(mixed[:, at:at + n], PS[0:RANK, 6 + h, 0:n])
            ins.then_inc(mixed_ready, 1)
            act_deviation(act, 1)

        def dve_l1(dve):
            v = nc.vector
            link(dve, v.tensor_reduce(has_in[0:T, :], pairs_t, X, ALU.max))
            v.tensor_scalar(has_in[0:T, :], has_in[0:T, :], 1.0, None, ALU.min)
            link(dve, v.tensor_scalar(ln_pairs, pairs[0:T, :], 1.0, None, ALU.max))
            v.tensor_scalar(pairs[0:T, :], pairs[0:T, :], 0.0, FAR, ALU.is_equal, ALU.mult).then_inc(clipped, 1)
            dve.wait_ge(p1_in, 16 * 5)
            dve.wait_ge(support_psum, 1)
            v.tensor_tensor(support, PS[0:T, 5, 0:NT * RANK].rearrange("p (t n) -> p t n", n=RANK),
                            s_row.unsqueeze(1).broadcast_to([T, NT, RANK]), ALU.mult).then_inc(support_ready, 1)
            dve.wait_ge(logs_ready, 1)
            dve.wait_ge(clipped, 1)
            v.scalar_tensor_tensor(out=pairs[0:T, :], in0=ln_pairs, scalar=float(HD) ** 0.5, in1=pairs[0:T, :],
                                   op0=ALU.mult, op1=ALU.add)
            dve.wait_ge(l1_psum, 1)
            dve_relu_and_add(dve, b1_row)
            dve_norm(dve, 1)
            v.tensor_tensor(xb, xN[0:T, :, :], over_tiles(be_row), ALU.add).then_inc(xb_ready, 1)

        def sync_l2(sp):
            for to, what in ((w1, "W1"), (w2, "W2"), (w_e, "W_e"), (b1_c, "b1"), (g1_c, "g1"), (beta1_c, "beta1"),
                             (b2_c[:, 0:KD], "b2"), (g2_c[:, 0:KD], "g2"), (beta2_c[:, 0:KD], "beta2")):
                sp.dma_start(to, p2[what]).then_inc(p2_in, 16)
            load_rows(sp, eps_c, p2["eps"], p2_in, T)
            sp.wait_ge(xb_ready, 1)
            sp.dma_start(xb_rows.rearrange("(t p) d -> p t d", p=T), xb).then_inc(xb_stored, 16)
            with sp.Fori(0, CHX // 4) as step:
                c0 = step * 4
                for pair in range(2):
                    c = c0 + 2 * pair
                    sp.wait_ge(attr_psum, done(c - 3))
                    sp.wait_ge(hot_ready, done(c - 3))
                    sp.wait_ge(msg_sum, done(c - 3))
                    sp.dma_start(row_buf[:, 2 * pair:2 * pair + 2, :].rearrange("p c e -> p (c e)"),
                                 table_p[:, ds(c * ROW, 2 * ROW)]).then_inc(rows_in[pair], 16)

        def rows_there(eng, c, j):
            eng.wait_ge(rows_in[j // 2], (c - j) * 4 + 16)

        def pool_l2(pool):
            g = nc.gpsimd
            pool.wait_ge(xb_stored, 16)
            with pool.Fori(0, CHX // 4) as step:
                c0 = step * 4
                for j in range(4):
                    c = c0 + j
                    rows_there(pool, c, j)
                    pool.wait_ge(msg_sum, done(c - 4))
                    pool.sem_inc(pool_tick, 1)
                    g.indirect_dma_start(out=x_src[:, j, :], out_offset=None, in_=xb_rows,
                                         in_offset=bass.IndirectOffsetOnAxis(
                                             ap=row_buf[:, j, SRCI:SRCI + 1].bitcast(I32), axis=0)
                                         ).then_inc(src_in[j], 16)

        def pe_l2(pe):
            t_ = nc.tensor
            pe.sem_inc(attr_psum, CREDIT)
            pe.sem_inc(edge_psum, CREDIT)
            pe.sem_inc(agg_psum, CREDIT)
            pe.wait_ge(p2_in, 16 * 10)
            pe.wait_ge(x_ready, 2)

            def turn_attr(c, j):
                rows_there(pe, c, j)
                pe.wait_ge(attr_out, done(c - 2))
                t_.transpose(PS[0:ROW, j % 2, 0:P], row_buf[:, j, :], ident[:, :]).then_inc(attr_psum, 1)

            def edge_product(c, j):
                pe.wait_ge(attr_out, done(c))
                pe.wait_ge(msg_sum, done(c - 2))
                t_.matmul(PS[:, 2 + j % 2, :], attr_t[:, j % 2, :], w_e, start=True, stop=True).then_inc(edge_psum, 1)

            def sum_by_dst(c, j):
                pe.wait_ge(msg_ready, done(c))
                pe.wait_ge(hot_ready, done(c))
                pe.wait_ge(agg_added, done(c - 2))
                t_.matmul(PS[0:T, 4 + j % 2, :], hot_dst2[:, j % 2, 0:T], msg[:, j % 2, :],
                          start=True, stop=True).then_inc(agg_psum, 1)

            def zero_bank(first):
                return t_.matmul(PS[0:T, 4, :], zero_w, node_f[:, 0:D], start=first, stop=not first, skip_group_check=True)

            turn_attr(0, 0)
            turn_attr(1, 1)
            edge_product(0, 0)
            def steps(n, first, sum_):
                with pe.Fori(0, n) as step:
                    c0 = first + step * 4
                    for j in range(4):
                        turn_attr(c0 + j + 2, (j + 2) % 4)
                        edge_product(c0 + j + 1, (j + 1) % 4)
                        sum_(c0 + j, j)

            def sum_in_tile(c, j):
                pe.wait_ge(msg_ready, done(c))
                pe.wait_ge(hot_ready, done(c))
                t_.matmul(PS[0:T, 4, :], hot_dst2[:, j % 2, 0:T], msg[:, j % 2, :],
                          start=False, stop=False, skip_group_check=True).then_inc(agg_psum, 1)

            is_packed = pe.value_load(packed[0:1, 0:1], min_val=0, max_val=1)
            with pe.If(is_packed):
                steps(CH // 4, 0, sum_by_dst)
            with pe.Else():
                with pe.Fori(0, NT) as t:
                    pe.wait_ge(tile_added, t + 1)
                    zero_bank(True)
                    steps(TC // 4, t * TC, sum_in_tile)
                    zero_bank(False).then_inc(tile_psum, 1)

            pe.wait_ge(attr_out, done(CH + 1))
            pe.wait_ge(h_ready, 1)
            transposes(agg)
            pe.wait_ge(xt_ready, 3 * NT)
            use = 0
            for m in range(2 * KD):
                for at, n in HALVES:
                    if use >= 8:
                        pe.wait_ge(z_out, use - 7)
                    for k in range(KD):
                        mm = t_.matmul(PS[:, use % 8, 0:n], w1[:, k, m * P:(m + 1) * P], h_tk[:, k, at:at + n],
                                       start=(k == 0), stop=(k == KD - 1))
                    mm.then_inc(z_psum, 1)
                    use += 1
            for m in range(KD):
                for at, n in HALVES:
                    pe.wait_ge(z_out, use - 7)
                    for k in range(2 * KD):
                        if m == 0 and at == 0:
                            pe.wait_ge(act_out, k + 1)
                        mm = t_.matmul(PS[:, use % 8, 0:n], w2[:, k, m * P:(m + 1) * P], z1[:, k, at:at + n],
                                       start=(k == 0), stop=(k == 2 * KD - 1))
                    mm.then_inc(z_psum, 1)
                    use += 1
            pe.wait_ge(z_out, use)
            pe.wait_ge(act_out, 3 * KD)
            for t in range(NT):
                for k in range(KD):
                    mm = t_.transpose(PS[0:T, t, k * P:(k + 1) * P], z2[:, k, t * T:(t + 1) * T], ident[:, :])
            mm.then_inc(back_psum, 1)

        def act_l2(act):
            act.sem_inc(attr_out, CREDIT)
            act.sem_inc(msg_ready, CREDIT)

            def keep_attr(c, j):
                act.wait_ge(attr_psum, done(c))
                act.wait_ge(edge_psum, done(c - 2))
                nc.scalar.copy(attr_t[:, j % 2, :], PS[0:EA, j % 2, 0:P]).then_inc(attr_out, 1)

            def relu(c, j):
                act.wait_ge(msg_sum, done(c))
                act.wait_ge(agg_psum, done(c - 2))
                nc.scalar.activation(msg[:, j % 2, :], msg_in[:, j % 2, :], ACT.Relu).then_inc(msg_ready, 1)

            keep_attr(0, 0)
            keep_attr(1, 1)
            relu(0, 0)
            with act.Fori(0, CH // 4) as step:
                c0 = step * 4
                for j in range(4):
                    keep_attr(c0 + j + 2, (j + 2) % 4)
                    relu(c0 + j + 1, (j + 1) % 4)
            act_turn(act, 2, h_t)

            use = 0
            tiles = 0
            for phase, (z, bias, parts) in enumerate(((z1, b1_c, 2 * KD), (z2, b2_c, KD))):
                for m in range(parts):
                    for at, n in HALVES:
                        act.wait_ge(z_psum, use + 1)
                        nc.scalar.activation(z[:, m, at:at + n], PS[:, use % 8, 0:n], ACT.Identity,
                                             bias=bias[:, m:m + 1]).then_inc(z_out, 1)
                        use += 1
                act.wait_ge(bn_var, phase + 1)
                nc.scalar.activation(bn_sd[:, 0:parts], bn_ve[:, 0:parts], ACT.Sqrt).then_inc(bn_dev, 1)
                act.wait_ge(bn_ready, phase + 1)
                for m in range(parts):
                    nc.scalar.activation(z[:, m, :], z[:, m, :], ACT.Silu, bias=shift_c[:, m:m + 1],
                                         scale=scale_c[:, m:m + 1]).then_inc(act_out, 1)
            act_deviation(act, 2)

        def dve_l2(dve):
            v = nc.vector
            v.memset(zero_w, 0.0)
            link(dve, v.memset(agg, 0.0))
            dve.sem_inc(msg_sum, CREDIT)
            dve.sem_inc(hot_ready, CREDIT)
            dve.sem_inc(agg_added, CREDIT)

            def message(c, j):
                rows_there(dve, c, j)
                dve.wait_ge(agg_psum, done(c - 2))
                v.tensor_scalar(hot_dst2[:, j % 2, 0:T], node_f[:, 0:T], row_buf[:, j, DSTL:DSTL + 1], None,
                                ALU.is_equal).then_inc(hot_ready, 1)
                dve.wait_ge(edge_psum, done(c))
                dve.wait_ge(src_in[j], (c - j) * 4 + 16)
                dve.wait_ge(msg_ready, done(c - 2))
                v.tensor_tensor(msg_in[:, j % 2, :], PS[:, 2 + j % 2, :], x_src[:, j, :], ALU.add).then_inc(msg_sum, 1)

            def add(c, j):
                t = dve.value_load(tile_of[0:1, ds(c, 1)], min_val=0, max_val=NT - 1)
                dve.wait_ge(agg_psum, done(c))
                dve.wait_ge(agg_added, done(c - 1))
                to = agg[:, ds(t, 1), :].rearrange("p a d -> p (a d)")
                v.tensor_tensor(to, PS[0:T, 4 + j % 2, :], to, ALU.add).then_inc(agg_added, 1)

            message(0, 0)

            def steps(n, first, add_):
                with dve.Fori(0, n) as step:
                    c0 = first + step * 4
                    for j in range(4):
                        message(c0 + j + 1, (j + 1) % 4)
                        if add_ is not None:
                            add_(c0 + j, j)

            is_packed = dve.value_load(packed[0:1, 0:1], min_val=0, max_val=1)
            with dve.If(is_packed):
                steps(CH // 4, 0, add)
                dve.wait_ge(agg_added, done(CH - 1))
                dve.sem_inc(agg_ready, 1)
            with dve.Else():
                dve.sem_inc(tile_added, 1)
                with dve.Fori(0, NT) as t:
                    steps(TC // 4, t * TC, None)
                    dve.wait_ge(tile_psum, t + 1)
                    v.tensor_copy(agg[:, ds(t, 1), :].rearrange("p a d -> p (a d)"), PS[0:T, 4, :]).then_inc(tile_added, 1)
                dve.wait_ge(tile_added, NT + 1)
                dve.sem_inc(agg_ready, 1)
            dve.wait_ge(agg_ready, 1)
            for landed in src_in:
                dve.wait_ge(landed, CHX // 4 * 16)
            dve.wait_ge(p2_in, 16 * 10)
            link(dve, v.tensor_scalar(eps_c, eps_c, 1.0, None, ALU.add))
            v.scalar_tensor_tensor(out=agg, in0=xN[0:T, :, :], scalar=eps_c, in1=agg, op0=ALU.mult,
                                   op1=ALU.add).then_inc(h_ready, 1)
            out_uses = 0
            for phase, (z, parts, gain, offset) in enumerate(((z1, 2 * KD, g1_c, beta1_c), (z2, KD, g2_c, beta2_c))):
                for m in range(parts):
                    out_uses += 2
                    dve.wait_ge(z_out, out_uses)
                    for h, (at, n) in enumerate(HALVES):
                        ins = v.bn_stats(bn_stat[:, m, 6 * h:6 * h + 6], z[:, m, at:at + n])
                link(dve, ins)
                for m in range(parts):
                    ins = v.bn_aggr(bn_mv[:, m, :], bn_stat[:, m, :].rearrange("p (a b) -> p a b", b=6))
                link(dve, ins)
                mean = bn_mv[:, 0:parts, 0:1].rearrange("p m a -> p (m a)")
                var = bn_mv[:, 0:parts, 1:2].rearrange("p m a -> p (m a)")
                v.tensor_scalar(bn_ve[:, 0:parts], var, EPS, None, ALU.add).then_inc(bn_var, 1)
                dve.wait_ge(bn_dev, phase + 1)
                link(dve, v.reciprocal(bn_ve[:, 0:parts], bn_sd[:, 0:parts]))
                link(dve, v.tensor_tensor(scale_c[:, 0:parts], bn_ve[:, 0:parts], gain[:, 0:parts], ALU.mult))
                link(dve, v.tensor_tensor(bn_ve[:, 0:parts], mean, scale_c[:, 0:parts], ALU.mult))
                v.tensor_tensor(shift_c[:, 0:parts], offset[:, 0:parts], bn_ve[:, 0:parts],
                                ALU.subtract).then_inc(bn_ready, 1)
            dve.wait_ge(back_psum, 1)
            for t in range(NT):
                ins = v.tensor_tensor(xN[0:T, t, :], PS[0:T, t, :], xN[0:T, t, :], ALU.add)
            link(dve, ins)
            dve_norm(dve, 2)

        def sync_l3(sp):
            sp.wait_ge(x_ready, 3)
            for to, row in ((mb2_row, p3["b2"]), (ln_g, p3["ln_g"]), (ln_b, p3["ln_b"])):
                load_rows(sp, to, row, l3_rows, T)
            sp.dma_start(mb1_c, p3["b1"]).then_inc(l3_rows, 16)
            with sp.Fori(0, LAYERS) as l:
                sp.wait_ge(w_used, l + 1)
                for n, name in enumerate(("Wq", "Wk", "Wv", "Ws")):
                    sp.dma_start(w_qkvs[n], p3[name][ds(l, 1)].rearrange("a p k o -> p (a k) o")).then_inc(l3_in, 16)
                sp.wait_ge(qk_out, l * 4 * KD + 1)
                sp.wait_ge(q_odd_out, l * 2 * KD + 1)
                sp.wait_ge(vs_out, l * 2 * NT + 1)
                for to, name in ((bq_c, "bq"), (bk_c, "bk")):
                    sp.dma_start(to, p3[name][ds(l, 1)].rearrange("a p k -> p (a k)")).then_inc(l3_in, 16)
                for to, name in ((bv_row, "bv"), (bs_row, "bs")):
                    sp.dma_start(to, p3[name][ds(l, 1)].to_broadcast((T, D))).then_inc(l3_in, 16)
            sp.wait_ge(w_used, LAYERS + 1)
            sp.dma_start(mlp1, p3["W1"]).then_inc(mlp_in, 16)
            sp.dma_start(mlp2, p3["W2"]).then_inc(mlp_in, 16)
            sp.wait_ge(x_ready, 6)
            sp.dma_start(out.rearrange("(t p) d -> p t d", p=T), xN[0:T, :, :]).then_inc(stored, 16)
            sp.wait_ge(stored, 16)

        STEPS = NT * HEADS

        def through(n):
            return n + 1 + 2

        def qk_emptied(eng, l, use):
            eng.wait_ge(qk_out, l * 4 * KD + use + 1 + 1)
            if use < 2 * KD:
                eng.wait_ge(q_odd_out, l * 2 * KD + use + 1 + 1)

        def pe_l3(pe):
            t_ = nc.tensor
            pe.wait_ge(x_ready, 3)
            for q in (w_used, ):
                pe.sem_inc(q, 1)
            for q in (score_psum, turn_psum):
                pe.sem_inc(q, 2)
            with pe.Fori(0, LAYERS) as l:
                pe.wait_ge(l3_x, l + 1)
                transposes(xN)
                pe.wait_ge(xt_ready, NT * 3 + NT + l * NT)
                pe.wait_ge(l3_in, l * 128 + 128)
                use = 0
                for w in range(2):
                    for m in range(KD):
                        for at, n in HALVES:
                            if use >= 8:
                                qk_emptied(pe, l, use - 8)
                            for k in range(KD):
                                mm = t_.matmul(PS[:, use % 8, 0:n], w_qkvs[w][:, k, m * P:(m + 1) * P],
                                               xTk[:, k, at:at + n], start=(k == 0), stop=(k == KD - 1))
                            mm.then_inc(proj, 1)
                            use += 1
                for w in range(2, 4):
                    for t in range(NT):
                        if use < 24:
                            qk_emptied(pe, l, use - 8)
                        else:
                            pe.wait_ge(vs_out, l * 2 * NT + use - 23 + 1)
                        for k in range(KD):
                            mm = t_.matmul(PS[0:T, use % 8, :], xTk[:, k, t * T:(t + 1) * T], w_qkvs[w][:, k, :],
                                           start=(k == 0), stop=(k == KD - 1))
                        mm.then_inc(proj, 1)
                        use += 1
                qk_emptied(pe, l, 2 * KD - 1)
                qk_emptied(pe, l, 4 * KD - 1)
                pe.wait_ge(vs_out, l * 2 * NT + 2 * NT + 1)
                pe.sem_inc(w_used, 1)

                def score(n):
                    h, t = divmod(n, NT)
                    pe.wait_ge(score_out, through(l * STEPS + n - 2))
                    for at, m in HALVES_B:
                        mm = t_.matmul(PS[0:T, n % 2 * 2 + at // 512, 0:m], q_t[h % 2][:, h // 2, t * T:(t + 1) * T],
                                       k_t[:, h // 2, at:at + m], start=True, stop=True)
                    mm.then_inc(score_psum, 1)

                def turn(n):
                    pe.wait_ge(probs_out, through(l * STEPS + n))
                    pe.wait_ge(turn_out, through(l * STEPS + n - 1))
                    for st in range(NT):
                        mm = t_.transpose(PS[0:T, 4 + st // 4, st % 4 * P:st % 4 * P + T],
                                          probs[:, n % 2, st * T:(st + 1) * T], identT)
                    mm.then_inc(turn_psum, 1)

                def mix(n):
                    h, st = divmod(n, NT)
                    if st == 0:
                        pe.wait_ge(turn_out, through(l * STEPS + n + NT - 1))
                        if h % 2 == 0 and h > 0:
                            pe.wait_ge(pair_out, l * KD + h // 2)
                    for at, m in HALVES_B:
                        mm = t_.matmul(PS[:, 6 + at // 512, 0:m], val[:, st, h * P:(h + 1) * P],
                                       probs_t[:, h % 2, st * N + at:st * N + at + m],
                                       start=(h % 2 == 0 and st == 0), stop=(h % 2 == 1 and st == NT - 1))
                    mm.then_inc(mixed_part, 1)

                score(0)
                for n in range(STEPS):
                    if n + 1 < STEPS:
                        score(n + 1)
                    turn(n)
                    if n >= NT:
                        mix(n - NT)
                for n in range(STEPS - NT, STEPS):
                    mix(n)
                pe.wait_ge(score_out, through(l * STEPS + STEPS - 1))
                pe.wait_ge(pair_out, (l + 1) * KD)
                for t in range(NT):
                    for j in range(KD):
                        mm = t_.transpose(PS[0:T, t, j * P:(j + 1) * P], mixed_t[:, j, t * T:(t + 1) * T], ident[:, :])
                    mm.then_inc(heads_psum, 1)
            pe.wait_ge(x_ready, 4)
            transposes(xN)
            pe.wait_ge(xt_ready, NT * (4 + LAYERS))
            pe.wait_ge(mlp_in, 32)
            use = 0
            for m in range(2 * KD):
                for at, n in HALVES:
                    if use >= 8:
                        pe.wait_ge(hid_out, use - 7)
                    for k in range(KD):
                        mm = t_.matmul(PS[:, use % 8, 0:n], mlp1[:, k, m * P:(m + 1) * P], xTk[:, k, at:at + n],
                                       start=(k == 0), stop=(k == KD - 1))
                    mm.then_inc(hid_psum, 1)
                    use += 1
            pe.wait_ge(hid_out, use)
            for t in range(NT):
                for k in range(2 * KD):
                    mm = t_.matmul(PS[0:T, t, :], hid[:, k, t * T:(t + 1) * T], mlp2[:, k, :],
                                   start=(k == 0), stop=(k == 2 * KD - 1))
            mm.then_inc(mlp_psum, 1)

        def act_l3(act):
            act.sem_inc(qk_out, 1)
            act.sem_inc(probs_out, 2)
            act.sem_inc(turn_out, 2)
            with act.Fori(0, LAYERS) as l:
                for b in range(NT):
                    act.wait_ge(xt_psum, 3 * NT + l * NT + b + 1)
                    nc.scalar.copy(xT[:, b * 4 * T:(b + 1) * 4 * T], PS[:, b, 0:4 * T]).then_inc(xt_ready, 1)
                act.wait_ge(l3_in, l * 128 + 128)
                use = 0
                for to, bias, n_p in ((q_t[0], bq_c, HD), (k_t, bk_c, P)):
                    for m in range(KD):
                        for at, n in HALVES:
                            act.wait_ge(proj, l * (4 * KD + 2 * NT) + use + 1)
                            nc.scalar.activation(to[0:n_p, m, at:at + n], PS[0:n_p, use % 8, 0:n], ACT.Identity,
                                                 bias=bias[0:n_p, m:m + 1]).then_inc(qk_out, 1)
                            use += 1

                def exponent(n):
                    act.wait_ge(score_out, through(l * STEPS + n))
                    act.wait_ge(turn_psum, through(l * STEPS + n - 2))
                    nc.scalar.activation(probs[:, n % 2, :], scores[:, n % 2, :], ACT.Exp,
                                         bias=minus_top[:, n % 4:n % 4 + 1], scale=float(HD) ** -0.5,
                                         accum_out=denom[:, n % NT, n // NT:n // NT + 1]).then_inc(probs_out, 1)

                def keep_turned(n):
                    act.wait_ge(turn_psum, through(l * STEPS + n))
                    h, t = divmod(n, NT)
                    if t == 0 and h >= 2:
                        act.wait_ge(mixed_part, l * STEPS + n - NT)
                    nc.scalar.copy(probs_t[:, h % 2, :].rearrange("p (s n) -> p s n", n=N)[:, :, t * T:(t + 1) * T],
                                   two_banks(4, T, NT * P).rearrange("p (t n) -> p t n", n=P)[:, :, 0:T]
                                   ).then_inc(turn_out, 1)

                def keep_pair(j):
                    act.wait_ge(mixed_part, l * STEPS + (j + 1) * 2 * NT)
                    for at, m in HALVES_B:
                        ins = nc.scalar.copy(mixed_t[:, j, at:at + m], PS[:, 6 + at // 512, 0:m])
                    ins.then_inc(pair_out, 1)

                exponent(0)
                for n in range(STEPS):
                    if n + 1 < STEPS:
                        exponent(n + 1)
                    keep_turned(n)
                    if n % (2 * NT) == 3 * NT % (2 * NT) - 1 and n > 2 * NT:
                        keep_pair(n // (2 * NT) - 1)
                keep_pair(KD - 1)
            act_deviation(act, 3)
            act_turn(act, 3 + LAYERS, xT)
            act.wait_ge(l3_rows, 64)
            use = 0
            for m in range(2 * KD):
                for at, n in HALVES:
                    act.wait_ge(hid_psum, use + 1)
                    nc.scalar.activation(hid[:, m, at:at + n], PS[:, use % 8, 0:n], ACT.Relu,
                                         bias=mb1_c[:, m:m + 1]).then_inc(hid_out, 1)
                    use += 1
            act_deviation(act, 4)
            act_deviation(act, 5)

        def dve_l3(dve):
            v = nc.vector
            dve.sem_inc(vs_out, 1)
            dve.sem_inc(score_out, 2)
            dve.sem_inc(q_odd_out, 1)
            v.memset(q_t[0][HD:P, :, :], 0.0)
            v.memset(q_t[1][0:HD, :, :], 0.0)
            link(dve, v.memset(val, 0.0))
            v.tensor_copy(enc, xN[0:T, :, :]).then_inc(l3_x, 1)
            with dve.Fori(0, LAYERS) as l:
                dve.wait_ge(l3_in, l * 128 + 128)
                use = 0
                for m in range(KD):
                    for at, n in HALVES:
                        dve.wait_ge(proj, l * (4 * KD + 2 * NT) + use + 1)
                        v.tensor_scalar(q_t[1][HD:P, m, at:at + n], PS[HD:P, use % 8, 0:n], bq_c[HD:P, m:m + 1], None,
                                        ALU.add).then_inc(q_odd_out, 1)
                        use += 1
                use = 4 * KD

                def two_heads(row, n):
                    return row.rearrange("p (j a d) -> p j a d", a=2, d=HD)[:, :, n, :]

                for t in range(NT):
                    dve.wait_ge(proj, l * (4 * KD + 2 * NT) + use + 1)
                    for n in range(2):
                        to = val[:, t, :].rearrange("p (j a d) -> p j a d", a=2, d=P)[:, :, n, n * HD:(n + 1) * HD]
                        ins = v.tensor_tensor(to, two_heads(PS[0:T, use % 8, :], n), two_heads(bv_row, n), ALU.add)
                    ins.then_inc(vs_out, 1)
                    use += 1
                for t in range(NT):
                    dve.wait_ge(proj, l * (4 * KD + 2 * NT) + use + 1)
                    v.tensor_tensor(rest[:, t, :], PS[0:T, use % 8, :], bs_row, ALU.add).then_inc(vs_out, 1)
                    use += 1
                dve.wait_ge(vs_out, l * 2 * NT + 2 * NT + 1)
                v.tensor_tensor(rest, rest, enc, ALU.add).then_inc(o_step, 1)

                def mask(n):
                    t = n % NT
                    dve.wait_ge(score_psum, through(l * STEPS + n))
                    dve.wait_ge(probs_out, through(l * STEPS + n - 2))
                    dve.sem_inc(tick, 1)
                    v.tensor_tensor_reduce(out=scores[:, n % 2, :], in0=two_banks(n % 2 * 2, T), in1=pairs_t[:, t, :],
                                           scale=1.0, scalar=3 * FAR, op0=ALU.add, op1=ALU.max,
                                           accum_out=top[:, n % 4:n % 4 + 1]).then_inc(top_ready, 1)
                    dve.wait_ge(top_ready, l * STEPS + n + 1)
                    v.tensor_scalar(minus_top[:, n % 4:n % 4 + 1], top[:, n % 4:n % 4 + 1], -float(HD) ** -0.5, None,
                                    ALU.mult).then_inc(score_out, 1)

                def finish(t):
                    at = l * (1 + 4 * NT) + 1 + 4 * t
                    dve.wait_ge(heads_psum, l * NT + t + 1)
                    dve.wait_ge(o_step, at)
                    v.tensor_scalar(inv[:, t, :], denom[:, t, :], 1e-16, None, ALU.add).then_inc(o_step, 1)
                    dve.wait_ge(o_step, at + 1)
                    v.reciprocal(inv[:, t, :], inv[:, t, :]).then_inc(o_step, 1)
                    dve.wait_ge(o_step, at + 2)
                    v.tensor_scalar(inv[:, t, :], inv[:, t, :], has_in[0:T, t:t + 1], None, ALU.mult).then_inc(o_step, 1)
                    dve.wait_ge(o_step, at + 3)
                    v.tensor_tensor(xN[0:T, t, :].rearrange("p (h d) -> p h d", d=HD),
                                    PS[0:T, t, :].rearrange("p (h d) -> p h d", d=HD),
                                    inv[:, t, :].unsqueeze(2).broadcast_to([T, HEADS, HD]), ALU.mult).then_inc(tile_out, 1)
                    dve.wait_ge(tile_out, l * NT + t + 1)
                    v.tensor_tensor(xN[0:T, t, :], xN[0:T, t, :], rest[:, t, :], ALU.add).then_inc(o_step, 1)

                for n in range(STEPS):
                    mask(n)
                for t in range(NT):
                    finish(t)
                dve.wait_ge(o_step, (l + 1) * (1 + 4 * NT))
                dve.sem_inc(l3_x, 1)
            dve.wait_ge(l3_rows, 64)
            dve_norm(dve, 3, ln_g, ln_b)
            dve.wait_ge(mlp_psum, 1)
            link(dve, v.tensor_tensor(xN[0:T, :, :], xN[0:T, :, :], over_tiles(mb2_row), ALU.add))
            for t in range(NT):
                ins = v.tensor_tensor(xN[0:T, t, :], PS[0:T, t, :], xN[0:T, t, :], ALU.add)
            link(dve, ins)
            dve_norm(dve, 4, ln_g, ln_b)
            for _ in range(2):
                link(dve, v.tensor_tensor(xN[0:T, :, :], xN[0:T, :, :], enc, ALU.add))
            dve_norm(dve, 5)

        @block.sync
        def _(sp):
            sync_sort(sp)
            sync_l0(sp)
            sync_l1(sp)
            sync_l2(sp)
            sync_l3(sp)

        @block.gpsimd
        def _(pool):
            pool_sort(pool)
            pool_l2(pool)

        @block.tensor
        def _(pe):
            pe_sort(pe)
            pe.wait_ge(plan_ready, 1)
            is_packed = pe.value_load(packed[0:1, 0:1], min_val=0, max_val=1)
            with pe.If(is_packed):
                pe_count_packed(pe)
            with pe.Else():
                pe_count(pe)
            pe_l0(pe)
            pe_l1(pe)
            pe_l2(pe)
            pe_l3(pe)

        @block.scalar
        def _(act):
            act_products(act)
            act.wait_ge(plan_ready, 1)
            is_packed = act.value_load(packed[0:1, 0:1], min_val=0, max_val=1)
            with act.If(is_packed):
                act.wait_ge(weights_ready, 1)
            with act.Else():
                act_count(act)
            act_l0(act)
            act_l1(act)
            act_l2(act)
            act_l3(act)

        @block.vector
        def _(dve):
            dve_sort(dve)
            dve_count_start(dve)
            is_packed = dve.value_load(packed[0:1, 0:1], min_val=0, max_val=1)
            with dve.If(is_packed):
                dve_count_packed(dve)
            with dve.Else():
                dve_count(dve)
            dve.sem_inc(tallied, 1)
            dve_l0(dve)
            dve_l1(dve)
            dve_l2(dve)
            dve_l3(dve)


def _tiles(w):
    import numpy as np
    w = np.asarray(w)
    k = w.shape[-2] // 128
    return np.ascontiguousarray(np.moveaxis(w.reshape(w.shape[:-2] + (k, 128, w.shape[-1])), -2, -3))


def _columns(b):
    import numpy as np
    b = np.asarray(b)
    return np.ascontiguousarray(np.moveaxis(b.reshape(b.shape[:-1] + (b.shape[-1] // 128, 128)), -1, -2))


def kernel(**inputs):
    import numpy as np
    import concourse.bacc as bacc
    from concourse.bass_utils import run_bass_kernel_spmd as run

    a = {name: np.ascontiguousarray(v) for name, v in inputs.items()}
    layers = [{}, {}, {}, {}]
    plain = {}
    for name, v in a.items():
        if name[0] == "L" and name[2:6] == "_gnn":
            layers[int(name[1])][name[7:]] = v
        else:
            plain[name] = v
    for name in ("W_self", "W_rel"):
        layers[0][name] = _tiles(np.swapaxes(layers[0][name], -1, -2))
    layers[1]["U"] = _tiles(layers[1]["U"])
    layers[2]["eps"] = layers[2]["eps"].reshape(1)
    for n, names in ((2, ("W1", "W2")), (3, ("Wq", "Wk", "Wv", "Ws", "W1", "W2"))):
        for name in names:
            layers[n][name] = _tiles(layers[n][name])
    for n, names in ((2, ("b1", "g1", "beta1", "b2", "g2", "beta2")), (3, ("bq", "bk", "b1"))):
        for name in names:
            layers[n][name] = _columns(layers[n][name])

    nc = bacc.Bacc("TRN2", target_bir_lowering=False, num_devices=1)
    arrays = {}

    def given(name, v):
        arrays[name] = v
        return nc.dram_tensor(name, v.shape, mybir.dt.from_np(v.dtype), kind="ExternalInput").ap()

    args = [given("in_" + name, plain[name]) for name in ("x", "src", "dst", "edge_attr_64", "edge_type_8", "edge_weight")]
    parameters = [{name: given(f"in_L{n}_{name}", v) for name, v in layer.items()} for n, layer in enumerate(layers)]
    out = nc.dram_tensor("out_x", (N, D), F32, kind="ExternalOutput").ap()
    program(nc, *args, *parameters, out)
    return run(nc, [arrays], core_ids=[0]).results[0]["out_x"]
```

```python
from contextlib import ExitStack

import concourse.bass as bass
from concourse import mybir

F32 = mybir.dt.float32
F16 = mybir.dt.float16
FR = mybir.dt.float32r
I32 = mybir.dt.int32
U16 = mybir.dt.uint16
ALU = mybir.AluOpType
ACT = mybir.ActivationFunctionType
X = mybir.AxisListType.X
ds = bass.ds

P = 128
N = 625
T = 125
NT = N // T
NP = N + 1
D = 512
KD = D // P
E = 20000
EC = E // T
R = 8
G = NT * R
GC = 5
TC = R * GC
CH = G * GC
assert CH * P >= E + G * (P - 1)
STEP = 8
CHX = CH + STEP
EA = 64
ROW = EA + 4
SRC, DSTL, WGT, SRCI = EA, EA + 1, EA + 2, EA + 3
RANK = 64
HEADS, HD = 8, 64
LAYERS = 2
EPS = 1e-5
FAR = -1e30
H0 = 313
HALVES = ((0, H0), (H0, N - H0))
HALVES_P = ((0, 512), (512, NP - 512))
HALVES_B = ((0, 512), (512, N - 512))
TURNS = (4, 4, 4, 4, 3, 3, 3)
T2 = T + 1
PRODUCTS = 1 + 2 * R
BY_POOL = 3
CREDIT = 8
AHEAD = 3
TURN_AHEAD = AHEAD + 1
PIECES = 16


def done(c):
    return c + 1 + CREDIT


def program(nc, x, src, dst, edge_attr, edge_type, edge_weight, p0, p1, p2, p3, out):
    with ExitStack() as ctx:
        def sem(name):
            return ctx.enter_context(nc.semaphore(name))

        table = nc.dram_tensor("sorted_rows", (P * CHX, ROW), F32, kind="Internal").ap()
        xb_rows = nc.dram_tensor("x_plus_b_e", (N, D), F32, kind="Internal").ap()
        products = nc.dram_tensor("x_times_w", (PRODUCTS, N, D), F32, kind="Internal").ap()
        table_p = table.rearrange("(p c) e -> p (c e)", p=P)

        base_bytes = -(-nc.sbuf_base // 64) * 64
        last = [0]

        def up(n):
            return n + (-n) % 8

        def place(name, shape, dt=F32, at=None):
            size = 1
            for n in shape[1:]:
                size *= n
            if at is None:
                at = last[0]
                last[0] += up(size)
            return nc.alloc_sbuf_tensor_at(name, shape, dt, offset=base_bytes + 4 * at)

        xN = place("xN", [P, NT, D])
        xT_at = last[0]
        xT = place("xT", [P, KD * N])
        pairs_at = last[0]
        pairs = place("pairs", [P, NT * N])
        wadj = place("wadj", [P, NT * N])
        ident = place("ident", [P, P])
        node_f = place("node_f", [P, NP])
        arena_at = last[0]
        arena = place("arena", [P, G * N])
        counts = place("counts", [P, G * N], U16, arena_at)
        upper_at = arena_at + up(G * N // 2)
        annex_at = last[0]
        annex = place("annex", [P, CHX * ROW])
        group = place("group", [1, CH], I32)
        tile_of = place("tile_of", [1, CH], I32)
        packed = place("packed", [1, 1], I32)
        stat = place("stat", [P, NT, 6])
        mv = place("mv", [P, NT, 2])
        sd = place("sd", [P, NT])
        rstd = place("rstd", [P, NT])
        ident_r = place("ident_r", [P, P], FR)
        has_in = place("has_in", [P, NT])
        w_lo = place("w_lo", [P, CH])
        w_hi = place("w_hi", [P, CH], FR)
        PS = ctx.enter_context(nc.psum_tensor("PS", [P, 8, 512], F32))

        xTk = xT[:, :].rearrange("p (k n) -> p k n", n=N)
        identT = ident[0:T, 0:T]

        def view(tensor, at, shape, parts=P):
            size = 1
            for n in shape:
                size *= n
            v = tensor[0:parts, at:at + size]
            if len(shape) == 2:
                v = v.rearrange("p (a b) -> p a b", b=shape[1])
            return v

        def two_banks(b, parts, n=N):
            return PS[0:parts, b:b + 2, :].rearrange("p b n -> p (b n)")[:, 0:n]

        rows = view(annex, 0, [EC, ROW], T)
        hot = place("hot", [T, G, EC], F16, arena_at)
        keep = place("keep", [T, G, EC], F16, arena_at + G * EC // 2)
        rank = view(arena, G * EC, [G, EC], T)
        past = view(arena, 0, [CH, G], 1)
        (src_f, dst_f, typ_f, wgt, tile, key, dst_l, slot_f, lo_f, hi_f) = [
            view(pairs, n * EC, [EC], T) for n in range(10)]
        (src_i, dst_i, typ_i, slot_i, lo_i, hi_i, pos_i) = [
            view(pairs, n * EC, [EC], T).bitcast(I32) for n in range(10, 17)]
        (cnt, chunks_f, upto, start, base, ones_g) = [view(pairs, 17 * EC + n * G, [G]) for n in range(6)]
        chunks_i = view(pairs, 17 * EC + 6 * G, [G]).bitcast(I32)
        group_no = xT[:, 0:G]
        chunk_no = xT[0:1, G:G + CH]
        group_f = xT[0:1, G + CH:G + 2 * CH]
        before = xT[0:T, 600:600 + T]
        ones_m = xT[0:T, 800:800 + P]
        pad = view(wadj, 0, [CHX // PIECES, ROW])
        crowded = xT[:, 950:951]
        slots_f = xT[:, 960:960 + G]

        sorted_rows = view(annex, 0, [CH, ROW])
        hot_src = place("hot_src", [P, 4, NP], FR, xT_at)
        hot_dst = place("hot_dst", [P, 4, P], FR, pairs_at + 64)
        hot_hi = place("hot_hi", [P, 4, P], FR, pairs_at + 64 + 4 * P)
        hot_lo = place("hot_lo", [P, 4, P], FR, pairs_at + 64 + 8 * P)

        x_hi = place("x_hi", [P, KD * N], FR, arena_at + 2 * G * EC)
        x_lo = place("x_lo", [P, KD * N], FR, arena_at + 2 * G * EC + up(KD * N))
        mat_at = arena_at + 2 * G * EC + 2 * up(KD * N)
        mat_hi = place("mat_hi", [P, KD, D], FR, mat_at)
        mat_lo = place("mat_lo", [P, KD, D], FR, mat_at + KD * D)
        mat = (view(arena, mat_at - arena_at + 2 * KD * D, [KD, D]), view(wadj, CHX // PIECES * ROW, [KD, D]))
        product = view(annex, EC * ROW, [NT, D], T)

        here = place("here", [P, NT, N], FR, annex_at)
        turned_at = annex_at + up(NT * N)
        turned = place("turned", [P, NT, NT, T2], FR, turned_at)
        h_out_at = turned_at + up(NT * NT * T2)
        h_hi = [place("h_hi_out", [T, NT, D], FR, h_out_at), place("h_hi_in", [T, NT, D], FR, upper_at)]
        h_lo = [place("h_lo_out", [T, NT, D], FR, h_out_at + NT * D),
                place("h_lo_in", [T, NT, D], FR, upper_at + NT * D)]
        h = [view(arena, upper_at - arena_at + (2 + n) * NT * D, [NT, D], T) for n in range(2)]
        h_bias = [view(arena, upper_at - arena_at + 4 * NT * D + n * D, [D], T) for n in range(2)]
        pairs_t = view(pairs, 0, [NT, N], T)
        wadj_t = view(wadj, 0, [NT, N], T)
        sums = view(arena, 0, [NT, D], T)

        u_w = view(arena, 3000, [KD, RANK])
        vt_w = view(arena, 3300, [D], RANK)
        s_row = view(arena, 3900, [RANK], T)
        b1_row = view(arena, 4000, [D], T)
        support = view(arena, 4600, [NT, RANK], T)
        mixed = view(arena, 5000, [N], RANK)
        be_row = view(arena, 6000, [D], T)
        xb = view(arena, 6600, [NT, D], T)
        ln_pairs = view(arena, 20000, [NT * N], T)

        row_buf = view(xT, 0, [STEP, ROW])
        x_src = view(arena, 0, [STEP, D])
        msg_in = view(arena, 9600, [4, D])
        msg = view(arena, 11700, [2, D])
        zero_w = view(arena, 19620, [T])
        hot_dst2 = place("hot_dst2", [P, 4, P], FR, arena_at + 12800)
        agg = view(arena, 14500, [NT, D], T)
        h_t = view(arena, 17100, [KD * N])
        h_tk = view(arena, 17100, [KD, N])
        z1 = view(arena, 20000, [2 * KD, N])
        z2 = view(arena, 0, [KD, N])
        w1 = view(annex, 0, [KD, 2 * D])
        w2 = view(annex, 2 * KD * D, [2 * KD, D])
        w_e = view(annex, 4 * KD * D, [D])
        w_e_hi = place("w_e_hi", [P, D], FR, annex_at + 9216)
        w_e_lo = place("w_e_lo", [P, D], FR, annex_at + 9728)
        attr2 = place("attr2", [P, 4, 2 * EA], FR, annex_at + 10240)
        attr_t = place("attr_t", [P, 4, P], FR, annex_at + 13056)
        msg_hi = place("msg_hi", [P, 2, D], FR, annex_at + 11008)
        msg_lo = place("msg_lo", [P, 2, D], FR, annex_at + 12032)
        small2 = 4 * KD * D + D
        (b1_c, g1_c, beta1_c, b2_c, g2_c, beta2_c, scale_c, shift_c, bn_ve, bn_sd) = [
            view(annex, small2 + 8 * n, [8]) for n in range(10)]
        eps_c = view(annex, small2 + 80, [1], T)
        bn_stat = view(annex, small2 + 96, [2 * KD, 12])
        bn_mv = view(annex, small2 + 192, [2 * KD, 2])

        q_t = [view(arena, n * KD * N, [KD, N]) for n in range(2)]
        k_t = view(arena, 2 * KD * N, [KD, N])
        val_at = 3 * KD * N
        val = view(arena, val_at, [NT, HEADS * P], T)
        probs_at = val_at + NT * HEADS * P
        probs_t = view(arena, probs_at, [2, NT * N], T)
        mixed_t = view(arena, probs_at + 2 * NT * N, [KD, N])
        scores_at = probs_at + 2 * NT * N + KD * N
        scores = view(arena, scores_at, [2, N], T)
        probs = view(arena, scores_at + 2 * N, [2, N], T)
        top = view(arena, scores_at + 4 * N, [4], T)
        minus_top = view(arena, scores_at + 4 * N + 4, [4], T)
        denom = view(arena, scores_at + 4 * N + 8, [NT, HEADS], T)
        inv = view(arena, scores_at + 4 * N + 8 + NT * HEADS, [NT, HEADS], T)
        enc = view(wadj, 0, [NT, D], T)
        rest = view(annex, 10880, [NT, D], T)
        with_bias = rest
        mlp1 = view(annex, 0, [KD, 2 * D])
        mlp2 = view(annex, 2 * KD * D, [2 * KD, D])
        hid = view(arena, 0, [2 * KD, N])
        w_qkvs = [view(annex, n * KD * D, [KD, D]) for n in range(4)]
        bq_c = view(annex, 8200, [KD])
        bk_c = view(annex, 8210, [KD])
        mb1_c = view(annex, 8220, [2 * KD])
        bv_row, bs_row, mb2_row, ln_g, ln_b = [view(annex, 8300 + D * n, [D], T) for n in range(5)]

        edges_in = sem("edges_in")
        attr_in = sem("attr_in")
        pad_ready = sem("pad_ready")
        cleared = sem("cleared")
        x_in = sem("x_in")
        consts = sem("consts")
        rows_ready = sem("rows_ready")
        keep_ready = sem("keep_ready")
        ranked = sem("ranked")
        prefixed = sem("prefixed")
        slots_ready = sem("slots_ready")
        scattered = sem("scattered")
        sorted_in = sem("sorted_in")
        v_step = sem("v_step")
        g_step = sem("g_step")
        zeroed = sem("zeroed")
        plan_ready = sem("plan_ready")
        plan_step = sem("plan_step")
        weights_rounded = sem("weights_rounded")
        weights_ready = sem("weights_ready")
        hot_made = sem("hot_made")
        hot_scaled = sem("hot_scaled")
        chunk_done = sem("chunk_done")
        counts_out = sem("counts_out")
        weights_out = sem("weights_out")
        tallied = sem("tallied")
        onehots = sem("onehots")
        counted = sem("counted")
        added = sem("added")
        xt_psum = sem("xt_psum")
        xt_ready = sem("xt_ready")
        x_split = sem("x_split")
        mat_in = [sem(f"mat_in{n}") for n in range(2)]
        mat_hi_ready = sem("mat_hi_ready")
        mat_lo_ready = sem("mat_lo_ready")
        mat_used = sem("mat_used")
        product_psum = sem("product_psum")
        product_out = sem("product_out")
        product_stored = sem("product_stored")
        here_rounded = sem("here_rounded")
        here_ready = sem("here_ready")
        here_added = sem("here_added")
        scratch = sem("scratch")
        out_act = sem("out_act")
        out_dve = sem("out_dve")
        h_in = [sem(f"h_in_{side}") for side in ("out", "in")]
        h_biased = [sem(f"h_biased_{side}") for side in ("out", "in")]
        h_hi_ready = [sem(f"h_hi_ready_{side}") for side in ("out", "in")]
        h_split = [sem(f"h_split_{side}") for side in ("out", "in")]
        h_used = [sem(f"h_used_{side}") for side in ("out", "in")]
        acc_done = sem("acc_done")
        var_ready = sem("var_ready")
        sd_ready = sem("sd_ready")
        x_ready = sem("x_ready")

        p1_in = sem("p1_in")
        support_psum = sem("support_psum")
        support_ready = sem("support_ready")
        mixed_psum = sem("mixed_psum")
        mixed_ready = sem("mixed_ready")
        l1_psum = sem("l1_psum")
        clipped = sem("clipped")
        logs_ready = sem("logs_ready")
        p2_in = sem("p2_in")
        xb_ready = sem("xb_ready")
        xb_stored = sem("xb_stored")
        rows_in = [sem(f"rows_in{n}") for n in range(STEP // 2)]
        src_in = [sem(f"src_in{n}") for n in range(STEP)]
        pool_tick = sem("pool_tick")
        w_e_in = sem("w_e_in")
        w_e_ready = sem("w_e_ready")
        attr_hi = sem("attr_hi")
        attr_lo = sem("attr_lo")
        msg_split = sem("msg_split")
        attr_psum = sem("attr_psum")
        attr_out = sem("attr_out")
        edge_psum = sem("edge_psum")
        msg_sum = sem("msg_sum")
        hot_ready = sem("hot_ready")
        msg_ready = sem("msg_ready")
        agg_psum = sem("agg_psum")
        agg_added = sem("agg_added")
        tile_psum = sem("tile_psum")
        tile_added = sem("tile_added")
        agg_ready = sem("agg_ready")
        h_ready = sem("h_ready")
        z_psum = sem("z_psum")
        z_out = sem("z_out")
        bn_var = sem("bn_var")
        bn_dev = sem("bn_dev")
        bn_ready = sem("bn_ready")
        act_out = sem("act_out")
        back_psum = sem("back_psum")
        l3_x = sem("l3_x")
        l3_in = sem("l3_in")
        l3_rows = sem("l3_rows")
        q_zeroed = sem("q_zeroed")
        val_zeroed = sem("val_zeroed")
        proj = sem("proj")
        qk_out = sem("qk_out")
        q_odd_out = sem("q_odd_out")
        vs_out = sem("vs_out")
        w_used = sem("w_used")
        score_psum = sem("score_psum")
        top_ready = sem("top_ready")
        score_out = sem("score_out")
        probs_out = sem("probs_out")
        turn_psum = sem("turn_psum")
        turn_out = sem("turn_out")
        mixed_part = sem("mixed_part")
        pair_out = sem("pair_out")
        heads_psum = sem("heads_psum")
        tile_out = sem("tile_out")
        o_step = sem("o_step")
        mlp_in = sem("mlp_in")
        hid_psum = sem("hid_psum")
        hid_out = sem("hid_out")
        mlp_psum = sem("mlp_psum")
        tile_normed = sem("tile_normed")
        stored = sem("stored")
        tick = sem("tick")

        block = ctx.enter_context(nc.Block())

        def load_rows(sp, to, row, done_sem, n):
            sp.dma_start(to, row.rearrange("(a d) -> a d", a=1).to_broadcast((n, row.shape[0]))).then_inc(done_sem, 16)

        def sync_sort(sp):
            for tile_to, row in ((src_i, src), (dst_i, dst), (typ_i, edge_type), (wgt, edge_weight)):
                sp.dma_start(tile_to, row.rearrange("(p c) -> p c", p=T)).then_inc(edges_in, 16)
            sp.dma_start(xN[0:T, :, :], x.rearrange("(t p) d -> p t d", p=T)).then_inc(x_in, 16)
            sp.dma_start(mat[0], p0["W_self"]).then_inc(mat_in[0], 16)
            sp.dma_start(mat[1], p0["W_rel"][0]).then_inc(mat_in[1], 16)
            sp.dma_start(rows[:, :, 0:EA], edge_attr.rearrange("(p c) e -> p c e", p=T)).then_inc(attr_in, 16)
            sp.wait_ge(mat_lo_ready, KD)
            sp.dma_start(mat[0], p0["W_rel"][1]).then_inc(mat_in[0], 16)
            sp.wait_ge(mat_lo_ready, 2 * KD)
            sp.dma_start(mat[1], p0["W_rel"][2]).then_inc(mat_in[1], 16)
            def store(i):
                sp.wait_ge(product_out, emptied(i, NT - 1))
                sp.dma_start(products[ds(i, 1)].rearrange("a (t p) d -> p (a t) d", p=T), product
                             ).then_inc(product_stored, 16)

            store(0)
            sp.wait_ge(pad_ready, 1)
            piece = CHX // PIECES * ROW
            for n in range(PIECES):
                if n == PIECES // 4:
                    store(1)
                sp.dma_start(table_p[:, n * piece:(n + 1) * piece],
                             pad.rearrange("p c e -> p (c e)")).then_inc(cleared, 16)

            def load_matrix(i, j):
                sp.wait_ge(mat_lo_ready, (i - 1) * KD)
                sp.dma_start(mat[j], p0["W_rel"][ds(i - 1, 1)].rearrange("a p k o -> p (a k) o")).then_inc(mat_in[j], 16)

            with sp.Fori(0, R - 2) as pair:
                for j in range(2):
                    load_matrix(pair * 2 + 4 + j, j)
                    store(pair * 2 + 2 + j)
            load_matrix(PRODUCTS - 1, 0)
            for i in range(PRODUCTS - 3, PRODUCTS):
                store(i)
            sp.wait_ge(scattered, 16 * EC)
            sp.wait_ge(product_stored, 16 * (PRODUCTS + 1))
            with sp.Fori(0, NT) as t:
                sp.wait_ge(sorted_in, t * 16 + 16)
                sp.dma_start(annex[:, ds(t * TC * ROW, TC * ROW)],
                             table_p[:, ds(t * TC * ROW, TC * ROW)]).then_inc(sorted_in, 16)

        def sync_l0(sp):
            def load(side, row, bias):
                sp.dma_start(h[side], row.rearrange("a (t p) d -> p (a t) d", p=T)).then_inc(h_in[side], 16)
                sp.dma_start(h_bias[side], bias.to_broadcast((T, D))).then_inc(h_in[side], 16)

            sp.wait_ge(product_psum, NT * PRODUCTS)
            sp.sem_inc(h_split[0], NT)
            load(1, products[0:1], p0["b_self"].rearrange("(a d) -> a d", a=1))

            def relations(first):
                with sp.Fori(0, R) as r:
                    for side in range(2):
                        sp.wait_ge(h_split[side], (first + r + 1) * NT)
                        load(side, products[ds(r + 1 + side * R, 1)], p0["b_rel"][ds(r + side * R, 1), :])

            relations(0)
            is_packed = sp.value_load(packed[0:1, 0:1], min_val=0, max_val=1)
            with sp.If(is_packed):
                relations(R)

        def split_rest(eng, unit, i, j):
            for k in range(KD):
                eng.wait_ge(mat_hi_ready, i * KD + k + 1)
                unit.tensor_tensor(mat_lo[:, k, :], mat[j][:, k, :], mat_hi[:, k, :].bitcast(F32),
                                  ALU.subtract).then_inc(mat_lo_ready, 1)

        def pool_sort(pool):
            g = nc.gpsimd
            g.iota(node_f[:, :], pattern=[[1, NP]], base=0, channel_multiplier=0,
                   allow_small_or_imprecise_dtypes=True).then_inc(consts, 1)
            g.iota(group_no, pattern=[[1, G]], base=0, channel_multiplier=0,
                   allow_small_or_imprecise_dtypes=True).then_inc(consts, 1)
            g.iota(chunk_no, pattern=[[1, CH]], base=0, channel_multiplier=0,
                   allow_small_or_imprecise_dtypes=True).then_inc(consts, 1)
            g.memset(ident[:, :], 0.0).then_inc(g_step, 1)
            g.memset(before, 1.0).then_inc(g_step, 1)
            g.memset(ones_m, 1.0).then_inc(consts, 1)
            pool.wait_ge(g_step, 2)
            g.affine_select(out=ident[:, :], in_=ident[:, :], compare_op=ALU.not_equal, fill=1.0, base=0,
                            pattern=[[-1, P]], channel_multiplier=1).then_inc(consts, 1)
            g.affine_select(out=before, in_=before, compare_op=ALU.is_gt, fill=0.0, base=0,
                            pattern=[[1, T]], channel_multiplier=-1).then_inc(consts, 1)
            g.memset(keep[:, :, :], 1.0).then_inc(g_step, 1)
            pool.wait_ge(g_step, 3)
            g.memset(keep[:, :, 0:1], 0.0).then_inc(keep_ready, 1)
            for i in range(BY_POOL):
                split_rest(pool, g, i, i % 2)
            pool.wait_ge(slots_ready, 1)
            pool.wait_ge(rows_ready, 1)
            pool.wait_ge(attr_in, 16)
            pool.wait_ge(cleared, 16 * PIECES)
            for c in range(EC):
                g.indirect_dma_start(out=table, out_offset=bass.IndirectOffsetOnAxis(ap=pos_i[:, c:c + 1], axis=0),
                                     in_=rows[:, c, :], in_offset=None).then_inc(scattered, 16)

        def pool_l0(pool):
            g = nc.gpsimd
            pool.wait_ge(tallied, 1)
            g.memset(here[:, :, :].bitcast(F32), 0.0).then_inc(here_added, 1)
            g.memset(pairs[0:T, :], 0.0).then_inc(zeroed, 1)

        def transposes(tile):
            for b in range(KD * NT):
                k, t = divmod(b, NT)
                mm = nc.tensor.transpose(PS[:, b // 4, b % 4 * T:(b % 4 + 1) * T], tile[0:T, t, k * P:(k + 1) * P], identT)
                if b % 4 == 3:
                    mm.then_inc(xt_psum, 1)

        def pe_sort(pe):
            pe.wait_ge(consts, 6)
            pe.wait_ge(x_in, 16)
            transposes(xN)
            pe.wait_ge(x_split, 1)
            multiply(pe, 0, 0, first=True)
            pe.wait_ge(ranked, 1)
            nc.tensor.matmul(PS[0:T, 7, 0:G], before, cnt[0:T, :], start=True, stop=True)
            nc.tensor.matmul(PS[:, 7, G:2 * G], ones_m, cnt[0:T, :], start=True, stop=True).then_inc(prefixed, 1)
            with pe.Fori(0, R) as pair:
                for j in range(2):
                    multiply(pe, pair * 2 + 1 + j, 1 - j)
            pe.wait_ge(product_out, emptied(PRODUCTS - 1, NT - 1))

        def bank_of(j, t):
            return 2 * j + t if t < 2 else t + 2

        def emptied(i, t):
            return i * NT + t + 1 + NT

        def multiply(pe, i, j, first=False):
            for k in range(KD):
                pe.wait_ge(mat_lo_ready, i * KD + k + 1)
                for t in range(NT):
                    if k == 0 and not first:
                        pe.wait_ge(product_out, emptied(i - 2 if t < 2 else i - 1, t))
                    at = k * N + t * T
                    for n, (a, b) in enumerate(((x_hi, mat_hi), (x_hi, mat_lo), (x_lo, mat_hi))):
                        mm = nc.tensor.matmul(PS[0:T, bank_of(j, t), :], a[:, at:at + T], b[:, k, :],
                                              start=(k == 0 and n == 0), stop=(k == KD - 1 and n == 2))
                    if k == KD - 1:
                        mm.then_inc(product_psum, 1)
                    elif t == NT - 1:
                        mm.then_inc(mat_used, 1)

        def pe_count(pe):
            mm = nc.tensor.matmul
            pe.sem_inc(chunk_done, CREDIT)
            with pe.Fori(0, NT) as t:
                for r in range(R):
                    bank = r % 2 * 2
                    pe.wait_ge(counts_out, t * R + r + 1)
                    for i in range(GC):
                        c = r * GC + i
                        pe.wait_ge(hot_made, t * TC + c + 1)
                        for at, n in HALVES_P:
                            mm(PS[0:T, bank + at // 512, 0:n], hot_dst[:, c % 4, 0:T], hot_src[:, c % 4, at:at + n],
                               start=(i == 0), stop=(i == GC - 1))
                        pe.wait_ge(hot_scaled, t * TC + c + 1)
                        if c == 0:
                            pe.wait_ge(weights_out, t + 1)
                        for part in (hot_hi, hot_lo):
                            for at, n in HALVES_P:
                                ins = mm(PS[0:T, 4 + at // 512, 0:n], part[:, c % 4, 0:T], hot_src[:, c % 4, at:at + n],
                                         start=(c == 0 and part is hot_hi), stop=(c == TC - 1 and part is hot_lo))
                        ins.then_inc(chunk_done, 1)

        def pe_count_packed(pe):
            mm = nc.tensor.matmul
            pe.sem_inc(counted, CREDIT)
            with pe.Fori(0, CH // 2) as step:
                for j in range(2):
                    c = step * 2 + j
                    pe.wait_ge(onehots, done(c))
                    pe.wait_ge(added, done(c - 2))
                    for at, n in HALVES_P:
                        mm(PS[0:T, 2 * j + at // 512, 0:n], hot_dst[:, j, 0:T], hot_src[:, j, at:at + n],
                           start=True, stop=True)
                    for part in (hot_hi, hot_lo):
                        for at, n in HALVES_P:
                            ins = mm(PS[0:T, 4 + 2 * j + at // 512, 0:n], part[:, j, 0:T], hot_src[:, j, at:at + n],
                                     start=(part is hot_hi), stop=(part is hot_lo))
                    ins.then_inc(counted, 1)

        def pe_l0(pe):
            t_ = nc.tensor
            pe.wait_ge(tallied, 1)
            for t in range(NT):
                pe.wait_ge(h_split[1], t + 1)
                for part in (h_hi[1], h_lo[1]):
                    mm = t_.matmul(PS[0:T, t, :], ident_r[0:T, 0:T], part[:, t, :],
                                   start=(part is h_hi[1]), stop=False, skip_group_check=True)
            mm.then_inc(h_used[1], 1)

            def relations(first):
                with pe.Fori(0, R) as r:
                    q = first + r
                    pe.wait_ge(here_ready, q + 1)
                    block_ = 0
                    for u, n in enumerate(TURNS):
                        if u >= 3:
                            if u % 2:
                                pe.wait_ge(out_act, q * 4 + (u - 3) // 2 + 1)
                            else:
                                pe.wait_ge(out_dve, q * 3 + (u - 3) // 2 + 1)
                        for i in range(n):
                            st, t = divmod(block_, NT)
                            block_ += 1
                            mm = t_.transpose(PS[0:T, 5 + u % 3, i * T2:(i + 1) * T2].bitcast(FR),
                                              here[0:T2, t, st * T:(st + 1) * T], ident_r[0:T2, 0:T2])
                        mm.then_inc(scratch, 1)
                    for side in range(2):
                        if side == 1:
                            pe.wait_ge(out_act, q * 4 + 4)
                            pe.wait_ge(out_dve, q * 3 + 3)
                        for k in range(NT):
                            pe.wait_ge(h_split[side], (q + 1) * NT + k + 1)
                            for t in range(NT):
                                edges = here[0:T, k, t * T:(t + 1) * T] if side == 0 else turned[0:T, k, t, 0:T]
                                for part in (h_hi[side], h_lo[side]):
                                    mm = t_.matmul(PS[0:T, t, :], edges, part[:, k, :], start=False,
                                                   stop=(k == NT - 1 and part is h_lo[side]), skip_group_check=True)
                        mm.then_inc(h_used[side], 1)
                pe.wait_ge(h_used[1], first + R + 1)

            relations(0)
            is_packed = pe.value_load(packed[0:1, 0:1], min_val=0, max_val=1)
            with pe.If(is_packed):
                relations(R)
            pe.sem_inc(acc_done, 1)

        def act_turn(act, turn, to):
            for b in range(NT):
                act.wait_ge(xt_psum, NT * turn + b + 1)
                nc.scalar.copy(to[:, b * 4 * T:(b + 1) * 4 * T], PS[:, b, 0:4 * T]).then_inc(xt_ready, 1)

        def act_deviation(act, turn):
            act.wait_ge(var_ready, turn + 1)
            nc.scalar.activation(sd[0:T, :], rstd[0:T, :], ACT.Sqrt).then_inc(sd_ready, 1)

        def act_products(act):
            for b in range(NT):
                act.wait_ge(xt_psum, b + 1)
                nc.scalar.copy(x_hi[:, b * 4 * T:(b + 1) * 4 * T], PS[:, b, 0:4 * T]).then_inc(xt_ready, 1)

            def out_(i, j):
                for t in range(NT):
                    act.wait_ge(product_psum, i * NT + t + 1)
                    if t == 0:
                        act.wait_ge(product_stored, i * 16 + 16)
                    nc.scalar.copy(product[:, t, :], PS[0:T, bank_of(j, t), :]).then_inc(product_out, 1)

            def parts(i, j, ks):
                for k in ks:
                    if k == 0:
                        act.wait_ge(mat_in[j], (i - j) * 8 + 16)
                    if k < KD - 1:
                        act.wait_ge(mat_used, (i - 1) * (KD - 1) + k + 1)
                    else:
                        act.wait_ge(product_psum, i * NT)
                    nc.scalar.copy(mat_hi[:, k, :], mat[j][:, k, :]).then_inc(mat_hi_ready, 1)

            act.sem_inc(product_out, NT)
            act.sem_inc(product_stored, 16)
            act.wait_ge(mat_in[0], 16)
            for k in range(KD):
                nc.scalar.copy(mat_hi[:, k, :], mat[0][:, k, :]).then_inc(mat_hi_ready, 1)
            with act.Fori(0, R) as pair:
                for j in range(2):
                    i = pair * 2 + j
                    parts(i + 1, 1 - j, (0, 1, 2))
                    out_(i, j)
                    parts(i + 1, 1 - j, (3,))
            out_(PRODUCTS - 1, 0)

        def act_count(act):
            act.sem_inc(counts_out, 2)
            w_hi_f = w_hi[:, :].bitcast(F32)
            with act.Fori(0, NT) as t:
                def counts_to_sbuf(r):
                    act.wait_ge(chunk_done, done(t * TC + (r + 1) * GC - 1))
                    nc.scalar.copy(counts[0:T, ds((t * R + r) * N, N)], two_banks(r % 2 * 2, T)).then_inc(counts_out, 1)

                act.wait_ge(weights_ready, t + 1)
                for i in range(TC):
                    c = t * TC + i
                    act.wait_ge(hot_made, c + 1)
                    act.wait_ge(chunk_done, done(c - 4))
                    for part, w in ((hot_hi, w_hi_f), (hot_lo, w_lo)):
                        ins = nc.scalar.activation(part[:, i % 4, 0:T], hot_dst[:, i % 4, 0:T].bitcast(F32), ACT.Copy,
                                                   scale=w[:, ds(c, 1)])
                    ins.then_inc(hot_scaled, 1)
                    if i % GC == 2 and i > GC:
                        counts_to_sbuf(i // GC - 1)
                counts_to_sbuf(R - 1)

        def act_l0(act):
            def rounded(side, q):
                if side == 0:
                    act.wait_ge(h_used[0], q + 1)
                for t in range(NT):
                    act.wait_ge(h_biased[side], q * NT + t + 1)
                    nc.scalar.copy(h_hi[side][:, t, :], h[side][:, t, :]).then_inc(h_hi_ready[side], 1)

            def stage(q, r, rest):
                act.wait_ge(h_used[0], q + 1)
                act.wait_ge(here_added, q + 1)
                by_rel = counts[0:T, :].rearrange("p (t r n) -> p t r n", t=NT, r=R)
                nc.scalar.copy(here[0:T, :, :], by_rel[:, :, ds(r, 1), :].rearrange("p t a n -> p t (a n)")
                               ).then_inc(here_rounded if rest else here_ready, 1)

            def turn(q, r, rest, more):
                for u in range(0, 7, 2):
                    act.wait_ge(scratch, q * 7 + u + 1)
                    if u == 0:
                        act.wait_ge(h_used[1], q + 1)
                    nc.scalar.copy(turned_blocks(u), PS[0:T, 5 + u % 3, 0:TURNS[u] * T2]).then_inc(out_act, 1)
                rounded(1, q + 1)
                if more:
                    stage(q + 1, r + 1, rest)
                    rounded(0, q + 1)

            def relations(first, rest):
                stage(first, 0, rest)
                rounded(0, first)
                with act.Fori(0, R - 1) as r:
                    turn(first + r, r, rest, True)
                turn(first + R - 1, R - 1, rest, False)

            act.wait_ge(tallied, 1)
            act.sem_inc(h_used[0], 1)
            rounded(1, 0)
            relations(0, False)
            is_packed = act.value_load(packed[0:1, 0:1], min_val=0, max_val=1)
            with act.If(is_packed):
                relations(R, True)
            act.wait_ge(clipped, 1)
            nc.scalar.activation(ln_pairs, ln_pairs, ACT.Ln).then_inc(logs_ready, 1)
            act_deviation(act, 0)

        def turned_blocks(u):
            at = sum(TURNS[:u])
            return turned[0:T, :, :, :].rearrange("p s t n -> p (s t n)")[:, at * T2:(at + TURNS[u]) * T2]

        v_steps = [0]

        def link(dve, ins):
            v_steps[0] += 1
            ins.then_inc(v_step, 1)
            dve.wait_ge(v_step, v_steps[0])

        def dve_sort(dve):
            v = nc.vector

            def step(ins):
                link(dve, ins)

            v.memset(pad, 0.0).then_inc(v_step, 1)
            v_steps[0] += 1
            dve.wait_ge(v_step, v_steps[0])
            v.memset(pad[:, :, DSTL:DSTL + 1], -1.0).then_inc(pad_ready, 1)
            step(v.memset(ones_g, 1.0))
            dve.wait_ge(edges_in, 64)
            v.tensor_copy(src_f, src_i)
            v.tensor_copy(dst_f, dst_i)
            step(v.tensor_copy(typ_f, typ_i))
            step(v.tensor_scalar(tile, dst_f, float(T), None, ALU.is_ge))
            for t in range(2, NT):
                step(v.scalar_tensor_tensor(out=tile, in0=dst_f, scalar=float(t * T), in1=tile, op0=ALU.is_ge, op1=ALU.add))
            step(v.scalar_tensor_tensor(out=key, in0=tile, scalar=float(R), in1=typ_f, op0=ALU.mult, op1=ALU.add))
            step(v.scalar_tensor_tensor(out=dst_l, in0=tile, scalar=-float(T), in1=dst_f, op0=ALU.mult, op1=ALU.add))
            dve.wait_ge(consts, 6)
            step(v.tensor_tensor(hot[:, :, :], key.unsqueeze(1).broadcast_to([T, G, EC]),
                                 group_no[0:T, :].unsqueeze(2).broadcast_to([T, G, EC]), ALU.is_equal))
            dve.wait_ge(xt_ready, NT)
            for b in range(NT):
                at = slice(b * 4 * T, (b + 1) * 4 * T)
                ins = v.tensor_tensor(x_lo[:, at], PS[:, b, 0:4 * T], x_hi[:, at].bitcast(F32), ALU.subtract)
            ins.then_inc(x_split, 1)
            dve.wait_ge(keep_ready, 1)
            step(v.tensor_tensor_scan(rank.rearrange("p g c -> p (g c)"), keep[:, :, :].rearrange("p g c -> p (g c)"),
                                      hot[:, :, :].rearrange("p g c -> p (g c)"), 0.0, ALU.mult, ALU.add))
            v.tensor_copy(cnt[0:T, :], rank[:, :, EC - 1:EC].rearrange("p g a -> p (g a)")).then_inc(ranked, 1)
            for col, what in ((SRC, src_f), (DSTL, dst_l), (WGT, wgt)):
                v.tensor_copy(rows[:, :, col:col + 1], what.unsqueeze(2))
            v.tensor_copy(rows[:, :, SRCI:SRCI + 1].bitcast(I32), src_i.unsqueeze(2)).then_inc(rows_ready, 1)
            dve.wait_ge(prefixed, 1)
            step(v.tensor_scalar(chunks_f, PS[:, 7, G:2 * G], float(P - 1), None, ALU.add))
            step(v.tensor_copy(chunks_i, chunks_f))
            step(v.tensor_scalar(chunks_i, chunks_i, 7, None, ALU.arith_shift_right))
            step(v.tensor_copy(chunks_f, chunks_i))
            step(v.tensor_tensor_scan(upto, ones_g, chunks_f, 0.0, ALU.mult, ALU.add))
            step(v.tensor_tensor(start, upto, chunks_f, ALU.subtract))
            step(v.tensor_reduce(crowded, PS[:, 7, G:2 * G], X, ALU.max))
            step(v.tensor_scalar(crowded, crowded, float(GC * P), None, ALU.is_gt))
            v.tensor_copy(packed[:, :], crowded[0:1, :])
            v.tensor_scalar(slots_f, group_no, float(GC * P), None, ALU.mult)
            step(v.tensor_scalar(start, start, float(P), None, ALU.mult))
            step(v.tensor_tensor(start, start, slots_f, ALU.subtract))
            step(v.scalar_tensor_tensor(out=start, in0=start, scalar=crowded, in1=slots_f, op0=ALU.mult, op1=ALU.add))
            step(v.tensor_tensor(base[0:T, :], start[0:T, :], PS[0:T, 7, 0:G], ALU.add))
            step(v.tensor_scalar(base[0:T, :], base[0:T, :], -1.0, None, ALU.add))
            step(v.tensor_tensor(rank, rank, base[0:T, :].unsqueeze(2).broadcast_to([T, G, EC]), ALU.add))
            step(v.tensor_tensor(rank, rank, hot[:, :, :], ALU.mult))
            step(v.tensor_reduce(slot_f, rank.rearrange("p g c -> p c g"), X, ALU.add))
            step(v.tensor_copy(slot_i, slot_f))
            v.tensor_scalar(lo_i, slot_i, P - 1, None, ALU.bitwise_and)
            step(v.tensor_scalar(hi_i, slot_i, 7, None, ALU.arith_shift_right))
            v.tensor_copy(hi_f, hi_i)
            step(v.tensor_copy(lo_f, lo_i))
            step(v.scalar_tensor_tensor(out=slot_f, in0=lo_f, scalar=float(CHX), in1=hi_f, op0=ALU.mult, op1=ALU.add))
            v.tensor_copy(pos_i, slot_f).then_inc(slots_ready, 1)
            dve.sem_inc(plan_ready, 1)
            dve.wait_ge(product_psum, NT * (BY_POOL - 1) + 1)
            with dve.Fori(0, (PRODUCTS - BY_POOL) // 2) as pair:
                for j in range(2):
                    split_rest(dve, v, pair * 2 + BY_POOL + j, (BY_POOL + j) % 2)

        def dve_count_start(dve):
            v = nc.vector
            dve.wait_ge(cleared, 16 * PIECES)
            v.memset(wadj[0:T, :], 0.0)
            v.tensor_copy(ident_r[:, :], ident[:, :])
            dve.sem_inc(sorted_in, 16)

        def split_weights(dve, t):
            v = nc.vector
            dve.wait_ge(sorted_in, t * 16 + 32)
            at = ds(t * TC, TC)
            weight = sorted_rows[:, at, WGT:WGT + 1].rearrange("p c a -> p (c a)")
            v.tensor_copy(w_hi[:, at], weight).then_inc(weights_rounded, 1)
            dve.wait_ge(weights_rounded, t + 1)
            v.tensor_tensor(w_lo[:, at], weight, w_hi[:, at].bitcast(F32), ALU.subtract).then_inc(weights_ready, 1)
            dve.wait_ge(weights_ready, t + 1)

        def column(c, n):
            return sorted_rows[:, ds(c, 1), n:n + 1].rearrange("p a b -> p (a b)")

        def dve_count(dve):
            v = nc.vector
            dve.sem_inc(weights_out, 1)
            with dve.Fori(0, NT) as t:
                split_weights(dve, t)
                for i in range(TC):
                    c = t * TC + i
                    dve.wait_ge(chunk_done, done(c - 4))
                    v.tensor_scalar(hot_dst[:, i % 4, 0:T], node_f[:, 0:T], column(c, DSTL), None, ALU.is_equal)
                    v.tensor_scalar(hot_src[:, i % 4, :], node_f[:, :], column(c, SRC), None,
                                    ALU.is_equal).then_inc(hot_made, 1)
                dve.wait_ge(chunk_done, done(t * TC + TC - 1))
                v.tensor_copy(wadj[0:T, ds(t * N, N)], two_banks(4, T)).then_inc(weights_out, 1)
            dve.wait_ge(weights_out, 1 + NT)
            dve.wait_ge(counts_out, 2 + G)

        def dve_count_packed(dve):
            v = nc.vector
            plan = [0]

            def step(ins):
                plan[0] += 1
                ins.then_inc(plan_step, 1)
                dve.wait_ge(plan_step, plan[0])

            with dve.Fori(0, NT) as t:
                split_weights(dve, t)
            step(v.tensor_tensor(past, upto[0:1, :].unsqueeze(1).broadcast_to([1, CH, G]),
                                 chunk_no.unsqueeze(2).broadcast_to([1, CH, G]), ALU.is_le))
            step(v.tensor_reduce(group_f, past, X, ALU.add))
            step(v.tensor_scalar(group_f, group_f, float(G - 1), None, ALU.min))
            step(v.tensor_copy(group[:, :], group_f))
            step(v.tensor_scalar(tile_of[:, :], group[:, :], 3, None, ALU.arith_shift_right))
            step(v.memset(counts[0:T, :], 0))
            dve.sem_inc(onehots, CREDIT)
            dve.sem_inc(added, CREDIT)

            def one_hots(c, j):
                v.tensor_scalar(hot_dst[:, j, 0:T], node_f[:, 0:T], column(c, DSTL), None, ALU.is_equal)
                v.tensor_scalar(hot_src[:, j, :], node_f[:, :], column(c, SRC), None, ALU.is_equal)
                for part, w in ((hot_hi, w_hi[:, :].bitcast(F32)), (hot_lo, w_lo)):
                    ins = v.tensor_scalar(part[:, j, 0:T], node_f[:, 0:T], column(c, DSTL), w[:, ds(c, 1)],
                                          ALU.is_equal, ALU.mult)
                ins.then_inc(onehots, 1)

            def add(c, j):
                g = dve.value_load(group[0:1, ds(c, 1)], min_val=0, max_val=G - 1)
                t = dve.value_load(tile_of[0:1, ds(c, 1)], min_val=0, max_val=NT - 1)
                dve.wait_ge(counted, done(c))
                dve.wait_ge(added, done(c - 1))
                to = counts[0:T, ds(g * N, N)]
                v.tensor_tensor(to, two_banks(2 * j, T), to, ALU.add)
                to = wadj[0:T, ds(t * N, N)]
                v.tensor_tensor(to, two_banks(4 + 2 * j, T), to, ALU.add).then_inc(added, 1)

            one_hots(0, 0)
            with dve.Fori(0, CH // 2 - 1) as s_:
                for j in range(2):
                    one_hots(s_ * 2 + j + 1, 1 - j)
                    add(s_ * 2 + j, j)
            one_hots(CH - 1, 1)
            add(CH - 2, 0)
            add(CH - 1, 1)
            dve.wait_ge(added, done(CH - 1))

        def dve_norm(dve, turn, scale_row=None, shift_row=None, enc_tiles=None, store=False, stats=None):
            v = nc.vector
            if stats is None:
                for t in range(NT):
                    stats = v.bn_stats(stat[0:T, t, :], xN[0:T, t, :])
            link(dve, stats)
            for t in range(NT):
                ins = v.bn_aggr(mv[0:T, t, :], stat[0:T, t, :])
            link(dve, ins)
            v.tensor_scalar(rstd[0:T, :], mv[0:T, :, 1:2].rearrange("p t a -> p (t a)"), EPS, None,
                            ALU.add).then_inc(var_ready, 1)
            if scale_row is not None:
                for t in range(NT):
                    ins = v.scalar_tensor_tensor(out=xN[0:T, t, :], in0=xN[0:T, t, :], scalar=mv[0:T, t, 0:1],
                                                 in1=scale_row[0:T, :], op0=ALU.subtract, op1=ALU.mult)
                link(dve, ins)
            dve.wait_ge(sd_ready, turn + 1)
            link(dve, v.reciprocal(rstd[0:T, :], sd[0:T, :]))
            for t in range(NT):
                if scale_row is not None:
                    shift = enc_tiles[:, t, :] if shift_row is None else shift_row[0:T, :]
                    ins = v.scalar_tensor_tensor(out=xN[0:T, t, :], in0=xN[0:T, t, :], scalar=rstd[0:T, t:t + 1],
                                                 in1=shift, op0=ALU.mult, op1=ALU.add)
                else:
                    ins = v.tensor_scalar(xN[0:T, t, :], xN[0:T, t, :], mv[0:T, t, 0:1], rstd[0:T, t:t + 1],
                                          ALU.subtract, ALU.mult)
                if store:
                    ins.then_inc(tile_normed, 1)
            if not store:
                ins.then_inc(x_ready, 1)
                dve.wait_ge(x_ready, turn + 1)

        def over_tiles(row):
            return row[0:T, :].unsqueeze(1).broadcast_to([T, NT, D])

        def dve_l0(dve):
            v = nc.vector
            step = [0]

            def split(side, q):
                dve.wait_ge(h_in[side], q * 32 + 32)
                for t in range(NT):
                    v.tensor_tensor(h[side][:, t, :], h[side][:, t, :], h_bias[side], ALU.add).then_inc(h_biased[side], 1)
                for t in range(NT):
                    dve.wait_ge(h_hi_ready[side], q * NT + t + 1)
                    v.tensor_tensor(h_lo[side][:, t, :], h[side][:, t, :], h_hi[side][:, t, :].bitcast(F32),
                                    ALU.subtract).then_inc(h_split[side], 1)

            def add_here(q, r, rest):
                if rest:
                    dve.wait_ge(here_rounded, r + 1)
                    by_rel = counts[0:T, :].rearrange("p (t r n) -> p t r n", t=NT, r=R)
                    v.tensor_tensor(here[0:T, :, :], by_rel[:, :, ds(r, 1), :].rearrange("p t a n -> p t (a n)"),
                                    here[0:T, :, :].bitcast(F32), ALU.subtract).then_inc(here_ready, 1)
                dve.wait_ge(here_ready, q + 1)
                v.tensor_tensor(pairs_t, pairs_t, here[0:T, :, :].bitcast(F32), ALU.add).then_inc(here_added, 1)

            def turn(q, r, rest, more):
                for u in range(1, 7, 2):
                    dve.wait_ge(scratch, q * 7 + u + 1)
                    if u == 1:
                        dve.wait_ge(h_used[1], q + 1)
                    v.tensor_copy(turned_blocks(u), PS[0:T, 5 + u % 3, 0:TURNS[u] * T2]).then_inc(out_dve, 1)
                split(1, q + 1)
                if more:
                    add_here(q + 1, r + 1, rest)
                    split(0, q + 1)

            def relations(first, rest):
                if rest:
                    add_here(first, 0, rest)
                split(0, first)
                if not rest:
                    add_here(first, 0, rest)
                with dve.Fori(0, R - 1) as r:
                    turn(first + r, r, rest, True)
                turn(first + R - 1, R - 1, rest, False)

            split(1, 0)
            dve.wait_ge(zeroed, 1)
            relations(0, False)
            is_packed = dve.value_load(packed[0:1, 0:1], min_val=0, max_val=1)
            with dve.If(is_packed):
                relations(R, True)
            dve.wait_ge(here_added, R + 1)
            link(dve, v.tensor_reduce(has_in[0:T, :], pairs_t, X, ALU.max))
            v.tensor_scalar(has_in[0:T, :], has_in[0:T, :], 1.0, None, ALU.min)
            link(dve, v.tensor_scalar(ln_pairs, pairs[0:T, :], 1.0, None, ALU.max))
            v.tensor_scalar(pairs[0:T, :], pairs[0:T, :], 0.0, FAR, ALU.is_equal, ALU.mult).then_inc(clipped, 1)
            dve.wait_ge(logs_ready, 1)
            dve.wait_ge(clipped, 1)
            v.scalar_tensor_tensor(out=pairs[0:T, :], in0=ln_pairs, scalar=float(HD) ** 0.5, in1=pairs[0:T, :],
                                   op0=ALU.mult, op1=ALU.add)
            dve.wait_ge(acc_done, 1)
            for t in range(NT):
                ins = v.scalar_tensor_tensor(out=xN[0:T, t, :], in0=PS[0:T, t, :], scalar=0.0, in1=xN[0:T, t, :],
                                             op0=ALU.max, op1=ALU.add)
            link(dve, ins)
            dve_norm(dve, 0)

        def sync_l1(sp):
            sp.wait_ge(acc_done, 1)
            sp.dma_start(u_w, p1["U"]).then_inc(p1_in, 16)
            sp.dma_start(vt_w, p1["Vt"]).then_inc(p1_in, 16)
            load_rows(sp, s_row, p1["s"], p1_in, T)
            load_rows(sp, b1_row, p1["bias"], p1_in, T)
            load_rows(sp, be_row, p2["b_e"], p1_in, T)

        def pe_l1(pe):
            t_ = nc.tensor
            pe.wait_ge(x_ready, 1)
            transposes(xN)
            pe.wait_ge(xt_ready, 2 * NT)
            pe.wait_ge(p1_in, 16 * 5)
            for t in range(NT):
                for k in range(KD):
                    mm = t_.matmul(PS[0:T, 5, t * RANK:(t + 1) * RANK], xTk[:, k, t * T:(t + 1) * T], u_w[:, k, :],
                                   start=(k == 0), stop=(k == KD - 1))
            mm.then_inc(support_psum, 1)
            pe.wait_ge(support_ready, 1)
            for h, (at, n) in enumerate(HALVES):
                for t in range(NT):
                    mm = t_.matmul(PS[0:RANK, 6 + h, 0:n], support[:, t, :], wadj_t[:, t, at:at + n],
                                   start=(t == 0), stop=(t == NT - 1))
            mm.then_inc(mixed_psum, 1)
            pe.wait_ge(mixed_ready, 1)
            for t in range(NT):
                t_.matmul(PS[0:T, t, :], mixed[:, t * T:(t + 1) * T], vt_w, start=True, stop=True).then_inc(l1_psum, 1)

        def act_l1(act):
            act_turn(act, 1, xT)
            act.wait_ge(mixed_psum, 1)
            for h, (at, n) in enumerate(HALVES):
                ins = nc.scalar.copy(mixed[:, at:at + n], PS[0:RANK, 6 + h, 0:n])
            ins.then_inc(mixed_ready, 1)
            act_deviation(act, 1)

        def dve_l1(dve):
            v = nc.vector
            dve.wait_ge(p1_in, 16 * 5)
            dve.wait_ge(support_psum, 1)
            v.tensor_tensor(support, PS[0:T, 5, 0:NT * RANK].rearrange("p (t n) -> p t n", n=RANK),
                            s_row.unsqueeze(1).broadcast_to([T, NT, RANK]), ALU.mult).then_inc(support_ready, 1)
            v.memset(zero_w, 0.0)
            dve.wait_ge(w_e_in, 32)
            link(dve, v.tensor_copy(w_e_hi[:, :], w_e))
            link(dve, v.memset(w_e_lo[:, :].bitcast(F32), 0.0))
            v.tensor_tensor(w_e_lo[0:EA, :], w_e[0:EA, :], w_e_hi[0:EA, :].bitcast(F32), ALU.subtract).then_inc(w_e_ready, 1)
            for t in range(NT):
                dve.wait_ge(l1_psum, t + 1)
                ins = v.tensor_tensor(sums[:, t, :], PS[0:T, t, :], b1_row, ALU.add)
            link(dve, ins)
            for t in range(NT):
                ins = v.scalar_tensor_tensor(out=xN[0:T, t, :], in0=sums[:, t, :], scalar=0.0, in1=xN[0:T, t, :],
                                             op0=ALU.max, op1=ALU.add)
            link(dve, ins)
            dve_norm(dve, 1)
            for t in range(NT):
                v.tensor_tensor(xb[:, t, :], xN[0:T, t, :], be_row, ALU.add).then_inc(xb_ready, 1)

        def sync_l2(sp):
            for half in range(2):
                sp.dma_start(w_e[half * EA:(half + 1) * EA, :], p2["W_e"]).then_inc(w_e_in, 16)
            for to, what in ((w1, "W1"), (w2, "W2"), (b1_c, "b1"), (g1_c, "g1"), (beta1_c, "beta1"),
                             (b2_c[:, 0:KD], "b2"), (g2_c[:, 0:KD], "g2"), (beta2_c[:, 0:KD], "beta2")):
                sp.dma_start(to, p2[what]).then_inc(p2_in, 16)
            load_rows(sp, eps_c, p2["eps"], p2_in, T)
            for t in range(NT):
                sp.wait_ge(xb_ready, t + 1)
                sp.dma_start(xb_rows[t * T:(t + 1) * T, :], xb[:, t, :]).then_inc(xb_stored, 16)
            def load_pair(c, pair):
                sp.wait_ge(attr_lo, done(c - 7))
                sp.wait_ge(hot_ready, done(c - 7))
                sp.wait_ge(msg_sum, done(c - 7))
                sp.dma_start(row_buf[:, 2 * pair:2 * pair + 2, :].rearrange("p c e -> p (c e)"),
                             table_p[:, ds(c * ROW, 2 * ROW)]).then_inc(rows_in[pair], 16)

            with sp.Fori(0, CH // STEP) as step:
                for pair in range(STEP // 2):
                    load_pair(step * STEP + 2 * pair, pair)
            for pair in range(3):
                load_pair(CH + 2 * pair, pair)

        def rows_there(eng, c, j):
            eng.wait_ge(rows_in[j // 2], (c - j) * (16 // STEP) + 16)

        def pool_l2(pool):
            g = nc.gpsimd
            pool.wait_ge(xb_stored, 16 * NT)

            def gather(c, j):
                rows_there(pool, c, j)
                pool.wait_ge(msg_sum, done(c - STEP))
                pool.sem_inc(pool_tick, 1)
                g.indirect_dma_start(out=x_src[:, j, :], out_offset=None, in_=xb_rows,
                                     in_offset=bass.IndirectOffsetOnAxis(
                                         ap=row_buf[:, j, SRCI:SRCI + 1].bitcast(I32), axis=0)
                                     ).then_inc(src_in[j], 16)

            with pool.Fori(0, CH // STEP) as step:
                for j in range(STEP):
                    gather(step * STEP + j, j)
            for j in range(AHEAD):
                gather(CH + j, j)

        def pool_l3(pool):
            g = nc.gpsimd
            pool.wait_ge(h_ready, 1)
            pool.wait_ge(msg_ready, done(CH + AHEAD - 1))
            g.memset(val, 0.0).then_inc(val_zeroed, 1)
            pool.wait_ge(val_zeroed, 1)
            g.memset(q_t[1][0:HD, :, :], 0.0).then_inc(q_zeroed, 1)
            pool.wait_ge(q_zeroed, 1)
            pool.wait_ge(back_psum, NT)
            g.memset(q_t[0][HD:P, :, :], 0.0).then_inc(q_zeroed, 1)

        def edge_bank(j):
            return (2, 3, 6, 7)[j % 4]

        def pe_l2(pe):
            t_ = nc.tensor
            pe.sem_inc(attr_psum, CREDIT)
            pe.sem_inc(edge_psum, CREDIT)
            pe.sem_inc(agg_psum, CREDIT)
            pe.wait_ge(p2_in, 16 * 9)
            pe.wait_ge(x_ready, 2)

            def turn_attr(c, j):
                pe.wait_ge(attr_lo, done(c - j % 2 + 1))
                pe.wait_ge(attr_out, done(c - 2))
                t_.transpose(PS[:, j % 2, 0:P].bitcast(FR), attr2[:, j % 4, :], ident_r[:, :]).then_inc(attr_psum, 1)

            def edge_product(c, j):
                pe.wait_ge(attr_out, done(c))
                pe.wait_ge(msg_sum, done(c - 4))
                t_.matmul(PS[:, edge_bank(j), :], attr_t[:, j % 4, :], w_e_hi[:, :], start=True, stop=False)
                t_.matmul(PS[:, edge_bank(j), :], attr_t[:, j % 4, :], w_e_lo[:, :], start=False, stop=True
                          ).then_inc(edge_psum, 1)

            def sum_messages(c, j, bank, alone):
                pe.wait_ge(hot_ready, done(c))
                if j % 2 == 0:
                    pe.wait_ge(msg_ready, done(c))
                    ins = t_.matmul(PS[0:T, bank, :], hot_dst2[:, j % 4, 0:T].bitcast(F32), msg[:, j // 2 % 2, :],
                                    start=alone, stop=alone, skip_group_check=True)
                else:
                    pe.wait_ge(msg_split, done(c))
                    for part in (msg_hi, msg_lo):
                        ins = t_.matmul(PS[0:T, bank, :], hot_dst2[:, j % 4, 0:T], part[:, j // 2 % 2, :],
                                        start=alone and part is msg_hi, stop=alone and part is msg_lo,
                                        skip_group_check=True)
                ins.then_inc(agg_psum, 1)

            def sum_by_dst(c, j):
                pe.wait_ge(agg_added, done(c - 2))
                sum_messages(c, j, 4 + j % 2, True)

            def sum_in_tile(c, j):
                sum_messages(c, j, 4, False)

            def zero_bank(first):
                return t_.matmul(PS[0:T, 4, :], zero_w, node_f[:, 0:D], start=first, stop=not first, skip_group_check=True)

            def steps(n, first, sum_):
                with pe.Fori(0, n) as step:
                    c0 = first + step * STEP
                    for j in range(STEP):
                        edge_product(c0 + j + AHEAD, (j + AHEAD) % STEP)
                        turn_attr(c0 + j + TURN_AHEAD, (j + TURN_AHEAD) % STEP)
                        sum_(c0 + j, j)

            pe.wait_ge(w_e_ready, 1)
            for c in range(TURN_AHEAD):
                turn_attr(c, c)
            for c in range(AHEAD):
                edge_product(c, c)
            is_packed = pe.value_load(packed[0:1, 0:1], min_val=0, max_val=1)
            with pe.If(is_packed):
                steps(CH // STEP, 0, sum_by_dst)
            with pe.Else():
                with pe.Fori(0, NT) as t:
                    pe.wait_ge(tile_added, t + 1)
                    zero_bank(True)
                    steps(TC // STEP, t * TC, sum_in_tile)
                    zero_bank(False).then_inc(tile_psum, 1)

            pe.wait_ge(attr_out, done(CH + TURN_AHEAD - 1))
            pe.wait_ge(h_ready, 1)
            transposes(agg)
            pe.wait_ge(xt_ready, 3 * NT)
            use = 0
            for m in range(2 * KD):
                for at, n in HALVES:
                    if use >= 8:
                        pe.wait_ge(z_out, use - 7)
                    for k in range(KD):
                        mm = t_.matmul(PS[:, use % 8, 0:n], w1[:, k, m * P:(m + 1) * P], h_tk[:, k, at:at + n],
                                       start=(k == 0), stop=(k == KD - 1))
                    mm.then_inc(z_psum, 1)
                    use += 1
            for m in range(KD):
                for at, n in HALVES:
                    pe.wait_ge(z_out, use - 7)
                    for k in range(2 * KD):
                        if m == 0 and at == 0:
                            pe.wait_ge(act_out, k + 1)
                        mm = t_.matmul(PS[:, use % 8, 0:n], w2[:, k, m * P:(m + 1) * P], z1[:, k, at:at + n],
                                       start=(k == 0), stop=(k == 2 * KD - 1))
                    mm.then_inc(z_psum, 1)
                    use += 1
            pe.wait_ge(z_out, use)
            pe.wait_ge(act_out, 3 * KD)
            for t in range(NT):
                for k in range(KD):
                    mm = t_.transpose(PS[0:T, t, k * P:(k + 1) * P], z2[:, k, t * T:(t + 1) * T], ident[:, :])
                mm.then_inc(back_psum, 1)

        def act_l2(act):
            act.sem_inc(attr_out, CREDIT)
            act.sem_inc(msg_ready, CREDIT)

            def round_attr(c, j):
                rows_there(act, c, j)
                act.wait_ge(attr_psum, done(c - 3))
                nc.scalar.copy(attr2[:, j % 4:j % 4 + 2, 0:EA], row_buf[:, j:j + 2, 0:EA]).then_inc(attr_hi, 2)

            def keep_attr(c, j):
                act.wait_ge(attr_psum, done(c))
                act.wait_ge(edge_psum, done(c - 4))
                nc.scalar.copy(attr_t[:, j % 4, :], PS[:, j % 2, 0:P]).then_inc(attr_out, 1)

            def relu(c, j):
                act.wait_ge(msg_sum, done(c))
                act.wait_ge(agg_psum, done(c - 4))
                nc.scalar.activation((msg_hi if j % 2 else msg)[:, j // 2 % 2, :], msg_in[:, j % 4, :],
                                     ACT.Relu).then_inc(msg_ready, 1)

            act.sem_inc(attr_hi, CREDIT)
            round_attr(0, 0)
            round_attr(2, 2)
            round_attr(4, 4)
            for c in range(TURN_AHEAD):
                keep_attr(c, c)
            for c in range(AHEAD):
                relu(c, c)
            with act.Fori(0, CH // STEP) as step:
                c0 = step * STEP
                for j in range(STEP):
                    keep_attr(c0 + j + TURN_AHEAD, (j + TURN_AHEAD) % STEP)
                    relu(c0 + j + AHEAD, (j + AHEAD) % STEP)
                    if j % 2 == 0:
                        round_attr(c0 + j + 6, (j + 6) % STEP)
            act_turn(act, 2, h_t)

            use = 0
            tiles = 0
            for phase, (z, bias, parts) in enumerate(((z1, b1_c, 2 * KD), (z2, b2_c, KD))):
                for m in range(parts):
                    for at, n in HALVES:
                        act.wait_ge(z_psum, use + 1)
                        nc.scalar.activation(z[:, m, at:at + n], PS[:, use % 8, 0:n], ACT.Identity,
                                             bias=bias[:, m:m + 1]).then_inc(z_out, 1)
                        use += 1
                act.wait_ge(bn_var, phase + 1)
                nc.scalar.activation(bn_sd[:, 0:parts], bn_ve[:, 0:parts], ACT.Sqrt).then_inc(bn_dev, 1)
                act.wait_ge(bn_ready, phase + 1)
                for m in range(parts):
                    nc.scalar.activation(z[:, m, :], z[:, m, :], ACT.Silu, bias=shift_c[:, m:m + 1],
                                         scale=scale_c[:, m:m + 1]).then_inc(act_out, 1)
            act_deviation(act, 2)

        def dve_l2(dve):
            v = nc.vector
            dve.sem_inc(msg_sum, CREDIT)
            dve.sem_inc(hot_ready, CREDIT)
            dve.sem_inc(agg_added, CREDIT)

            def rest_of_attr(c, j):
                dve.wait_ge(attr_hi, done(c + 1))
                v.tensor_tensor(attr2[:, j % 4:j % 4 + 2, EA:2 * EA], row_buf[:, j:j + 2, 0:EA],
                                attr2[:, j % 4:j % 4 + 2, 0:EA].bitcast(F32), ALU.subtract).then_inc(attr_lo, 2)

            def message(c, j):
                rows_there(dve, c, j)
                dve.wait_ge(agg_psum, done(c - 4))
                v.tensor_scalar(hot_dst2[:, j % 4, 0:T], node_f[:, 0:T], row_buf[:, j, DSTL:DSTL + 1], None,
                                ALU.is_equal).then_inc(hot_ready, 1)
                dve.wait_ge(edge_psum, done(c))
                dve.wait_ge(src_in[j], (c - j) * (16 // STEP) + 16)
                dve.wait_ge(msg_ready, done(c - 4))
                v.tensor_tensor(msg_in[:, j % 4, :], PS[:, edge_bank(j), :], x_src[:, j, :], ALU.add).then_inc(msg_sum, 1)

            def add(c, j):
                t = dve.value_load(tile_of[0:1, ds(c, 1)], min_val=0, max_val=NT - 1)
                dve.wait_ge(agg_psum, done(c))
                dve.wait_ge(agg_added, done(c - 1))
                to = agg[:, ds(t, 1), :].rearrange("p a d -> p (a d)")
                v.tensor_tensor(to, PS[0:T, 4 + j % 2, :], to, ALU.add).then_inc(agg_added, 1)

            def rest_of_message(c, j):
                dve.wait_ge(msg_ready, done(c))
                dve.wait_ge(agg_psum, done(c - 4))
                n = j // 2 % 2
                v.scalar_tensor_tensor(out=msg_lo[:, n, :], in0=msg_in[:, j % 4, :], scalar=0.0,
                                       in1=msg_hi[:, n, :].bitcast(F32),
                                       op0=ALU.max, op1=ALU.subtract).then_inc(msg_split, 2)

            dve.sem_inc(attr_lo, CREDIT)
            dve.sem_inc(msg_split, CREDIT)
            rest_of_attr(0, 0)
            rest_of_attr(2, 2)
            rest_of_attr(4, 4)
            for c in range(AHEAD):
                message(c, c)

            def steps(n, first, add_):
                with dve.Fori(0, n) as step:
                    c0 = first + step * STEP
                    for j in range(STEP):
                        message(c0 + j + AHEAD, (j + AHEAD) % STEP)
                        if j % 2 == 0:
                            rest_of_message(c0 + j + 1, j + 1)
                        else:
                            rest_of_attr(c0 + j + 5, (j + 5) % STEP)
                        if add_ is not None:
                            add_(c0 + j, j)

            is_packed = dve.value_load(packed[0:1, 0:1], min_val=0, max_val=1)
            with dve.If(is_packed):
                v.memset(agg, 0.0).then_inc(agg_ready, 1)
                dve.wait_ge(agg_ready, 1)
                steps(CH // STEP, 0, add)
                dve.wait_ge(agg_added, done(CH - 1))
                dve.sem_inc(agg_ready, 1)
            with dve.Else():
                dve.sem_inc(agg_ready, 1)
                dve.sem_inc(tile_added, 1)
                with dve.Fori(0, NT) as t:
                    steps(TC // STEP, t * TC, None)
                    dve.wait_ge(tile_psum, t + 1)
                    v.tensor_copy(agg[:, ds(t, 1), :].rearrange("p a d -> p (a d)"), PS[0:T, 4, :]).then_inc(tile_added, 1)
                dve.wait_ge(tile_added, NT + 1)
                dve.sem_inc(agg_ready, 1)
            dve.wait_ge(agg_ready, 2)
            dve.wait_ge(p2_in, 16 * 9)
            link(dve, v.tensor_scalar(eps_c, eps_c, 1.0, None, ALU.add))
            v.scalar_tensor_tensor(out=agg, in0=xN[0:T, :, :], scalar=eps_c, in1=agg, op0=ALU.mult,
                                   op1=ALU.add).then_inc(h_ready, 1)
            out_uses = 0
            for phase, (z, parts, gain, offset) in enumerate(((z1, 2 * KD, g1_c, beta1_c), (z2, KD, g2_c, beta2_c))):
                for m in range(parts):
                    out_uses += 2
                    dve.wait_ge(z_out, out_uses)
                    for h, (at, n) in enumerate(HALVES):
                        ins = v.bn_stats(bn_stat[:, m, 6 * h:6 * h + 6], z[:, m, at:at + n])
                link(dve, ins)
                for m in range(parts):
                    ins = v.bn_aggr(bn_mv[:, m, :], bn_stat[:, m, :].rearrange("p (a b) -> p a b", b=6))
                link(dve, ins)
                mean = bn_mv[:, 0:parts, 0:1].rearrange("p m a -> p (m a)")
                var = bn_mv[:, 0:parts, 1:2].rearrange("p m a -> p (m a)")
                v.tensor_scalar(bn_ve[:, 0:parts], var, EPS, None, ALU.add).then_inc(bn_var, 1)
                dve.wait_ge(bn_dev, phase + 1)
                link(dve, v.reciprocal(bn_ve[:, 0:parts], bn_sd[:, 0:parts]))
                link(dve, v.tensor_tensor(scale_c[:, 0:parts], bn_ve[:, 0:parts], gain[:, 0:parts], ALU.mult))
                link(dve, v.tensor_tensor(bn_ve[:, 0:parts], mean, scale_c[:, 0:parts], ALU.mult))
                v.tensor_tensor(shift_c[:, 0:parts], offset[:, 0:parts], bn_ve[:, 0:parts],
                                ALU.subtract).then_inc(bn_ready, 1)
            for t in range(NT):
                dve.wait_ge(back_psum, t + 1)
                ins = v.tensor_tensor(xN[0:T, t, :], PS[0:T, t, :], xN[0:T, t, :], ALU.add)
            link(dve, ins)
            dve_norm(dve, 2)

        def sync_l3(sp):
            sp.wait_ge(back_psum, NT)
            for to, row in ((mb2_row, p3["b2"]), (ln_g, p3["ln_g"]), (ln_b, p3["ln_b"])):
                load_rows(sp, to, row, l3_rows, T)
            sp.dma_start(mb1_c, p3["b1"]).then_inc(l3_rows, 16)
            with sp.Fori(0, LAYERS) as l:
                sp.wait_ge(w_used, l + 1)
                for n, name in enumerate(("Wq", "Wk", "Wv", "Ws")):
                    sp.dma_start(w_qkvs[n], p3[name][ds(l, 1)].rearrange("a p k o -> p (a k) o")).then_inc(l3_in, 16)
                sp.wait_ge(qk_out, l * 4 * KD + 1)
                sp.wait_ge(q_odd_out, l * 2 * KD + 1)
                sp.wait_ge(vs_out, l * 2 * NT + 1)
                for to, name in ((bq_c, "bq"), (bk_c, "bk")):
                    sp.dma_start(to, p3[name][ds(l, 1)].rearrange("a p k -> p (a k)")).then_inc(l3_in, 16)
                for to, name in ((bv_row, "bv"), (bs_row, "bs")):
                    sp.dma_start(to, p3[name][ds(l, 1)].to_broadcast((T, D))).then_inc(l3_in, 16)
            sp.wait_ge(w_used, LAYERS + 1)
            sp.dma_start(mlp1, p3["W1"]).then_inc(mlp_in, 16)
            sp.dma_start(mlp2, p3["W2"]).then_inc(mlp_in, 16)
            for t in range(NT):
                sp.wait_ge(tile_normed, t + 1)
                sp.dma_start(out[t * T:(t + 1) * T, :], xN[0:T, t, :]).then_inc(stored, 16)
            sp.wait_ge(stored, 16 * NT)

        STEPS = NT * HEADS

        def through(n):
            return n + 1 + 2

        def qk_emptied(eng, l, use):
            eng.wait_ge(qk_out, l * 4 * KD + use + 1 + 1)
            if use < 2 * KD:
                eng.wait_ge(q_odd_out, l * 2 * KD + use + 1 + 1)

        def pe_l3(pe):
            t_ = nc.tensor
            pe.sem_inc(w_used, 1)
            pe.wait_ge(x_ready, 3)
            pe.wait_ge(q_zeroed, 2)
            for q in (score_psum, turn_psum):
                pe.sem_inc(q, 2)
            with pe.Fori(0, LAYERS) as l:
                pe.wait_ge(l3_x, l + 1)
                transposes(xN)
                pe.wait_ge(xt_ready, NT * 3 + NT + l * NT)
                pe.wait_ge(l3_in, l * 128 + 128)
                use = 0
                for w in range(2):
                    for m in range(KD):
                        for at, n in HALVES:
                            if use >= 8:
                                qk_emptied(pe, l, use - 8)
                            for k in range(KD):
                                mm = t_.matmul(PS[:, use % 8, 0:n], w_qkvs[w][:, k, m * P:(m + 1) * P],
                                               xTk[:, k, at:at + n], start=(k == 0), stop=(k == KD - 1))
                            mm.then_inc(proj, 1)
                            use += 1
                for w in range(2, 4):
                    for t in range(NT):
                        if use < 24:
                            qk_emptied(pe, l, use - 8)
                        else:
                            pe.wait_ge(vs_out, l * 2 * NT + use - 23 + 1)
                        for k in range(KD):
                            mm = t_.matmul(PS[0:T, use % 8, :], xTk[:, k, t * T:(t + 1) * T], w_qkvs[w][:, k, :],
                                           start=(k == 0), stop=(k == KD - 1))
                        mm.then_inc(proj, 1)
                        use += 1
                qk_emptied(pe, l, 2 * KD - 1)
                qk_emptied(pe, l, 4 * KD - 1)
                pe.wait_ge(vs_out, l * 2 * NT + 2 * NT + 1)
                pe.sem_inc(w_used, 1)

                def score(n):
                    h, t = divmod(n, NT)
                    pe.wait_ge(score_out, through(l * STEPS + n - 2))
                    for at, m in HALVES_B:
                        mm = t_.matmul(PS[0:T, n % 2 * 2 + at // 512, 0:m], q_t[h % 2][:, h // 2, t * T:(t + 1) * T],
                                       k_t[:, h // 2, at:at + m], start=True, stop=True)
                    mm.then_inc(score_psum, 1)

                def turn(n):
                    pe.wait_ge(probs_out, through(l * STEPS + n))
                    pe.wait_ge(turn_out, through(l * STEPS + n - 1))
                    for st in range(NT):
                        mm = t_.transpose(PS[0:T, 4 + st // 4, st % 4 * P:st % 4 * P + T],
                                          probs[:, n % 2, st * T:(st + 1) * T], identT)
                    mm.then_inc(turn_psum, 1)

                def mix(n):
                    h, st = divmod(n, NT)
                    if st == 0:
                        pe.wait_ge(turn_out, through(l * STEPS + n + NT - 1))
                        if h % 2 == 0 and h > 0:
                            pe.wait_ge(pair_out, l * KD + h // 2)
                    for at, m in HALVES_B:
                        mm = t_.matmul(PS[:, 6 + at // 512, 0:m], val[:, st, h * P:(h + 1) * P],
                                       probs_t[:, h % 2, st * N + at:st * N + at + m],
                                       start=(h % 2 == 0 and st == 0), stop=(h % 2 == 1 and st == NT - 1))
                    mm.then_inc(mixed_part, 1)

                score(0)
                for n in range(STEPS):
                    if n + 1 < STEPS:
                        score(n + 1)
                    turn(n)
                    if n >= NT:
                        mix(n - NT)
                for n in range(STEPS - NT, STEPS):
                    mix(n)
                pe.wait_ge(score_out, through(l * STEPS + STEPS - 1))
                pe.wait_ge(pair_out, (l + 1) * KD)
                for t in range(NT):
                    for j in range(KD):
                        mm = t_.transpose(PS[0:T, t, j * P:(j + 1) * P], mixed_t[:, j, t * T:(t + 1) * T], ident[:, :])
                    mm.then_inc(heads_psum, 1)
            pe.wait_ge(x_ready, 4)
            transposes(xN)
            pe.wait_ge(xt_ready, NT * (4 + LAYERS))
            pe.wait_ge(mlp_in, 32)
            use = 0
            for m in range(2 * KD):
                for at, n in HALVES:
                    if use >= 8:
                        pe.wait_ge(hid_out, use - 7)
                    for k in range(KD):
                        mm = t_.matmul(PS[:, use % 8, 0:n], mlp1[:, k, m * P:(m + 1) * P], xTk[:, k, at:at + n],
                                       start=(k == 0), stop=(k == KD - 1))
                    mm.then_inc(hid_psum, 1)
                    use += 1
            pe.wait_ge(hid_out, use)
            for t in range(NT):
                for k in range(2 * KD):
                    mm = t_.matmul(PS[0:T, t, :], hid[:, k, t * T:(t + 1) * T], mlp2[:, k, :],
                                   start=(k == 0), stop=(k == 2 * KD - 1))
                mm.then_inc(mlp_psum, 1)

        def act_l3(act):
            act.sem_inc(qk_out, 1)
            act.sem_inc(probs_out, 2)
            act.sem_inc(turn_out, 2)
            with act.Fori(0, LAYERS) as l:
                for b in range(NT):
                    act.wait_ge(xt_psum, 3 * NT + l * NT + b + 1)
                    nc.scalar.copy(xT[:, b * 4 * T:(b + 1) * 4 * T], PS[:, b, 0:4 * T]).then_inc(xt_ready, 1)
                act.wait_ge(l3_in, l * 128 + 128)
                use = 0
                for to, bias, n_p in ((q_t[0], bq_c, HD), (k_t, bk_c, P)):
                    for m in range(KD):
                        for at, n in HALVES:
                            act.wait_ge(proj, l * (4 * KD + 2 * NT) + use + 1)
                            nc.scalar.activation(to[0:n_p, m, at:at + n], PS[0:n_p, use % 8, 0:n], ACT.Identity,
                                                 bias=bias[0:n_p, m:m + 1]).then_inc(qk_out, 1)
                            use += 1

                def exponent(n):
                    act.wait_ge(score_out, through(l * STEPS + n))
                    act.wait_ge(turn_psum, through(l * STEPS + n - 2))
                    nc.scalar.activation(probs[:, n % 2, :], scores[:, n % 2, :], ACT.Exp,
                                         bias=minus_top[:, n % 4:n % 4 + 1], scale=float(HD) ** -0.5,
                                         accum_out=denom[:, n % NT, n // NT:n // NT + 1]).then_inc(probs_out, 1)

                def keep_turned(n):
                    act.wait_ge(turn_psum, through(l * STEPS + n))
                    h, t = divmod(n, NT)
                    if t == 0 and h >= 2:
                        act.wait_ge(mixed_part, l * STEPS + n - NT)
                    nc.scalar.copy(probs_t[:, h % 2, :].rearrange("p (s n) -> p s n", n=N)[:, :, t * T:(t + 1) * T],
                                   two_banks(4, T, NT * P).rearrange("p (t n) -> p t n", n=P)[:, :, 0:T]
                                   ).then_inc(turn_out, 1)

                def keep_pair(j):
                    act.wait_ge(mixed_part, l * STEPS + (j + 1) * 2 * NT)
                    for at, m in HALVES_B:
                        ins = nc.scalar.copy(mixed_t[:, j, at:at + m], PS[:, 6 + at // 512, 0:m])
                    ins.then_inc(pair_out, 1)

                exponent(0)
                for n in range(STEPS):
                    if n + 1 < STEPS:
                        exponent(n + 1)
                    keep_turned(n)
                    if n % (2 * NT) == 3 * NT % (2 * NT) - 1 and n > 2 * NT:
                        keep_pair(n // (2 * NT) - 1)
                keep_pair(KD - 1)
            act_deviation(act, 3)
            act_turn(act, 3 + LAYERS, xT)
            act.wait_ge(l3_rows, 64)
            use = 0
            for m in range(2 * KD):
                for at, n in HALVES:
                    act.wait_ge(hid_psum, use + 1)
                    nc.scalar.activation(hid[:, m, at:at + n], PS[:, use % 8, 0:n], ACT.Relu,
                                         bias=mb1_c[:, m:m + 1]).then_inc(hid_out, 1)
                    use += 1
            act_deviation(act, 4)
            act_deviation(act, 5)

        def dve_l3(dve):
            v = nc.vector
            dve.sem_inc(vs_out, 1)
            dve.sem_inc(score_out, 2)
            dve.sem_inc(q_odd_out, 1)
            dve.wait_ge(val_zeroed, 1)
            dve.sem_inc(l3_x, 1)
            v.tensor_copy(enc, xN[0:T, :, :])
            with dve.Fori(0, LAYERS) as l:
                dve.wait_ge(l3_in, l * 128 + 128)
                use = 0
                for m in range(KD):
                    for at, n in HALVES:
                        dve.wait_ge(proj, l * (4 * KD + 2 * NT) + use + 1)
                        v.tensor_scalar(q_t[1][HD:P, m, at:at + n], PS[HD:P, use % 8, 0:n], bq_c[HD:P, m:m + 1], None,
                                        ALU.add).then_inc(q_odd_out, 1)
                        use += 1
                use = 4 * KD

                def two_heads(row, n):
                    return row.rearrange("p (j a d) -> p j a d", a=2, d=HD)[:, :, n, :]

                for t in range(NT):
                    dve.wait_ge(proj, l * (4 * KD + 2 * NT) + use + 1)
                    for n in range(2):
                        to = val[:, t, :].rearrange("p (j a d) -> p j a d", a=2, d=P)[:, :, n, n * HD:(n + 1) * HD]
                        ins = v.tensor_tensor(to, two_heads(PS[0:T, use % 8, :], n), two_heads(bv_row, n), ALU.add)
                    ins.then_inc(vs_out, 1)
                    use += 1
                for t in range(NT):
                    dve.wait_ge(proj, l * (4 * KD + 2 * NT) + use + 1)
                    v.tensor_tensor(rest[:, t, :], PS[0:T, use % 8, :], bs_row, ALU.add).then_inc(vs_out, 1)
                    use += 1
                dve.wait_ge(vs_out, l * 2 * NT + 2 * NT + 1)
                v.tensor_tensor(rest, rest, enc, ALU.add).then_inc(o_step, 1)

                def mask(n):
                    t = n % NT
                    dve.wait_ge(score_psum, through(l * STEPS + n))
                    dve.wait_ge(probs_out, through(l * STEPS + n - 2))
                    dve.sem_inc(tick, 1)
                    v.tensor_tensor_reduce(out=scores[:, n % 2, :], in0=two_banks(n % 2 * 2, T), in1=pairs_t[:, t, :],
                                           scale=1.0, scalar=3 * FAR, op0=ALU.add, op1=ALU.max,
                                           accum_out=top[:, n % 4:n % 4 + 1]).then_inc(top_ready, 1)
                    dve.wait_ge(top_ready, l * STEPS + n + 1)
                    v.tensor_scalar(minus_top[:, n % 4:n % 4 + 1], top[:, n % 4:n % 4 + 1], -float(HD) ** -0.5, None,
                                    ALU.mult).then_inc(score_out, 1)

                def finish(t):
                    at = l * (1 + 4 * NT) + 1 + 4 * t
                    dve.wait_ge(heads_psum, l * NT + t + 1)
                    dve.wait_ge(o_step, at)
                    v.tensor_scalar(inv[:, t, :], denom[:, t, :], 1e-16, None, ALU.add).then_inc(o_step, 1)
                    dve.wait_ge(o_step, at + 1)
                    v.reciprocal(inv[:, t, :], inv[:, t, :]).then_inc(o_step, 1)
                    dve.wait_ge(o_step, at + 2)
                    v.tensor_scalar(inv[:, t, :], inv[:, t, :], has_in[0:T, t:t + 1], None, ALU.mult).then_inc(o_step, 1)
                    dve.wait_ge(o_step, at + 3)
                    v.tensor_tensor(xN[0:T, t, :].rearrange("p (h d) -> p h d", d=HD),
                                    PS[0:T, t, :].rearrange("p (h d) -> p h d", d=HD),
                                    inv[:, t, :].unsqueeze(2).broadcast_to([T, HEADS, HD]), ALU.mult).then_inc(tile_out, 1)
                    dve.wait_ge(tile_out, l * NT + t + 1)
                    v.tensor_tensor(xN[0:T, t, :], xN[0:T, t, :], rest[:, t, :], ALU.add).then_inc(o_step, 1)

                for n in range(STEPS):
                    mask(n)
                for t in range(NT):
                    finish(t)
                dve.wait_ge(o_step, (l + 1) * (1 + 4 * NT))
                dve.sem_inc(l3_x, 1)
            dve.wait_ge(l3_rows, 64)
            dve_norm(dve, 3, ln_g, ln_b)
            link(dve, v.tensor_tensor(with_bias, xN[0:T, :, :], over_tiles(mb2_row), ALU.add))
            link(dve, v.tensor_scalar(enc, enc, 2.0, None, ALU.mult))
            link(dve, v.tensor_tensor(enc, enc, over_tiles(ln_b), ALU.add))
            for t in range(NT):
                dve.wait_ge(mlp_psum, t + 1)
                link(dve, v.tensor_tensor(xN[0:T, t, :], PS[0:T, t, :], with_bias[:, t, :], ALU.add))
                ins = v.bn_stats(stat[0:T, t, :], xN[0:T, t, :])
            dve_norm(dve, 4, ln_g, enc_tiles=enc, stats=ins)
            dve_norm(dve, 5, store=True)

        @block.sync
        def _(sp):
            sync_sort(sp)
            sync_l0(sp)
            sync_l1(sp)
            sync_l2(sp)
            sync_l3(sp)

        @block.gpsimd
        def _(pool):
            pool_sort(pool)
            pool_l0(pool)
            pool_l2(pool)
            pool_l3(pool)

        @block.tensor
        def _(pe):
            pe_sort(pe)
            pe.wait_ge(plan_ready, 1)
            is_packed = pe.value_load(packed[0:1, 0:1], min_val=0, max_val=1)
            with pe.If(is_packed):
                pe_count_packed(pe)
            with pe.Else():
                pe_count(pe)
            pe_l0(pe)
            pe_l1(pe)
            pe_l2(pe)
            pe_l3(pe)

        @block.scalar
        def _(act):
            act_products(act)
            act.wait_ge(plan_ready, 1)
            is_packed = act.value_load(packed[0:1, 0:1], min_val=0, max_val=1)
            with act.If(is_packed):
                act.wait_ge(weights_ready, NT)
            with act.Else():
                act_count(act)
            act_l0(act)
            act_l1(act)
            act_l2(act)
            act_l3(act)

        @block.vector
        def _(dve):
            dve_sort(dve)
            dve_count_start(dve)
            is_packed = dve.value_load(packed[0:1, 0:1], min_val=0, max_val=1)
            with dve.If(is_packed):
                dve_count_packed(dve)
            with dve.Else():
                dve_count(dve)
            dve.sem_inc(tallied, 1)
            dve_l0(dve)
            dve_l1(dve)
            dve_l2(dve)
            dve_l3(dve)


def _tiles(w):
    import numpy as np
    w = np.asarray(w)
    k = w.shape[-2] // 128
    return np.ascontiguousarray(np.moveaxis(w.reshape(w.shape[:-2] + (k, 128, w.shape[-1])), -2, -3))


def _columns(b):
    import numpy as np
    b = np.asarray(b)
    return np.ascontiguousarray(np.moveaxis(b.reshape(b.shape[:-1] + (b.shape[-1] // 128, 128)), -1, -2))


def kernel(**inputs):
    import numpy as np
    import concourse.bacc as bacc
    from concourse.bass_utils import run_bass_kernel_spmd as run

    a = {name: np.ascontiguousarray(v) for name, v in inputs.items()}
    layers = [{}, {}, {}, {}]
    plain = {}
    for name, v in a.items():
        if name[0] == "L" and name[2:6] == "_gnn":
            layers[int(name[1])][name[7:]] = v
        else:
            plain[name] = v
    for name in ("W_self", "W_rel"):
        layers[0][name] = _tiles(np.swapaxes(layers[0][name], -1, -2))
    layers[1]["U"] = _tiles(layers[1]["U"])
    layers[2]["eps"] = layers[2]["eps"].reshape(1)
    for n, names in ((2, ("W1", "W2")), (3, ("Wq", "Wk", "Wv", "Ws", "W1", "W2"))):
        for name in names:
            layers[n][name] = _tiles(layers[n][name])
    for n, names in ((2, ("b1", "g1", "beta1", "b2", "g2", "beta2")), (3, ("bq", "bk", "b1"))):
        for name in names:
            layers[n][name] = _columns(layers[n][name])

    nc = bacc.Bacc("TRN2", target_bir_lowering=False, num_devices=1)
    arrays = {}

    def given(name, v):
        arrays[name] = v
        return nc.dram_tensor(name, v.shape, mybir.dt.from_np(v.dtype), kind="ExternalInput").ap()

    args = [given("in_" + name, plain[name]) for name in ("x", "src", "dst", "edge_attr_64", "edge_type_8", "edge_weight")]
    parameters = [{name: given(f"in_L{n}_{name}", v) for name, v in layer.items()} for n, layer in enumerate(layers)]
    out = nc.dram_tensor("out_x", (N, D), F32, kind="ExternalOutput").ap()
    program(nc, *args, *parameters, out)
    return run(nc, [arrays], core_ids=[0]).results[0]["out_x"]
```
